# Optimizing a Trainium2 kernel written in Bass

```python
import numpy as np
import jax
import jax.numpy as jnp

def _softmax(x, axis=-1):
    return jax.nn.softmax(x, axis=axis)

def _gelu(x):
    return jax.nn.gelu(x, approximate=True)

def _silu(x):
    return jax.nn.silu(x)

def _sigmoid(x):
    return jax.nn.sigmoid(x)

def _layernorm(x, axis=-1, eps=1e-05):
    m = jnp.mean(x, axis=axis, keepdims=True)
    v = jnp.var(x, axis=axis, keepdims=True)
    return (x - m) / jnp.sqrt(v + eps)

def _scatter_add(tgt, idx, src, axis=0):
    return tgt.at[idx].add(src)

def _segment_sum(src, seg, n):
    return jax.ops.segment_sum(src, seg, n)
kernel_name = 'mk_macaron_d2_jaxref_r8_4ea749'

def setup_inputs(seed: int=0):
    np.random.seed(seed)
    _w = jnp.asarray

    def _L0_attn_setup():
        import jax, jax.numpy as jnp
        import numpy as np
        LN_EPS = 1e-05
        WKV_EPS = 1e-08
        NEG_INF = -1e+38

        def _layernorm(x, g, b):
            m = jnp.mean(x, axis=-1, keepdims=True)
            v = jnp.mean(jnp.square(x - m), axis=-1, keepdims=True)
            return (x - m) * jax.lax.rsqrt(v + LN_EPS) * g + b

        def _wkv(w, u, k, v):
            B, T, C = k.shape
            aa0 = jnp.zeros((B, C), k.dtype)
            bb0 = jnp.full((B, C), NEG_INF, k.dtype)

            def step(carry, kv_t):
                aa, bb = carry
                kk, vv = kv_t
                ww = u + kk
                p = jnp.maximum(bb, ww)
                e1 = jnp.exp(bb - p)
                e2 = jnp.exp(ww - p)
                y_t = (e1 * aa + e2 * vv) / (e1 + e2 + WKV_EPS)
                ww = w + bb
                p = jnp.maximum(ww, kk)
                e1 = jnp.exp(ww - p)
                e2 = jnp.exp(kk - p)
                aa = e1 * aa + e2 * vv
                bb = p + jnp.log(e1 + e2 + WKV_EPS)
                return ((aa, bb), y_t)
            (aa, bb), ys = jax.lax.scan(step, (aa0, bb0), (jnp.swapaxes(k, 0, 1), jnp.swapaxes(v, 0, 1)))
            y = jnp.swapaxes(ys, 0, 1)
            new_state = jnp.stack([aa, bb], axis=-1)
            return (y, new_state)

        def _reference_tuple_inner(x, time_decay, time_first, W_tm, g1, b1, tmk, tmv, tmr, W_cm, W_cp, g2, b2, cmk, cmr):
            x_prev = jnp.concatenate([x[:, :1], x[:, :-1]], axis=1)
            kvr = _layernorm(x, g1, b1) @ W_tm
            k, v, r = jnp.split(kvr, 3, axis=-1)
            k = k * tmk + x_prev * (1.0 - tmk)
            v = v * tmv + x_prev * (1.0 - tmv)
            r = jax.nn.sigmoid(r * tmr + x_prev * (1.0 - tmr))
            y, new_state = _wkv(time_decay, time_first, k, v)
            x = x + r * y
            xp = jnp.concatenate([x[:, -1:], x[:, :-1]], axis=1)
            xn = _layernorm(x, g2, b2)
            kk = xn @ W_cm
            cmk4 = jnp.tile(cmk, (1, 1, 4))
            xp4 = jnp.tile(xp, (1, 1, 4))
            kk = kk * cmk4 + xp4 * (1.0 - cmk4)
            rr = jax.nn.sigmoid(xn * cmr + xp * (1.0 - cmr))
            vv = jnp.square(jax.nn.relu(kk)) @ W_cp
            x = x + rr * vv
            return (x, new_state)
        key = jax.random.key(seed)
        ks = jax.random.split(key, 12)
        B, T, C = (8, 256, 128)
        scale = 0.02
        return {'x': jax.random.normal(ks[0], (B, T, C), jnp.float32), 'time_decay': jax.random.uniform(ks[1], (C,), jnp.float32, -1.0, 1.0), 'time_first': jax.random.uniform(ks[2], (C,), jnp.float32, -1.0, 1.0), 'W_tm': jax.random.normal(ks[3], (C, 3 * C), jnp.float32) * scale, 'g1': jnp.ones((C,), jnp.float32), 'b1': jnp.zeros((C,), jnp.float32), 'tmk': jax.random.uniform(ks[4], (1, 1, C), jnp.float32), 'tmv': jax.random.uniform(ks[5], (1, 1, C), jnp.float32), 'tmr': jax.random.uniform(ks[6], (1, 1, C), jnp.float32), 'W_cm': jax.random.normal(ks[7], (C, 4 * C), jnp.float32) * scale, 'W_cp': jax.random.normal(ks[8], (4 * C, C), jnp.float32) * scale, 'g2': jnp.ones((C,), jnp.float32), 'b2': jnp.zeros((C,), jnp.float32), 'cmk': jax.random.uniform(ks[9], (1, 1, C), jnp.float32), 'cmr': jax.random.uniform(ks[10], (1, 1, C), jnp.float32)}
    _L0_attn_in = _L0_attn_setup()

    def _L0_ffn_setup():
        import jax, jax.numpy as jnp
        import numpy as np
        E = 8
        TOPK = 2
        H = 128
        I = 128
        ISH = I * 2
        B, S = (2, 128)
        key = jax.random.key(seed)
        ks = jax.random.split(key, 7)
        s = 0.02
        return {'hidden_states': jax.random.normal(ks[0], (B, S, H), jnp.float32), 'w_router': jax.random.normal(ks[1], (H, E), jnp.float32) * s, 'fc1_w': jax.random.normal(ks[2], (E, H, 2 * I), jnp.float32) * s, 'fc2_w': jax.random.normal(ks[3], (E, I, H), jnp.float32) * s, 'gate_w': jax.random.normal(ks[4], (H, ISH), jnp.float32) * s, 'up_w': jax.random.normal(ks[5], (H, ISH), jnp.float32) * s, 'down_w': jax.random.normal(ks[6], (ISH, H), jnp.float32) * s}
    _L0_ffn_in = _L0_ffn_setup()

    def _L1_attn_setup():
        import jax, jax.numpy as jnp
        import numpy as np
        D_MODEL = 128
        D_STATE = 64
        N_HEADS = 16
        CHUNK = 64

        def segsum(x):
            T = x.shape[-1]
            xx = jnp.broadcast_to(x[..., None], x.shape + (T,))
            lower = jnp.tril(jnp.ones((T, T), dtype=bool), -1)
            xs = jnp.cumsum(jnp.where(lower, xx, 0.0), axis=-2)
            keep = jnp.tril(jnp.ones((T, T), dtype=bool), 0)
            return jnp.where(keep, xs, -jnp.inf)

        def ssd_minimal(X, A, B, C, block_len):
            b, L, h, p = X.shape
            n = B.shape[-1]
            c = L // block_len
            l = block_len
            X = X.reshape(b, c, l, h, p)
            A = A.reshape(b, c, l, h).transpose(0, 3, 1, 2)
            B = B.reshape(b, c, l, h, n)
            C = C.reshape(b, c, l, h, n)
            A_cumsum = jnp.cumsum(A, axis=-1)
            Lmat = jnp.exp(segsum(A))
            Y_diag = jnp.einsum('bclhn,bcshn,bhcls,bcshp->bclhp', C, B, Lmat, X)
            decay_states = jnp.exp(A_cumsum[:, :, :, -1:] - A_cumsum)
            states = jnp.einsum('bclhn,bhcl,bclhp->bchpn', B, decay_states, X)
            init = jnp.zeros_like(states[:, :1])
            states = jnp.concatenate([init, states], axis=1)
            A_last = A_cumsum[:, :, :, -1]
            decay_chunk = jnp.exp(segsum(jnp.pad(A_last, ((0, 0), (0, 0), (1, 0)))))
            new_states = jnp.einsum('bhzc,bchpn->bzhpn', decay_chunk, states)
            states, final_state = (new_states[:, :-1], new_states[:, -1])
            state_decay_out = jnp.exp(A_cumsum)
            Y_off = jnp.einsum('bclhn,bchpn,bhcl->bclhp', C, states, state_decay_out)
            Y = (Y_diag + Y_off).reshape(b, L, h, p)
            return (Y, final_state)

        def mamba2_forward(x, W_in, W_dt, b_dt, W_B, W_C, W_out, A_log):
            b, L, d = x.shape
            h, n = (N_HEADS, D_STATE)
            p = d // h
            xz = x @ W_in.T
            x_in, z = (xz[..., :d], xz[..., d:])
            dt = jax.nn.softplus(x @ W_dt.T + b_dt)
            A = -jnp.exp(A_log)[None, None, :] * dt
            B = (x @ W_B.T).reshape(b, L, h, n)
            C = (x @ W_C.T).reshape(b, L, h, n)
            X = x_in.reshape(b, L, h, p) * dt[..., None]
            Y, new_state = ssd_minimal(X, A, B, C, CHUNK)
            y = Y.reshape(b, L, d) * jax.nn.silu(z)
            y = y @ W_out.T
            return (y, new_state)

        def _reference_tuple_inner(x, W_in, W_dt, b_dt, W_B, W_C, W_out, A_log):
            return mamba2_forward(x, W_in, W_dt, b_dt, W_B, W_C, W_out, A_log)
        key = jax.random.key(seed)
        ks = jax.random.split(key, 7)
        d, h, n = (D_MODEL, N_HEADS, D_STATE)
        x = jax.random.normal(ks[0], (2, 512, d), dtype=jnp.float32)
        lim_in = 0.5 * np.sqrt(6.0 / (d + 2 * d))
        W_in = jax.random.uniform(ks[1], (2 * d, d), minval=-lim_in, maxval=lim_in, dtype=jnp.float32)
        lim_out = 0.5 * np.sqrt(6.0 / (d + d))
        W_out = jax.random.uniform(ks[2], (d, d), minval=-lim_out, maxval=lim_out, dtype=jnp.float32)
        lim = 1.0 / np.sqrt(d)
        W_dt = jax.random.uniform(ks[3], (h, d), minval=-lim, maxval=lim, dtype=jnp.float32)
        b_dt = jnp.zeros((h,), dtype=jnp.float32)
        W_B = jax.random.uniform(ks[4], (h * n, d), minval=-lim, maxval=lim, dtype=jnp.float32)
        W_C = jax.random.uniform(ks[5], (h * n, d), minval=-lim, maxval=lim, dtype=jnp.float32)
        A_log = jnp.log(jnp.linspace(1.0, 16.0, h)).astype(jnp.float32)
        return {'x': x, 'W_in': W_in, 'W_dt': W_dt, 'b_dt': b_dt, 'W_B': W_B, 'W_C': W_C, 'W_out': W_out, 'A_log': A_log}
    _L1_attn_in = _L1_attn_setup()

    def _L1_ffn_setup():
        import jax, jax.numpy as jnp
        import numpy as np
        N_EXPERTS = 8
        TOP_K = 2
        D_MODEL = 128
        HIDDEN = 512
        ROUTED_H = 128
        BATCH, SEQ = (2, 512)
        key = jax.random.key(seed)
        ks = jax.random.split(key, 8)
        std = 0.02
        return {'x': jax.random.normal(ks[0], (BATCH, SEQ, D_MODEL), dtype=jnp.float32), 'w12': std * jax.random.normal(ks[1], (N_EXPERTS, 2 * ROUTED_H, D_MODEL), dtype=jnp.float32), 'w3': std * jax.random.normal(ks[2], (N_EXPERTS, D_MODEL, ROUTED_H), dtype=jnp.float32), 'shared_w1': std * jax.random.normal(ks[3], (HIDDEN, D_MODEL), dtype=jnp.float32), 'shared_w2': std * jax.random.normal(ks[4], (HIDDEN, D_MODEL), dtype=jnp.float32), 'shared_w3': std * jax.random.normal(ks[5], (D_MODEL, HIDDEN), dtype=jnp.float32), 'router_w': std * jax.random.normal(ks[6], (N_EXPERTS, D_MODEL), dtype=jnp.float32), 'expert_bias': jnp.zeros((N_EXPERTS,), dtype=jnp.float32)}
    _L1_ffn_in = _L1_ffn_setup()
    _d = {'L0_attn_x': _L0_attn_in['x'], 'L0_attn_time_decay': _L0_attn_in['time_decay'], 'L0_attn_time_first': _L0_attn_in['time_first'], 'L0_attn_W_tm': _L0_attn_in['W_tm'], 'L0_attn_g1': _L0_attn_in['g1'], 'L0_attn_b1': _L0_attn_in['b1'], 'L0_attn_tmk': _L0_attn_in['tmk'], 'L0_attn_tmv': _L0_attn_in['tmv'], 'L0_attn_tmr': _L0_attn_in['tmr'], 'L0_attn_W_cm': _L0_attn_in['W_cm'], 'L0_attn_W_cp': _L0_attn_in['W_cp'], 'L0_attn_g2': _L0_attn_in['g2'], 'L0_attn_b2': _L0_attn_in['b2'], 'L0_attn_cmk': _L0_attn_in['cmk'], 'L0_attn_cmr': _L0_attn_in['cmr'], 'L0_ffn_w_router': _L0_ffn_in['w_router'], 'L0_ffn_fc1_w': _L0_ffn_in['fc1_w'], 'L0_ffn_fc2_w': _L0_ffn_in['fc2_w'], 'L0_ffn_gate_w': _L0_ffn_in['gate_w'], 'L0_ffn_up_w': _L0_ffn_in['up_w'], 'L0_ffn_down_w': _L0_ffn_in['down_w'], 'L1_attn_W_in': _L1_attn_in['W_in'], 'L1_attn_W_dt': _L1_attn_in['W_dt'], 'L1_attn_b_dt': _L1_attn_in['b_dt'], 'L1_attn_W_B': _L1_attn_in['W_B'], 'L1_attn_W_C': _L1_attn_in['W_C'], 'L1_attn_W_out': _L1_attn_in['W_out'], 'L1_attn_A_log': _L1_attn_in['A_log'], 'L1_ffn_w12': _L1_ffn_in['w12'], 'L1_ffn_w3': _L1_ffn_in['w3'], 'L1_ffn_shared_w1': _L1_ffn_in['shared_w1'], 'L1_ffn_shared_w2': _L1_ffn_in['shared_w2'], 'L1_ffn_shared_w3': _L1_ffn_in['shared_w3'], 'L1_ffn_router_w': _L1_ffn_in['router_w'], 'L1_ffn_expert_bias': _L1_ffn_in['expert_bias']}
    _x0 = _d['L0_attn_x']
    _d['L0_attn_x'] = jax.random.normal(jax.random.fold_in(jax.random.key(seed), 1), (8, 256, 128), dtype=_x0.dtype)
    del _x0
    return _d

def reference(L0_attn_x, L0_attn_time_decay, L0_attn_time_first, L0_attn_W_tm, L0_attn_g1, L0_attn_b1, L0_attn_tmk, L0_attn_tmv, L0_attn_tmr, L0_attn_W_cm, L0_attn_W_cp, L0_attn_g2, L0_attn_b2, L0_attn_cmk, L0_attn_cmr, L0_ffn_w_router, L0_ffn_fc1_w, L0_ffn_fc2_w, L0_ffn_gate_w, L0_ffn_up_w, L0_ffn_down_w, L1_attn_W_in, L1_attn_W_dt, L1_attn_b_dt, L1_attn_W_B, L1_attn_W_C, L1_attn_W_out, L1_attn_A_log, L1_ffn_w12, L1_ffn_w3, L1_ffn_shared_w1, L1_ffn_shared_w2, L1_ffn_shared_w3, L1_ffn_router_w, L1_ffn_expert_bias):

    def _L0_attn_ref(x, time_decay, time_first, W_tm, g1, b1, tmk, tmv, tmr, W_cm, W_cp, g2, b2, cmk, cmr):
        import jax, jax.numpy as jnp
        import numpy as np
        LN_EPS = 1e-05
        WKV_EPS = 1e-08
        NEG_INF = -1e+38

        def _layernorm(x, g, b):
            m = jnp.mean(x, axis=-1, keepdims=True)
            v = jnp.mean(jnp.square(x - m), axis=-1, keepdims=True)
            return (x - m) * jax.lax.rsqrt(v + LN_EPS) * g + b

        def _wkv(w, u, k, v):
            B, T, C = k.shape
            aa0 = jnp.zeros((B, C), k.dtype)
            bb0 = jnp.full((B, C), NEG_INF, k.dtype)

            def step(carry, kv_t):
                aa, bb = carry
                kk, vv = kv_t
                ww = u + kk
                p = jnp.maximum(bb, ww)
                e1 = jnp.exp(bb - p)
                e2 = jnp.exp(ww - p)
                y_t = (e1 * aa + e2 * vv) / (e1 + e2 + WKV_EPS)
                ww = w + bb
                p = jnp.maximum(ww, kk)
                e1 = jnp.exp(ww - p)
                e2 = jnp.exp(kk - p)
                aa = e1 * aa + e2 * vv
                bb = p + jnp.log(e1 + e2 + WKV_EPS)
                return ((aa, bb), y_t)
            (aa, bb), ys = jax.lax.scan(step, (aa0, bb0), (jnp.swapaxes(k, 0, 1), jnp.swapaxes(v, 0, 1)))
            y = jnp.swapaxes(ys, 0, 1)
            new_state = jnp.stack([aa, bb], axis=-1)
            return (y, new_state)

        def _reference_tuple_inner(x, time_decay, time_first, W_tm, g1, b1, tmk, tmv, tmr, W_cm, W_cp, g2, b2, cmk, cmr):
            x_prev = jnp.concatenate([x[:, :1], x[:, :-1]], axis=1)
            kvr = _layernorm(x, g1, b1) @ W_tm
            k, v, r = jnp.split(kvr, 3, axis=-1)
            k = k * tmk + x_prev * (1.0 - tmk)
            v = v * tmv + x_prev * (1.0 - tmv)
            r = jax.nn.sigmoid(r * tmr + x_prev * (1.0 - tmr))
            y, new_state = _wkv(time_decay, time_first, k, v)
            x = x + r * y
            xp = jnp.concatenate([x[:, -1:], x[:, :-1]], axis=1)
            xn = _layernorm(x, g2, b2)
            kk = xn @ W_cm
            cmk4 = jnp.tile(cmk, (1, 1, 4))
            xp4 = jnp.tile(xp, (1, 1, 4))
            kk = kk * cmk4 + xp4 * (1.0 - cmk4)
            rr = jax.nn.sigmoid(xn * cmr + xp * (1.0 - cmr))
            vv = jnp.square(jax.nn.relu(kk)) @ W_cp
            x = x + rr * vv
            return (x, new_state)
        return _reference_tuple_inner(x, time_decay, time_first, W_tm, g1, b1, tmk, tmv, tmr, W_cm, W_cp, g2, b2, cmk, cmr)[0]

    def _L0_ffn_ref(hidden_states, w_router, fc1_w, fc2_w, gate_w, up_w, down_w):
        import jax, jax.numpy as jnp
        import numpy as np
        E = 8
        TOPK = 2
        H = 128
        I = 128
        ISH = I * 2
        B, S = (2, 128)
        orig_shape = hidden_states.shape
        x = hidden_states.reshape(-1, orig_shape[-1])
        logits = x @ w_router
        top_logits, top_idx = jax.lax.top_k(logits, TOPK)
        scores = jax.nn.softmax(top_logits, axis=-1)
        flat_idx = top_idx.reshape(-1)
        sorted_idx = jnp.argsort(flat_idx)
        permuted = x[sorted_idx // TOPK]
        eid = flat_idx[sorted_idx]
        out_perm = jnp.zeros((permuted.shape[0], orig_shape[-1]), x.dtype)
        for e in range(E):
            m = (eid == e).astype(x.dtype)[:, None]
            h1 = permuted * m @ fc1_w[e]
            proj, gate = jnp.split(h1, 2, axis=-1)
            out_perm = out_perm + jax.nn.silu(proj) * gate @ fc2_w[e]
        unperm = jnp.zeros_like(out_perm).at[sorted_idx].set(out_perm)
        moe_out = (unperm.reshape(-1, TOPK, orig_shape[-1]) * scores[:, :, None]).sum(axis=1)
        moe_out = moe_out.reshape(orig_shape)
        shared = jax.nn.silu(hidden_states @ gate_w) * (hidden_states @ up_w) @ down_w
        return moe_out + shared

    def _L1_attn_ref(x, W_in, W_dt, b_dt, W_B, W_C, W_out, A_log):
        import jax, jax.numpy as jnp
        import numpy as np
        D_MODEL = 128
        D_STATE = 64
        N_HEADS = 16
        CHUNK = 64

        def segsum(x):
            T = x.shape[-1]
            xx = jnp.broadcast_to(x[..., None], x.shape + (T,))
            lower = jnp.tril(jnp.ones((T, T), dtype=bool), -1)
            xs = jnp.cumsum(jnp.where(lower, xx, 0.0), axis=-2)
            keep = jnp.tril(jnp.ones((T, T), dtype=bool), 0)
            return jnp.where(keep, xs, -jnp.inf)

        def ssd_minimal(X, A, B, C, block_len):
            b, L, h, p = X.shape
            n = B.shape[-1]
            c = L // block_len
            l = block_len
            X = X.reshape(b, c, l, h, p)
            A = A.reshape(b, c, l, h).transpose(0, 3, 1, 2)
            B = B.reshape(b, c, l, h, n)
            C = C.reshape(b, c, l, h, n)
            A_cumsum = jnp.cumsum(A, axis=-1)
            Lmat = jnp.exp(segsum(A))
            Y_diag = jnp.einsum('bclhn,bcshn,bhcls,bcshp->bclhp', C, B, Lmat, X)
            decay_states = jnp.exp(A_cumsum[:, :, :, -1:] - A_cumsum)
            states = jnp.einsum('bclhn,bhcl,bclhp->bchpn', B, decay_states, X)
            init = jnp.zeros_like(states[:, :1])
            states = jnp.concatenate([init, states], axis=1)
            A_last = A_cumsum[:, :, :, -1]
            decay_chunk = jnp.exp(segsum(jnp.pad(A_last, ((0, 0), (0, 0), (1, 0)))))
            new_states = jnp.einsum('bhzc,bchpn->bzhpn', decay_chunk, states)
            states, final_state = (new_states[:, :-1], new_states[:, -1])
            state_decay_out = jnp.exp(A_cumsum)
            Y_off = jnp.einsum('bclhn,bchpn,bhcl->bclhp', C, states, state_decay_out)
            Y = (Y_diag + Y_off).reshape(b, L, h, p)
            return (Y, final_state)

        def mamba2_forward(x, W_in, W_dt, b_dt, W_B, W_C, W_out, A_log):
            b, L, d = x.shape
            h, n = (N_HEADS, D_STATE)
            p = d // h
            xz = x @ W_in.T
            x_in, z = (xz[..., :d], xz[..., d:])
            dt = jax.nn.softplus(x @ W_dt.T + b_dt)
            A = -jnp.exp(A_log)[None, None, :] * dt
            B = (x @ W_B.T).reshape(b, L, h, n)
            C = (x @ W_C.T).reshape(b, L, h, n)
            X = x_in.reshape(b, L, h, p) * dt[..., None]
            Y, new_state = ssd_minimal(X, A, B, C, CHUNK)
            y = Y.reshape(b, L, d) * jax.nn.silu(z)
            y = y @ W_out.T
            return (y, new_state)

        def _reference_tuple_inner(x, W_in, W_dt, b_dt, W_B, W_C, W_out, A_log):
            return mamba2_forward(x, W_in, W_dt, b_dt, W_B, W_C, W_out, A_log)
        return _reference_tuple_inner(x, W_in, W_dt, b_dt, W_B, W_C, W_out, A_log)[0]

    def _L1_ffn_ref(x, w12, w3, shared_w1, shared_w2, shared_w3, router_w, expert_bias):
        import jax, jax.numpy as jnp
        import numpy as np
        N_EXPERTS = 8
        TOP_K = 2
        D_MODEL = 128
        HIDDEN = 512
        ROUTED_H = 128
        BATCH, SEQ = (2, 512)
        b, s, d = x.shape
        xf = x.reshape(-1, d)
        shared = jax.nn.silu(xf @ shared_w1.T) * (xf @ shared_w2.T) @ shared_w3.T
        scores = jax.nn.sigmoid(xf @ router_w.T)
        _, top_idx = jax.lax.top_k(scores + expert_bias, TOP_K)
        mask = jax.nn.one_hot(top_idx, N_EXPERTS, dtype=xf.dtype).sum(axis=-2)
        gates = scores * mask
        h12 = jnp.einsum('td,ehd->teh', xf, w12)
        h1, h2 = jnp.split(h12, 2, axis=-1)
        h = jax.nn.silu(h1) * h2 * gates[:, :, None]
        routed = jnp.einsum('teh,edh->td', h, w3)
        return (shared + routed).reshape(b, s, d)
    x = L0_attn_x
    x = x + 0.5 * _L0_ffn_ref(_layernorm(x, axis=-1), L0_ffn_w_router, L0_ffn_fc1_w, L0_ffn_fc2_w, L0_ffn_gate_w, L0_ffn_up_w, L0_ffn_down_w)
    x = x + _L0_attn_ref(_layernorm(x, axis=-1), L0_attn_time_decay, L0_attn_time_first, L0_attn_W_tm, L0_attn_g1, L0_attn_b1, L0_attn_tmk, L0_attn_tmv, L0_attn_tmr, L0_attn_W_cm, L0_attn_W_cp, L0_attn_g2, L0_attn_b2, L0_attn_cmk, L0_attn_cmr)
    x = x + 0.5 * _L0_ffn_ref(_layernorm(x, axis=-1), L0_ffn_w_router, L0_ffn_fc1_w, L0_ffn_fc2_w, L0_ffn_gate_w, L0_ffn_up_w, L0_ffn_down_w)
    x = x + 0.5 * _L1_ffn_ref(_layernorm(x, axis=-1), L1_ffn_w12, L1_ffn_w3, L1_ffn_shared_w1, L1_ffn_shared_w2, L1_ffn_shared_w3, L1_ffn_router_w, L1_ffn_expert_bias)
    x = x + _L1_attn_ref(_layernorm(x, axis=-1), L1_attn_W_in, L1_attn_W_dt, L1_attn_b_dt, L1_attn_W_B, L1_attn_W_C, L1_attn_W_out, L1_attn_A_log)
    x = x + 0.5 * _L1_ffn_ref(_layernorm(x, axis=-1), L1_ffn_w12, L1_ffn_w3, L1_ffn_shared_w1, L1_ffn_shared_w2, L1_ffn_shared_w3, L1_ffn_router_w, L1_ffn_expert_bias)
    return x

_drawn_inputs = setup_inputs


def setup_inputs(seed=0):
    import zlib

    import numpy as np

    out = dict(_drawn_inputs(seed))
    spreads = {'L0_attn_g1': (1.0, 0.6),
     'L0_attn_b1': (0.0, 0.1),
     'L0_attn_g2': (1.0, 0.6),
     'L0_attn_b2': (0.0, 0.706),
     'L1_attn_b_dt': (0.0, 0.8),
     'L1_ffn_expert_bias': (0.0, 0.8)}
    factors = {'L0_attn_W_cm': 3.395,
     'L0_ffn_w_router': 8.0,
     'L0_ffn_fc1_w': 8.0,
     'L0_ffn_fc2_w': 8.0,
     'L0_ffn_gate_w': 8.0,
     'L0_ffn_up_w': 8.0,
     'L0_ffn_down_w': 8.0,
     'L1_attn_W_dt': 4.286,
     'L1_attn_A_log': 8.0,
     'L1_ffn_w12': 8.0,
     'L1_ffn_w3': 8.0,
     'L1_ffn_shared_w1': 8.0,
     'L1_ffn_shared_w2': 8.0,
     'L1_ffn_shared_w3': 8.0,
     'L1_ffn_router_w': 8.0}
    for name, (base, spread) in spreads.items():
        noise = np.random.default_rng([zlib.crc32(name.encode()), seed]).standard_normal(out[name].shape)
        drawn = base * np.exp(spread * noise) if base else spread * noise
        out[name] = jnp.asarray(drawn.astype(out[name].dtype))
    for name, factor in factors.items():
        out[name] = (out[name] * factor).astype(out[name].dtype)
    return out
```

```python
from contextlib import ExitStack

import concourse.bass as bass
from concourse import mybir

ALU = mybir.AluOpType
ACT = mybir.ActivationFunctionType
F32 = mybir.dt.float32
F32R = mybir.dt.float32r
BF16 = mybir.dt.bfloat16
U32 = mybir.dt.uint32

P = 128
BATCH, SEQ = 8, 256
TOKENS = BATCH * SEQ
TILES = TOKENS // P
BT = 4
BLK = BT * P
NBLK = TILES // BT
EXPERTS = 8
LN_EPS = 1e-5

STAGES = ("ffn0", "rwkv", "ffn0", "ffn1", "mamba", "ffn1")


class Count:

    def __init__(self, sem):
        self.sem = sem
        self.base = 0

    def at(self, value):
        least = value if isinstance(value, int) else value.min_val
        assert least + self.base > 0
        return value + self.base


class FfnWeights:

    def __init__(self, sb, tag, shared):
        self.shared = shared
        self.units = shared + EXPERTS
        self.up = [sb(f"{tag}_up{s}", [P, self.units, 2, P], F32R) for s in ("hi", "lo")]
        self.down = [sb(f"{tag}_down{s}", [P, self.units, P], F32R) for s in ("hi", "lo")]
        self.router = [sb(f"{tag}_router{s}", [P, P], F32R) for s in ("hi", "lo")]


def split_phase(nc, c, sb, tag, jobs, extra):
    with ExitStack() as ctx:
        raws = [ctx.enter_context(sb(f"{tag}_rawbuf{k}", [P] + list(j[0]), F32)) for k, j in enumerate(jobs)]
        block = ctx.enter_context(nc.Block())

        @block.sync
        def _(sp):
            for k, (shape, parts, hi, lo) in enumerate(jobs):
                for view, source in parts:
                    sp.dma_start(view(raws[k]), source).then_inc(c[f"raw{k}"].sem, 16)
            for dst, source in extra:
                sp.dma_start(dst, source).then_inc(c["plain"].sem, 16)
            if extra:
                sp.wait_ge(c["plain"].sem, c["plain"].at(16 * len(extra)))

        @block.scalar
        def _(act):
            for k, (shape, parts, hi, lo) in enumerate(jobs):
                act.wait_ge(c[f"raw{k}"].sem, c[f"raw{k}"].at(16 * len(parts)))
                nc.scalar.copy(hi, raws[k][:]).then_inc(c["raw_hi"].sem, 1)

        @block.vector
        def _(dve):
            for k, (shape, parts, hi, lo) in enumerate(jobs):
                dve.wait_ge(c["raw_hi"].sem, c["raw_hi"].at(k + 1))
                nc.vector.tensor_tensor(lo, raws[k][:], hi.bitcast(F32), ALU.subtract)

    for k, (shape, parts, hi, lo) in enumerate(jobs):
        c[f"raw{k}"].base += 16 * len(parts)
    c["raw_hi"].base += len(jobs)
    c["plain"].base += 16 * len(extra)


def three_pass(pe, out, weights, moving, start, stop):
    pe.matmul(out, weights[0], moving[0], start=start, stop=False)
    pe.matmul(out, weights[0], moving[1], start=False, stop=False)
    return pe.matmul(out, weights[1], moving[0], start=False, stop=stop)


def ffn_phase(nc, tag, counts, spare, sb, ps, x, xt, consts, w, softmax, expert_bias):
    U, S = w.units, w.shared
    LEAD = 3
    HR = 5 if U % 5 == 0 else 4
    DVE_SLOTS = (0, 1, 3, 6, 7)
    PE_SLOTS = (2, 4, 5, 8)
    ACT_SLOTS = (2, 4, 6 if softmax else 5)
    xhi, xlo = xt
    c = counts
    credit = {"down": HR, "sil": 2, "p1": 2, "hhi": 2, "hlo": 2, "prod": 2, "row": 1, "acc_s": 1, "ot": 1, "out": 2}
    for name, k in credit.items():
        c[name].base += k
    with ExitStack() as ctx:
        def tile(name, shape, dt=F32):
            return ctx.enter_context(sb(f"{tag}_{name}", shape, dt))

        stats = tile("stats", [P, BT, 6])
        moments = tile("moments", [P, BT, 2])
        veps = tile("veps", [P, BT])
        rstd = tile("rstd", [P, BT])
        xn = tile("xn", [P, BT, P])
        logits_t = tile("logits_t", [EXPERTS, BLK])
        key = tile("key", [P, BT, EXPERTS])
        th = tile("th", [P, BT, EXPERTS])
        score = tile("score", [P, BT, EXPERTS])
        top = tile("top", [P, BT, 8])
        topi = tile("topi", [P, BT, 8], U32)
        hot = tile("hot", [P, 2, BT, EXPERTS])
        gap = tile("gap", [P, BT])
        gth = tile("gth", [P, BT])
        g12 = tile("g12", [P, 2, BT])
        hot1 = tile("hot1", [P, BT, EXPERTS])
        gates = tile("gates", [P, BT * EXPERTS * 32])
        gates_t = tile("gates_t", [P, 2, BLK])
        gate_row = tile("gate_row", [P, 2, BLK])
        sil = tile("sil", [P, 2, BLK])
        p1 = tile("p1", [P, 2, BLK])
        prod = tile("prod", [P, 2, BLK])
        hhi = tile("hhi", [P, HR, BLK], F32R)
        hlo = tile("hlo", [P, HR, BLK], F32R)
        acc_s = tile("acc_s", [P, BLK])
        ps_a = ctx.enter_context(ps(f"{tag}_ps_a", [P, 2, BLK], F32))
        ps_b = ctx.enter_context(ps(f"{tag}_ps_b", [P, 2, BLK], F32))
        ps_acc = ctx.enter_context(ps(f"{tag}_ps_acc", [P, BLK], F32))
        ps_t = ctx.enter_context(ps(f"{tag}_ps_t", [P, BLK], F32))
        ps_l = ctx.enter_context(ps(f"{tag}_ps_l", [P, BLK], F32))
        block = ctx.enter_context(nc.Block())
        gates_w = gates[:].rearrange("p (j e s) -> p j e s", j=BT, s=32)[:, :, :, 0]
        rank = consts["iota8"]

        def src(g):
            return prod[:, g % 2, :]

        @block.tensor
        def _(pe):
            def up(n, u):
                if u == 0:
                    pe.wait_ge(c["xlo"].sem, c["xlo"].at(n + 1))
                g = n * U + u
                xs = [xhi[:, bass.ts(n, BLK)], xlo[:, bass.ts(n, BLK)]]
                pe.wait_ge(c["sil"].sem, c["sil"].at(g - 1))
                three_pass(pe, ps_a[:, u % 2], [t[:, u, 0] for t in w.up], xs, True, True).then_inc(c["a"].sem, 1)
                pe.wait_ge(c["p1"].sem, c["p1"].at(g - 1))
                three_pass(pe, ps_b[:, u % 2], [t[:, u, 1] for t in w.up], xs, True, True).then_inc(c["b"].sem, 1)

            def down(n, u):
                g = n * U + u
                if u == 0:
                    pe.wait_ge(c["acc_s"].sem, c["acc_s"].at(n))
                pe.wait_ge(c["hlo"].sem, c["hlo"].at(g + 1))
                three_pass(pe, ps_acc[:], [t[:, u] for t in w.down], [hhi[:, u % HR], hlo[:, u % HR]],
                           u == 0, u == U - 1).then_inc(c["down"].sem, 1)

            def head(n, step):
                if step == 0:
                    pe.wait_ge(c["xn"].sem, c["xn"].at(n + 1))
                    for j in range(BT):
                        last = pe.transpose(ps_t[:, bass.ts(j, P)], xn[:, j], consts["ident"][:])
                    last.then_inc(c["xt"].sem, 1)
                if step == 1:
                    pe.wait_ge(c["xlo"].sem, c["xlo"].at(n + 1))
                    xs = [xhi[:, bass.ts(n, BLK)], xlo[:, bass.ts(n, BLK)]]
                    pe.wait_ge(c["out"].sem, c["out"].at(n - 1))
                    three_pass(pe, ps_l[:], [t[:] for t in w.router], xs, True, True).then_inc(c["lg"].sem, 1)
                if step == 2:
                    pe.wait_ge(c["lgs"].sem, c["lgs"].at(n + 1))
                    pe.sem_inc(spare["pe"], 1)
                    for j in range(BT):
                        last = pe.transpose(ps_t[:, bass.ts(j, EXPERTS)], logits_t[:, bass.ts(j, P)],
                                            consts["ident"][0:EXPERTS, 0:EXPERTS])
                    last.then_inc(c["lgt"].sem, 1)
                if step == 3:
                    pe.wait_ge(c["gates"].sem, c["gates"].at(n + 1))
                    for h, bank in enumerate((ps_t, ps_l)):
                        for j in range(BT):
                            last = pe.transpose(bank[:, bass.ts(j, P)], gates[:, (2 * j + h) * P:(2 * j + h + 1) * P],
                                                consts["ident"][:])
                    last.then_inc(c["gt"].sem, 1)

            def final(n):
                pe.wait_ge(c["acc_s"].sem, c["acc_s"].at(n + 1))
                pe.wait_ge(c["gts"].sem, c["gts"].at(n + 2 if has_next(n) else NBLK))
                for j in range(BT):
                    last = pe.transpose(ps_l[:, bass.ts(j, P)], acc_s[:, bass.ts(j, P)], consts["ident"][:])
                last.then_inc(c["ot"].sem, 1)

            def has_next(n):
                return not isinstance(n, int) or n + 1 < NBLK

            def body(n, more):
                for p in range(U):
                    u = p + LEAD
                    if u < U:
                        up(n, u)
                    elif more:
                        up(n + 1, u - U)
                    if p < U - 1:
                        down(n, p)
                    if p == U - 2:
                        down(n, U - 1)
                    if more and p in PE_SLOTS:
                        head(n + 1, PE_SLOTS.index(p))
                final(n)

            for name, k in credit.items():
                pe.sem_inc(c[name].sem, k)
            for step in range(4):
                head(0, step)
            for u in range(LEAD):
                up(0, u)
            with pe.Fori(0, NBLK - 1) as n:
                body(n, True)
            body(NBLK - 1, False)

        @block.scalar
        def _(act):
            def unit(n, u):
                g = n * U + u
                act.wait_ge(c["a"].sem, c["a"].at(g + 1))
                act.wait_ge(c["p1"].sem, c["p1"].at(g - 1))
                nc.scalar.activation(sil[:, u % 2], ps_a[:, u % 2], ACT.Silu).then_inc(c["sil"].sem, 1)

            def high(n, u):
                g = n * U + u
                if u < S:
                    act.wait_ge(c["p1"].sem, c["p1"].at(g + 1))
                else:
                    act.wait_ge(c["prod"].sem, c["prod"].at(n * EXPERTS + u - S + 1))
                act.wait_ge(c["down"].sem, c["down"].at(g + 1 - HR))
                nc.scalar.copy(hhi[:, u % HR], src(u)).then_inc(c["hhi"].sem, 1)

            def head(n, step):
                if step == 0:
                    act.wait_ge(c["xt"].sem, c["xt"].at(n + 1))
                    nc.scalar.copy(xhi[:, bass.ts(n, BLK)], ps_t[:]).then_inc(c["xhi"].sem, 1)
                if step == 1:
                    act.wait_ge(c["lg"].sem, c["lg"].at(n + 1))
                    nc.scalar.copy(logits_t[:], ps_l[0:EXPERTS, :]).then_inc(c["lgs"].sem, 1)
                if step == 2:
                    if softmax:
                        act.wait_ge(c["gap"].sem, c["gap"].at(n + 1))
                        nc.scalar.activation(gth[:], gap[:], ACT.Tanh, scale=0.5).then_inc(c["gth"].sem, 1)
                    else:
                        act.wait_ge(c["lgt"].sem, c["lgt"].at(n + 1))
                        nc.scalar.activation(th[:], ps_t[:, 0:BT * EXPERTS].rearrange("p (j e) -> p j e", j=BT),
                                             ACT.Tanh, scale=0.5).then_inc(c["gth"].sem, 1)

            def gates_out(n):
                act.wait_ge(c["gt"].sem, c["gt"].at(n + 1))
                act.wait_ge(c["row"].sem, c["row"].at(n * EXPERTS))
                nc.scalar.copy(gates_t[:, 0], ps_t[:])
                nc.scalar.copy(gates_t[:, 1], ps_l[:]).then_inc(c["gts"].sem, 1)

            def final(n):
                act.wait_ge(c["down"].sem, c["down"].at((n + 1) * U))
                act.wait_ge(c["ot"].sem, c["ot"].at(n))
                nc.scalar.copy(acc_s[:], ps_acc[:]).then_inc(c["acc_s"].sem, 1)

            def body(n, more):
                for p in range(U):
                    u = p + LEAD
                    if u < U:
                        unit(n, u)
                        high(n, u - 1)
                    elif more:
                        unit(n + 1, u - U)
                        if u == U:
                            high(n, U - 1)
                        else:
                            high(n + 1, u - U - 1)
                    elif u == U:
                        high(n, U - 1)
                    if more and p in ACT_SLOTS:
                        head(n + 1, ACT_SLOTS.index(p))
                if more:
                    gates_out(n + 1)
                final(n)

            for step in range(3):
                head(0, step)
            gates_out(0)
            for u in range(LEAD):
                unit(0, u)
                if u >= 1:
                    high(0, u - 1)
            with act.Fori(0, NBLK - 1) as n:
                body(n, True)
            body(NBLK - 1, False)

        @block.vector
        def _(dve):
            def unit(n, u):
                g = n * U + u
                dve.wait_ge(c["sil"].sem, c["sil"].at(g + 1))
                dve.wait_ge(c["b"].sem, c["b"].at(g + 1))
                if u < S:
                    dst = src(u)
                    dve.wait_ge(c["hhi"].sem, c["hhi"].at(g - 1))
                    dve.wait_ge(c["hlo"].sem, c["hlo"].at(g - 1))
                else:
                    dst = p1[:, u % 2]
                    dve.wait_ge(c["prod"].sem, c["prod"].at(n * EXPERTS + u - S - 1))
                nc.vector.tensor_tensor(dst, sil[:, u % 2], ps_b[:, u % 2], ALU.mult).then_inc(c["p1"].sem, 1)

            def low(n, u):
                g = n * U + u
                dve.wait_ge(c["hhi"].sem, c["hhi"].at(g + 1))
                nc.vector.tensor_tensor(hlo[:, u % HR], src(u), hhi[:, u % HR].bitcast(F32),
                                        ALU.subtract).then_inc(c["hlo"].sem, 1)

            def head(n, step):
                if step == 0:
                    for j in range(BT):
                        last = nc.vector.bn_stats(stats[:, j], x[:, n * BT + j])
                    last.then_inc(c["stats"].sem, 1)
                    dve.wait_ge(c["stats"].sem, c["stats"].at(n + 1))
                    dve.sem_inc(spare["dve"], 1)
                    for j in range(BT):
                        last = nc.vector.bn_aggr(moments[:, j], stats[:, j])
                    last.then_inc(c["moments"].sem, 1)
                if step == 1:
                    dve.wait_ge(c["rstd"].sem, c["rstd"].at(n + 1))
                    dve.wait_ge(c["moments"].sem, c["moments"].at(n + 1))
                    for j in range(BT):
                        last = nc.vector.tensor_scalar(xn[:, j], x[:, n * BT + j], moments[:, j, 0:1], rstd[:, j:j + 1],
                                                       ALU.subtract, ALU.mult)
                    last.then_inc(c["xn"].sem, 1)
                if step == 2:
                    dve.wait_ge(c["xhi"].sem, c["xhi"].at(n + 1))
                    nc.vector.tensor_tensor(xlo[:, bass.ts(n, BLK)], ps_t[:], xhi[:, bass.ts(n, BLK)].bitcast(F32),
                                            ALU.subtract).then_inc(c["xlo"].sem, 1)
                if step == 3:
                    k0 = 5 * n
                    if softmax:
                        dve.wait_ge(c["lgt"].sem, c["lgt"].at(n + 1))
                        nc.vector.tensor_copy(key[:], ps_t[:, 0:BT * EXPERTS].rearrange(
                            "p (j e) -> p j e", j=BT)).then_inc(c["route"].sem, 1)
                        dve.wait_ge(c["route"].sem, c["route"].at(k0 + 1))
                        dve.sem_inc(spare["dve"], 1)
                    else:
                        dve.wait_ge(c["gth"].sem, c["gth"].at(n + 1))
                        nc.vector.tensor_scalar(score[:], th[:], 0.5, 0.5, ALU.mult, ALU.add).then_inc(c["score"].sem, 1)
                        dve.wait_ge(c["score"].sem, c["score"].at(n + 1))
                        nc.vector.tensor_tensor(key[:], score[:], expert_bias[:].unsqueeze(1).broadcast_to([P, BT, EXPERTS]),
                                                ALU.add).then_inc(c["route"].sem, 1)
                        dve.wait_ge(c["route"].sem, c["route"].at(k0 + 1))
                        dve.sem_inc(spare["dve"], 1)
                    for j in range(BT):
                        last = nc.vector.max(top[:, j], key[:, j])
                    last.then_inc(c["route"].sem, 1)
                    dve.wait_ge(c["route"].sem, c["route"].at(k0 + 2))
                    dve.sem_inc(spare["dve"], 1)
                    for j in range(BT):
                        last = nc.vector.max_index(topi[:, j], top[:, j], key[:, j])
                    last.then_inc(c["route"].sem, 1)
                    if softmax:
                        nc.vector.tensor_tensor(gap[:], top[:, :, 0], top[:, :, 1], ALU.subtract).then_inc(c["gap"].sem, 1)
                    dve.wait_ge(c["route"].sem, c["route"].at(k0 + 3))
                    for k in range(2):
                        last = nc.vector.tensor_tensor(hot[:, k], rank[:], topi[:, :, k:k + 1].broadcast_to([P, BT, EXPERTS]),
                                                       ALU.is_equal)
                    last.then_inc(c["route"].sem, 1)
                if step == 4:
                    k0 = 5 * n
                    if softmax:
                        dve.wait_ge(c["gth"].sem, c["gth"].at(n + 1))
                        nc.vector.tensor_scalar(g12[:, 0], gth[:], 0.5, 0.5, ALU.mult, ALU.add)
                        nc.vector.tensor_scalar(g12[:, 1], gth[:], -0.5, 0.5, ALU.mult, ALU.add).then_inc(c["score"].sem, 1)
                        dve.wait_ge(c["score"].sem, c["score"].at(n + 1))
                        dve.wait_ge(c["route"].sem, c["route"].at(k0 + 4))
                        nc.vector.tensor_tensor(score[:], hot[:, 0], g12[:, 0].unsqueeze(2).broadcast_to([P, BT, EXPERTS]),
                                                ALU.mult)
                        nc.vector.tensor_tensor(hot1[:], hot[:, 1], g12[:, 1].unsqueeze(2).broadcast_to([P, BT, EXPERTS]),
                                                ALU.mult).then_inc(c["route"].sem, 1)
                        dve.wait_ge(c["route"].sem, c["route"].at(k0 + 5))
                        nc.vector.tensor_tensor(gates_w, score[:], hot1[:], ALU.add).then_inc(c["gates"].sem, 1)
                    else:
                        dve.wait_ge(c["route"].sem, c["route"].at(k0 + 4))
                        nc.vector.tensor_tensor(hot1[:], hot[:, 0], hot[:, 1], ALU.add).then_inc(c["route"].sem, 1)
                        dve.wait_ge(c["route"].sem, c["route"].at(k0 + 5))
                        nc.vector.tensor_tensor(gates_w, score[:], hot1[:], ALU.mult).then_inc(c["gates"].sem, 1)

            def final(n):
                dve.wait_ge(c["ot"].sem, c["ot"].at(n + 1))
                xb = x[:, bass.ts(n, BT)]
                nc.vector.scalar_tensor_tensor(out=xb, in0=ps_l[:].rearrange("p (j c) -> p j c", j=BT), scalar=0.5,
                                               in1=xb, op0=ALU.mult, op1=ALU.add).then_inc(c["out"].sem, 1)

            def body(n, more):
                for p in range(U):
                    u = p + LEAD
                    if u < U:
                        unit(n, u)
                        low(n, u - 1)
                    elif more:
                        unit(n + 1, u - U)
                        if u == U:
                            low(n, U - 1)
                        else:
                            low(n + 1, u - U - 1)
                    elif u == U:
                        low(n, U - 1)
                    if more and p in DVE_SLOTS:
                        head(n + 1, DVE_SLOTS.index(p))
                final(n)

            nc.vector.memset(gates[:], 0.0).then_inc(c["zero"].sem, 1)
            dve.wait_ge(c["zero"].sem, c["zero"].at(1))
            for step in range(5):
                head(0, step)
            for u in range(LEAD):
                unit(0, u)
                if u >= 1:
                    low(0, u - 1)
            with dve.Fori(0, NBLK - 1) as n:
                body(n, True)
            body(NBLK - 1, False)

        @block.gpsimd
        def _(pool):
            def row(n, e):
                g = n * EXPERTS + e
                if e == 0:
                    pool.wait_ge(c["gts"].sem, c["gts"].at(n + 1))
                pool.wait_ge(c["prod"].sem, c["prod"].at(g - 1 if e else g))
                pool.sem_inc(spare["pool"], 1)
                q = 32 * (e % 4)
                nc.gpsimd.partition_broadcast(gate_row[:, e % 2], gates_t[q:q + 1, e // 4], P).then_inc(c["row"].sem, 1)

            def weigh(n, e):
                g = n * EXPERTS + e
                u = S + e
                pool.wait_ge(c["row"].sem, c["row"].at(g + min(2, EXPERTS - e)))
                pool.wait_ge(c["p1"].sem, c["p1"].at(n * U + u + 1))
                pool.wait_ge(c["hlo"].sem, c["hlo"].at(n * U + u - 1))
                nc.gpsimd.tensor_tensor(src(u), p1[:, u % 2], gate_row[:, e % 2], ALU.mult).then_inc(c["prod"].sem, 1)

            def head(n):
                pool.wait_ge(c["moments"].sem, c["moments"].at(n + 1))
                pool.sem_inc(spare["pool"], 1)
                nc.gpsimd.tensor_scalar(veps[:], moments[:, :, 1], LN_EPS, None, ALU.add).then_inc(c["veps"].sem, 1)
                pool.wait_ge(c["veps"].sem, c["veps"].at(n + 1))
                nc.gpsimd.tensor_tensor(rstd[:], veps[:], consts["minus_half"][:], ALU.pow).then_inc(c["rstd"].sem, 1)

            def body(n, more):
                for e in range(EXPERTS):
                    if e == 0:
                        row(n, 0)
                    if e == 1 and more:
                        pool.wait_ge(c["rstd"].sem, c["rstd"].at(n + 2))
                        pool.sem_inc(spare["pool"], 1)
                    if e + 1 < EXPERTS:
                        row(n, e + 1)
                    weigh(n, e)
                    if e == 0 and more:
                        head(n + 1)

            head(0)
            with pool.Fori(0, NBLK - 1) as n:
                body(n, True)
            body(NBLK - 1, False)

    per = {"a": U, "b": U, "sil": U, "p1": U, "hhi": U, "hlo": U, "prod": EXPERTS, "row": EXPERTS, "route": 5}
    for name in ("xn", "xt", "xhi", "xlo", "lg", "lgs", "lgt", "gth", "gates", "gt", "gts", "acc_s", "ot", "out",
                 "stats", "moments", "veps", "rstd", "score"):
        per[name] = 1
    if softmax:
        per["gap"] = 1
    for name, k in per.items():
        c[name].base += k * NBLK
    c["down"].base += U * NBLK
    c["zero"].base += 1


def rwkv_phase(nc, counts, spare, sb, ps, x, xt, consts, w, v):
    LOW = -1e38
    NS = BLK // SEQ
    T1 = SEQ + 1
    c = counts
    credit = {"r_out": 1}
    for name, k in credit.items():
        c[name].base += k
    with ExitStack() as ctx:
        def tiles(name, shape, dt=F32):
            return [ctx.enter_context(sb(f"rw_{name}{h}", shape, dt)) for h in range(2)]

        stats = tiles("stats", [P, BT, 6])
        mom = tiles("mom", [P, BT, 2])
        rs = tiles("rs", [P, 7, BT])
        ytok = tiles("ytok", [P, BT, P])
        ztok = tiles("ztok", [P, BT, P])
        y0 = tiles("y0", [P, NS, T1])
        zf = tiles("zf", [P, BLK])
        xpk, xpv, xpr = tiles("xpk", [P, BLK]), tiles("xpv", [P, BLK]), tiles("xpr", [P, BLK])
        key, val = tiles("key", [P, NS, SEQ]), tiles("val", [P, NS, SEQ])
        rg = tiles("rg", [P, NS, SEQ])
        mx, bb, aa, x2 = (tiles(n, [P, NS, T1]) for n in ("mx", "bb", "aa", "x2"))
        t1, t2, t3, t4 = (tiles(n, [P, NS, SEQ]) for n in ("t1", "t2", "t3", "t4"))
        sq = tiles("sq", [P, BLK])
        shi, slo = tiles("shi", [P, 2, BLK], F32R), tiles("slo", [P, 2, BLK], F32R)
        b1 = ctx.enter_context(ps("rw_b1", [P, BLK], F32))
        b2 = ctx.enter_context(ps("rw_b2", [P, BLK], F32))
        ba, bv, bc = ([ctx.enter_context(ps(f"rw_{n}{h}", [P, BLK], F32)) for h in range(2)] for n in ("ba", "bv", "bc"))
        block = ctx.enter_context(nc.Block())
        ident = consts["ident"]

        def seqs(bank):
            return bank[:].rearrange("p (b t) -> p b t", b=NS)

        def tok(bank):
            return bank[:].rearrange("p (j c) -> p j c", j=BT)

        def mid(buf):
            return buf[:, :, 1:T1]

        def prev(buf):
            return buf[:, :, 0:SEQ]

        def blk(t, m):
            return t[:, bass.ts(m, BLK)]

        def w_row():
            return v["w"].broadcast_to([P, SEQ])

        @block.tensor
        def _(pe):
            def turn_ln(h, m):
                pe.wait_ge(c["r_tok"].sem, c["r_tok"].at(m + 1))
                if h == 0:
                    pe.wait_ge(c["r_out"].sem, c["r_out"].at(m))
                else:
                    pe.wait_ge(c["r_zf"].sem, c["r_zf"].at(m))
                for src, bank in ((ytok, b1), (ztok, b2)):
                    for j in range(BT):
                        last = pe.transpose(bank[:, bass.ts(j, P)], src[h][:, j], ident[:])
                last.then_inc(c["r_tt"].sem, 1)

            def kvr(h, m):
                pe.wait_ge(c["r_zl"].sem, c["r_zl"].at(m + 1))
                for q, bank in enumerate((ba[h], bv[h], bc[h])):
                    three_pass(pe, bank[:], [t[:, q] for t in w["tm"]], [blk(xt[0], m), blk(xt[1], m)],
                               True, True).then_inc(c["r_kvr"].sem, 1)

            def turn_x2(h, m):
                pe.wait_ge(c["r_x2"].sem, c["r_x2"].at(m + 1))
                if h == 0:
                    pe.wait_ge(c["r_zf"].sem, c["r_zf"].at(m + 2))
                else:
                    pe.wait_ge(c["r_tok2"].sem, c["r_tok2"].at(m))
                for j in range(BT):
                    b, s = j // 2, j % 2
                    last = pe.transpose(b1[:, bass.ts(j, P)], x2[h][:, b, 1 + s * P:1 + (s + 1) * P], ident[:])
                last.then_inc(c["r_t2"].sem, 1)

            def turn_ln2(h, m):
                pe.wait_ge(c["r_tok2"].sem, c["r_tok2"].at(m + 1))
                if h == 1:
                    pe.wait_ge(c["r_zf2"].sem, c["r_zf2"].at(m))
                for j in range(BT):
                    last = pe.transpose(b2[:, bass.ts(j, P)], ztok[h][:, j], ident[:])
                last.then_inc(c["r_t3"].sem, 1)

            def channel(h, m):
                pe.wait_ge(c["r_zl2"].sem, c["r_zl2"].at(m + 1))
                xs = [blk(xt[0], m), blk(xt[1], m)]

                def grow(j):
                    if j >= 2:
                        pe.wait_ge(c["r_kx"].sem, c["r_kx"].at(4 * m + j - 1))
                    three_pass(pe, (ba[h], bv[h])[j % 2][:], [t[:, j] for t in w["cm"]], xs, True, True).then_inc(c["r_kk"].sem, 1)

                def shrink(j):
                    pe.wait_ge(c["r_sl"].sem, c["r_sl"].at(4 * m + j + 1))
                    three_pass(pe, bc[h][:], [t[:, j] for t in w["cp"]], [shi[h][:, j % 2], slo[h][:, j % 2]],
                               j == 0, j == 3).then_inc(c["r_vv"].sem, 1)

                grow(0)
                grow(1)
                for j in range(4):
                    if j + 2 < 4:
                        grow(j + 2)
                    shrink(j)

            def turn_out(h, m):
                pe.wait_ge(c["r_o"].sem, c["r_o"].at(m + 1))
                if h == 0:
                    pe.wait_ge(c["r_tok2"].sem, c["r_tok2"].at(m + 2))
                else:
                    pe.wait_ge(c["r_out"].sem, c["r_out"].at(m))
                for j in range(BT):
                    b, s = j // 2, j % 2
                    last = pe.transpose(b1[:, bass.ts(j, P)], t4[h][:, b, s * P:(s + 1) * P], ident[:])
                last.then_inc(c["r_ot"].sem, 1)

            for name, k in credit.items():
                pe.sem_inc(c[name].sem, k)
            with pe.Fori(0, NBLK // 2) as i:
                for h in range(2):
                    turn_ln(h, i * 2 + h)
                for h in range(2):
                    kvr(h, i * 2 + h)
                for h in range(2):
                    turn_x2(h, i * 2 + h)
                for h in range(2):
                    turn_ln2(h, i * 2 + h)
                for h in range(2):
                    channel(h, i * 2 + h)
                for h in range(2):
                    turn_out(h, i * 2 + h)

        @block.scalar
        def _(act):
            A = nc.scalar.activation

            def take_ln(h, m):
                act.wait_ge(c["r_tt"].sem, c["r_tt"].at(m + 1))
                nc.scalar.copy(mid(y0[h]), seqs(b1))
                nc.scalar.copy(y0[h][:, :, 0:1], seqs(b1)[:, :, 0:1]).then_inc(c["r_y0"].sem, 1)
                A(zf[h][:], b2[:], ACT.Identity, bias=v["b1"], scale=v["g1"]).then_inc(c["r_zf"].sem, 1)
                act.wait_ge(c["r_zf"].sem, c["r_zf"].at(m + 1))
                act.sem_inc(spare["act"], 1)
                nc.scalar.copy(blk(xt[0], m), zf[h][:]).then_inc(c["r_zh"].sem, 1)

            def mixes(h, m):
                act.wait_ge(c["r_y0"].sem, c["r_y0"].at(m + 1))
                for q, dst in enumerate((xpk, xpv, xpr)):
                    last = A(dst[h][:].rearrange("p (b t) -> p b t", b=NS), prev(y0[h]), ACT.Copy, scale=v["om" + "kvr"[q]])
                last.then_inc(c["r_xp"].sem, 1)

            def decays(h, m):
                act.wait_ge(c["r_dm"].sem, c["r_dm"].at(m + 1))
                A(t1[h][:], t1[h][:], ACT.Exp, bias=v["w"])
                act.wait_ge(c["r_dk"].sem, c["r_dk"].at(m + 1))
                A(t2[h][:], t2[h][:], ACT.Exp).then_inc(c["r_d"].sem, 1)

            def logs(h, m):
                act.wait_ge(c["r_B"].sem, c["r_B"].at(m + 1))
                A(t3[h][:], t3[h][:], ACT.Ln).then_inc(c["r_ln"].sem, 1)

            def factors(h, m):
                act.wait_ge(c["r_a1"].sem, c["r_a1"].at(m + 1))
                A(t1[h][:], t1[h][:], ACT.Exp, bias=v["w"])
                act.wait_ge(c["r_a2"].sem, c["r_a2"].at(m + 1))
                A(t2[h][:], t2[h][:], ACT.Exp).then_inc(c["r_e"].sem, 1)

            def weights(h, m):
                act.wait_ge(c["r_r"].sem, c["r_r"].at(m + 1))
                A(rg[h][:], rg[h][:], ACT.Tanh, scale=0.5).then_inc(c["r_tr"].sem, 1)
                act.wait_ge(c["r_du"].sem, c["r_du"].at(m + 1))
                A(t3[h][:], t3[h][:], ACT.Tanh, bias=v["nuh"], scale=0.5).then_inc(c["r_th"].sem, 1)

            def take_ln2(h, m):
                act.wait_ge(c["r_t3"].sem, c["r_t3"].at(m + 1))
                A(zf[h][:], b2[:], ACT.Identity, bias=v["b2"], scale=v["g2"]).then_inc(c["r_zf2"].sem, 1)
                act.wait_ge(c["r_zf2"].sem, c["r_zf2"].at(m + 1))
                act.sem_inc(spare["act"], 1)
                nc.scalar.copy(blk(xt[0], m), zf[h][:]).then_inc(c["r_zh2"].sem, 1)

            def mixes2(h, m):
                act.wait_ge(c["r_x2w"].sem, c["r_x2w"].at(m + 1))
                A(xpk[h][:].rearrange("p (b t) -> p b t", b=NS), prev(x2[h]), ACT.Copy, scale=v["omck"])
                A(xpr[h][:].rearrange("p (b t) -> p b t", b=NS), prev(x2[h]), ACT.Copy, scale=v["omcr"]).then_inc(c["r_xp2"].sem, 1)

            def gate(h, m):
                act.wait_ge(c["r_rr"].sem, c["r_rr"].at(m + 1))
                A(rg[h][:].rearrange("p b t -> p (b t)"), xpr[h][:], ACT.Tanh, scale=0.5).then_inc(c["r_tr2"].sem, 1)

            def square_hi(h, m):
                for j in range(4):
                    act.wait_ge(c["r_sq"].sem, c["r_sq"].at(4 * m + j + 1))
                    if j >= 2:
                        act.wait_ge(c["r_vv"].sem, c["r_vv"].at(4 * m + j - 1))
                    nc.scalar.copy(shi[h][:, j % 2], sq[h][:]).then_inc(c["r_sh"].sem, 1)

            with act.Fori(0, NBLK // 2) as i:
                for h in range(2):
                    take_ln(h, i * 2 + h)
                for h in range(2):
                    mixes(h, i * 2 + h)
                for h in range(2):
                    decays(h, i * 2 + h)
                for h in range(2):
                    logs(h, i * 2 + h)
                for h in range(2):
                    factors(h, i * 2 + h)
                for h in range(2):
                    weights(h, i * 2 + h)
                for h in range(2):
                    mixes2(h, i * 2 + h)
                for h in range(2):
                    take_ln2(h, i * 2 + h)
                for h in range(2):
                    gate(h, i * 2 + h)
                for h in range(2):
                    square_hi(h, i * 2 + h)

        @block.vector
        def _(dve):
            V = nc.vector

            def ln_stats(h, m):
                for j in range(BT):
                    last = V.bn_stats(stats[h][:, j], x[:, m * BT + j])
                last.then_inc(c["r_st"].sem, 1)
                dve.wait_ge(c["r_st"].sem, c["r_st"].at(m + 1))
                dve.sem_inc(spare["dve"], 1)
                for j in range(BT):
                    last = V.bn_aggr(mom[h][:, j], stats[h][:, j])
                last.then_inc(c["r_mom"].sem, 1)

            def ln_apply(h, m):
                dve.wait_ge(c["r_rs"].sem, c["r_rs"].at(m + 1))
                for j in range(BT):
                    V.tensor_scalar(ytok[h][:, j], x[:, m * BT + j], mom[h][:, j, 0:1], rs[h][:, 1, j:j + 1],
                                    ALU.subtract, ALU.mult)
                    last = V.tensor_scalar(ztok[h][:, j], x[:, m * BT + j], mom[h][:, j, 0:1], rs[h][:, 6, j:j + 1],
                                           ALU.subtract, ALU.mult)
                last.then_inc(c["r_tok"].sem, 1)

            def low(h, m):
                dve.wait_ge(c["r_zh"].sem, c["r_zh"].at(m + 1))
                V.tensor_tensor(blk(xt[1], m), zf[h][:], blk(xt[0], m).bitcast(F32), ALU.subtract).then_inc(c["r_zl"].sem, 1)

            def mix(h, m):
                for q, (bank, xp, dst, name) in enumerate(((ba, xpk, key, "k"), (bv, xpv, val, "v"), (bc, xpr, rg, "r"))):
                    dve.wait_ge(c["r_kvr"].sem, c["r_kvr"].at(3 * m + q + 1))
                    dve.wait_ge(c["r_xp"].sem, c["r_xp"].at(m + 1))
                    V.scalar_tensor_tensor(out=dst[h][:], in0=seqs(bank[h]), scalar=v["tm" + name],
                                           in1=xp[h][:].rearrange("p (b t) -> p b t", b=NS),
                                           op0=ALU.mult, op1=ALU.add).then_inc(c["r_" + name].sem, 1)

            def running_max(h, m):
                dve.wait_ge(c["r_k"].sem, c["r_k"].at(m + 1))
                for b in range(NS):
                    last = V.tensor_tensor_scan(mx[h][:, b, 1:T1], w_row(), key[h][:, b], LOW, ALU.add, ALU.max)
                last.then_inc(c["r_M"].sem, 1)

            def max_step(h, m):
                dve.wait_ge(c["r_M"].sem, c["r_M"].at(m + 1))
                V.tensor_tensor(t1[h][:], prev(mx[h]), mid(mx[h]), ALU.subtract).then_inc(c["r_dm"].sem, 1)

            def sums(h, m):
                dve.wait_ge(c["r_d"].sem, c["r_d"].at(m + 1))
                for b in range(NS):
                    last = V.tensor_tensor_scan(t3[h][:, b], t1[h][:, b], t2[h][:, b], 0.0, ALU.mult, ALU.add)
                last.then_inc(c["r_B"].sem, 1)

            def log_state(h, m):
                dve.wait_ge(c["r_ln"].sem, c["r_ln"].at(m + 1))
                V.tensor_tensor(mid(bb[h]), mid(mx[h]), t3[h][:], ALU.add).then_inc(c["r_bb"].sem, 1)

            def peaks(h, m):
                dve.wait_ge(c["r_bb"].sem, c["r_bb"].at(m + 1))
                V.scalar_tensor_tensor(out=t4[h][:], in0=prev(bb[h]), scalar=v["w"], in1=key[h][:],
                                       op0=ALU.add, op1=ALU.max).then_inc(c["r_pm"].sem, 1)

            def peak_gap(h, m):
                dve.wait_ge(c["r_pm"].sem, c["r_pm"].at(m + 1))
                V.tensor_tensor(t1[h][:], prev(bb[h]), t4[h][:], ALU.subtract).then_inc(c["r_a1"].sem, 1)

            def numerator(h, m):
                dve.wait_ge(c["r_e"].sem, c["r_e"].at(m + 1))
                dve.wait_ge(c["r_v"].sem, c["r_v"].at(m + 1))
                V.tensor_tensor(t2[h][:], t2[h][:], val[h][:], ALU.mult).then_inc(c["r_ev"].sem, 1)

            def numerator_scan(h, m):
                dve.wait_ge(c["r_ev"].sem, c["r_ev"].at(m + 1))
                for b in range(NS):
                    last = V.tensor_tensor_scan(aa[h][:, b, 1:T1], t1[h][:, b], t2[h][:, b], 0.0, ALU.mult, ALU.add)
                last.then_inc(c["r_aa"].sem, 1)

            def diff(h, m):
                dve.wait_ge(c["r_aa"].sem, c["r_aa"].at(m + 1))
                V.tensor_tensor(t1[h][:], prev(aa[h]), val[h][:], ALU.subtract).then_inc(c["r_q"].sem, 1)

            def blend1(h, m):
                dve.wait_ge(c["r_q"].sem, c["r_q"].at(m + 1))
                dve.wait_ge(c["r_th"].sem, c["r_th"].at(m + 1))
                V.scalar_tensor_tensor(out=t1[h][:], in0=t3[h][:], scalar=1.0, in1=t1[h][:],
                                       op0=ALU.add, op1=ALU.mult).then_inc(c["r_q2"].sem, 1)

            def blend2(h, m):
                dve.wait_ge(c["r_q2"].sem, c["r_q2"].at(m + 1))
                V.scalar_tensor_tensor(out=t2[h][:], in0=t1[h][:], scalar=0.5, in1=val[h][:],
                                       op0=ALU.mult, op1=ALU.add).then_inc(c["r_y"].sem, 1)

            def receptance(h, m):
                dve.wait_ge(c["r_y"].sem, c["r_y"].at(m + 1))
                dve.wait_ge(c["r_tr"].sem, c["r_tr"].at(m + 1))
                V.scalar_tensor_tensor(out=t1[h][:], in0=rg[h][:], scalar=1.0, in1=t2[h][:],
                                       op0=ALU.add, op1=ALU.mult).then_inc(c["r_ry"].sem, 1)

            def add_x(h, m):
                dve.wait_ge(c["r_ry"].sem, c["r_ry"].at(m + 1))
                V.scalar_tensor_tensor(out=mid(x2[h]), in0=t1[h][:], scalar=0.5, in1=mid(y0[h]),
                                       op0=ALU.mult, op1=ALU.add).then_inc(c["r_x2"].sem, 1)

            def wrap_x(h, m):
                dve.wait_ge(c["r_x2"].sem, c["r_x2"].at(m + 1))
                V.tensor_copy(x2[h][:, :, 0:1], x2[h][:, :, SEQ:T1]).then_inc(c["r_x2w"].sem, 1)

            def ln2_stats(h, m):
                dve.wait_ge(c["r_t2"].sem, c["r_t2"].at(m + 1))
                for j in range(BT):
                    last = V.bn_stats(stats[h][:, j], b1[:, bass.ts(j, P)])
                last.then_inc(c["r_st2"].sem, 1)
                dve.wait_ge(c["r_st2"].sem, c["r_st2"].at(m + 1))
                dve.sem_inc(spare["dve"], 1)
                for j in range(BT):
                    last = V.bn_aggr(mom[h][:, j], stats[h][:, j])
                last.then_inc(c["r_mom2"].sem, 1)
                dve.wait_ge(c["r_rs2"].sem, c["r_rs2"].at(m + 1))
                for j in range(BT):
                    last = V.tensor_scalar(ztok[h][:, j], b1[:, bass.ts(j, P)], mom[h][:, j, 0:1], rs[h][:, 1, j:j + 1],
                                           ALU.subtract, ALU.mult)
                last.then_inc(c["r_tok2"].sem, 1)

            def low2(h, m):
                dve.wait_ge(c["r_zh2"].sem, c["r_zh2"].at(m + 1))
                V.tensor_tensor(blk(xt[1], m), zf[h][:], blk(xt[0], m).bitcast(F32), ALU.subtract).then_inc(c["r_zl2"].sem, 1)
                dve.wait_ge(c["r_xp2"].sem, c["r_xp2"].at(m + 1))
                V.scalar_tensor_tensor(out=xpr[h][:], in0=zf[h][:], scalar=v["cmr"], in1=xpr[h][:],
                                       op0=ALU.mult, op1=ALU.add).then_inc(c["r_rr"].sem, 1)

            def channel(h, m):
                for j in range(4):
                    dve.wait_ge(c["r_kk"].sem, c["r_kk"].at(4 * m + j + 1))
                    if j >= 1:
                        dve.wait_ge(c["r_sl"].sem, c["r_sl"].at(4 * m + j))
                    V.scalar_tensor_tensor(out=xpv[h][:], in0=(ba[h], bv[h])[j % 2][:], scalar=v["cmk"], in1=xpk[h][:],
                                           op0=ALU.mult, op1=ALU.add).then_inc(c["r_kx"].sem, 1)
                    dve.wait_ge(c["r_kx"].sem, c["r_kx"].at(4 * m + j + 1))
                    V.scalar_tensor_tensor(out=sq[h][:], in0=xpv[h][:], scalar=0.0, in1=xpv[h][:],
                                           op0=ALU.max, op1=ALU.mult).then_inc(c["r_sq"].sem, 1)
                    dve.wait_ge(c["r_sh"].sem, c["r_sh"].at(4 * m + j + 1))
                    V.tensor_tensor(slo[h][:, j % 2], sq[h][:], shi[h][:, j % 2].bitcast(F32),
                                    ALU.subtract).then_inc(c["r_sl"].sem, 1)

            def gated(h, m):
                dve.wait_ge(c["r_vv"].sem, c["r_vv"].at(4 * m + 4))
                dve.wait_ge(c["r_tr2"].sem, c["r_tr2"].at(m + 1))
                V.scalar_tensor_tensor(out=t1[h][:], in0=rg[h][:], scalar=1.0, in1=seqs(bc[h]),
                                       op0=ALU.add, op1=ALU.mult).then_inc(c["r_g"].sem, 1)
                dve.wait_ge(c["r_g"].sem, c["r_g"].at(m + 1))
                V.scalar_tensor_tensor(out=t4[h][:], in0=t1[h][:], scalar=0.5, in1=mid(x2[h]),
                                       op0=ALU.mult, op1=ALU.add).then_inc(c["r_o"].sem, 1)

            def add_out(h, m):
                dve.wait_ge(c["r_ot"].sem, c["r_ot"].at(m + 1))
                xb = x[:, bass.ts(m, BT)]
                V.tensor_tensor(xb, tok(b1), xb, ALU.add).then_inc(c["r_out"].sem, 1)

            for h in range(2):
                V.memset(mx[h][:, :, 0:1], LOW)
                V.memset(bb[h][:, :, 0:1], LOW)
                last = V.memset(aa[h][:, :, 0:1], 0.0)
            last.then_inc(c["r_pad"].sem, 1)
            dve.wait_ge(c["r_pad"].sem, c["r_pad"].at(1))
            with dve.Fori(0, NBLK // 2) as i:
                for h in range(2):
                    ln_stats(h, i * 2 + h)
                for h in range(2):
                    ln_apply(h, i * 2 + h)
                for h in range(2):
                    low(h, i * 2 + h)
                for h in range(2):
                    mix(h, i * 2 + h)
                for h in range(2):
                    running_max(h, i * 2 + h)
                for h in range(2):
                    max_step(h, i * 2 + h)
                for h in range(2):
                    sums(h, i * 2 + h)
                for h in range(2):
                    log_state(h, i * 2 + h)
                for h in range(2):
                    peaks(h, i * 2 + h)
                for h in range(2):
                    peak_gap(h, i * 2 + h)
                for h in range(2):
                    numerator(h, i * 2 + h)
                for h in range(2):
                    numerator_scan(h, i * 2 + h)
                for h in range(2):
                    diff(h, i * 2 + h)
                for h in range(2):
                    blend1(h, i * 2 + h)
                for h in range(2):
                    blend2(h, i * 2 + h)
                for h in range(2):
                    receptance(h, i * 2 + h)
                for h in range(2):
                    add_x(h, i * 2 + h)
                for h in range(2):
                    wrap_x(h, i * 2 + h)
                for h in range(2):
                    ln2_stats(h, i * 2 + h)
                for h in range(2):
                    low2(h, i * 2 + h)
                for h in range(2):
                    channel(h, i * 2 + h)
                for h in range(2):
                    gated(h, i * 2 + h)
                for h in range(2):
                    add_out(h, i * 2 + h)

        @block.gpsimd
        def _(pool):
            G = nc.gpsimd
            half = consts["minus_half"]

            def ln_scale(h, m):
                r, var = rs[h], mom[h][:, :, 1]
                pool.wait_ge(c["r_mom"].sem, c["r_mom"].at(m + 1))
                pool.sem_inc(spare["pool"], 1)
                G.tensor_scalar(r[:, 0], var, LN_EPS, None, ALU.add).then_inc(c["r_c1"].sem, 1)
                pool.wait_ge(c["r_c1"].sem, c["r_c1"].at(6 * m + 1))
                G.tensor_tensor(r[:, 1], r[:, 0], half[:], ALU.pow).then_inc(c["r_c1"].sem, 1)
                pool.wait_ge(c["r_c1"].sem, c["r_c1"].at(6 * m + 2))
                G.tensor_tensor(r[:, 2], r[:, 1], r[:, 1], ALU.mult).then_inc(c["r_c1"].sem, 1)
                pool.wait_ge(c["r_c1"].sem, c["r_c1"].at(6 * m + 3))
                G.tensor_tensor(r[:, 3], r[:, 2], var, ALU.mult).then_inc(c["r_c1"].sem, 1)
                pool.wait_ge(c["r_c1"].sem, c["r_c1"].at(6 * m + 4))
                pool.sem_inc(spare["pool"], 1)
                G.tensor_scalar(r[:, 4], r[:, 3], LN_EPS, None, ALU.add).then_inc(c["r_c1"].sem, 1)
                pool.wait_ge(c["r_c1"].sem, c["r_c1"].at(6 * m + 5))
                G.tensor_tensor(r[:, 5], r[:, 4], half[:], ALU.pow).then_inc(c["r_c1"].sem, 1)
                pool.wait_ge(c["r_c1"].sem, c["r_c1"].at(6 * m + 6))
                G.tensor_tensor(r[:, 6], r[:, 5], r[:, 1], ALU.mult).then_inc(c["r_rs"].sem, 1)

            def below_max(h, m):
                pool.wait_ge(c["r_M"].sem, c["r_M"].at(m + 1))
                G.tensor_tensor(t2[h][:], key[h][:], mid(mx[h]), ALU.subtract).then_inc(c["r_dk"].sem, 1)

            def below_peak(h, m):
                pool.wait_ge(c["r_pm"].sem, c["r_pm"].at(m + 1))
                G.tensor_tensor(t2[h][:], key[h][:], t4[h][:], ALU.subtract).then_inc(c["r_a2"].sem, 1)

            def bonus(h, m):
                pool.wait_ge(c["r_bb"].sem, c["r_bb"].at(m + 1))
                G.tensor_tensor(t3[h][:], prev(bb[h]), key[h][:], ALU.subtract).then_inc(c["r_du"].sem, 1)

            def ln2_scale(h, m):
                r = rs[h]
                pool.wait_ge(c["r_mom2"].sem, c["r_mom2"].at(m + 1))
                pool.sem_inc(spare["pool"], 1)
                G.tensor_scalar(r[:, 0], mom[h][:, :, 1], LN_EPS, None, ALU.add).then_inc(c["r_c2"].sem, 1)
                pool.wait_ge(c["r_c2"].sem, c["r_c2"].at(m + 1))
                G.tensor_tensor(r[:, 1], r[:, 0], half[:], ALU.pow).then_inc(c["r_rs2"].sem, 1)

            with pool.Fori(0, NBLK // 2) as i:
                for h in range(2):
                    ln_scale(h, i * 2 + h)
                for h in range(2):
                    below_max(h, i * 2 + h)
                for h in range(2):
                    below_peak(h, i * 2 + h)
                for h in range(2):
                    bonus(h, i * 2 + h)
                for h in range(2):
                    ln2_scale(h, i * 2 + h)

    per = {"r_kvr": 3, "r_kk": 4, "r_vv": 4, "r_kx": 4, "r_sq": 4, "r_sh": 4, "r_sl": 4, "r_c1": 6}
    for name in RWKV_SEMS:
        if name != "r_pad":
            c[name].base += per.get(name, 1) * NBLK


RWKV_SEMS = ("r_st r_mom r_rs r_tok r_tt r_y0 r_zf r_zh r_zl r_xp r_kvr r_k r_v r_r r_M r_dm r_dk r_d r_B r_ln r_bb r_pm "
             "r_a1 r_a2 r_e r_ev r_aa r_du r_tr r_th r_q r_q2 r_y r_ry r_x2 r_x2w r_t2 r_st2 r_mom2 r_rs2 r_tok2 r_t3 "
             "r_zf2 r_zh2 r_zl2 r_xp2 r_rr r_tr2 r_kk r_kx r_sq r_sh r_sl r_vv r_g r_o r_ot r_out r_c1 r_c2 r_pad").split()


HEADS, STATE, HEAD_DIM = 16, 64, 8

MAMBA_SEMS = ("m_st m_mom m_c m_rs m_tok m_t m_xh m_xl m_pj m_u m_na m_ex m_ln m_dt m_dA m_dh m_dl m_X m_zs m_bc m_bh m_bl "
              "m_sum m_ee m_Xd m_rh m_rl m_D m_E m_CB m_off m_s m_Y m_yo m_yb m_yt m_yT m_yh m_yl m_ow m_out").split()


def mamba_phase(nc, counts, spare, sb, ps, x, consts, w, v):
    c = counts
    credit = {"m_out": 1, "m_bl": 2, "m_s": 2, "m_off": 1, "m_E": 2}
    for name, k in credit.items():
        c[name].base += k
    GROUPS = HEADS // 4
    with ExitStack() as ctx:
        def tiles(name, shape, dt=F32):
            return [ctx.enter_context(sb(f"mb_{name}{h}", shape, dt)) for h in range(2)]

        stats, mom = tiles("stats", [P, 2, 6]), tiles("mom", [P, 2, 2])
        rs = tiles("rs", [P, 2, 2])
        xn = tiles("xn", [P, 2, P])
        xs = [tiles("xs" + p, [P, SEQ], F32R) for p in ("hi", "lo")]
        u, na, dt, dA = (tiles(n, [P, 2, HEADS]) for n in ("u", "na", "dt", "dA"))
        dAp = [tiles("dA" + p, [P, 2, HEADS], F32R) for p in ("hi", "lo")]
        xin, zs, ytok = (tiles(n, [P, 2, P]) for n in ("xin", "zs", "ytok"))
        ee = tiles("ee", [P, 2, HEADS])
        xd, yo = tiles("xd", [P, P]), tiles("yo", [P, P])
        bc = [tiles("bc" + p, [P, 4, 4, SEQ], F32R) for p in ("hi", "lo")]
        yT = [tiles("yT" + p, [P, SEQ], F32R) for p in ("hi", "lo")]
        rh, rl = tiles("rh", [P, 4, P], F32R), tiles("rl", [P, 4, P], F32R)
        ex = tiles("ex", [P, 4, P])
        sm = [tiles(f"sm{q}", [P, 4, P]) for q in range(2)]
        off = tiles("off", [P, 4, P])
        ps_d = [ctx.enter_context(ps(f"mb_d{t}", [P, 4, P], F32)) for t in range(2)]
        ps_c = [ctx.enter_context(ps(f"mb_c{t}", [P, 4, SEQ], F32)) for t in range(2)]
        ps_p = ctx.enter_context(ps("mb_p", [P, 2, SEQ], F32))
        ps_y = ctx.enter_context(ps("mb_y", [P, 512], F32))
        y_diag = [ps_y[:, 0:P], ps_y[:, P:2 * P]]
        y_off = ps_y[:, 2 * P:3 * P]
        ps_dt = ps_y[:, 384:416]
        ps_sum = ps_y[:, 416:448]
        block = ctx.enter_context(nc.Block())
        ident = consts["ident"]

        def head_of(q, k):
            return 4 * q + 2 * (k % 2) + k // 2

        def by_head(t):
            return t.rearrange("p (h d) -> p h d", d=HEAD_DIM)

        def spread(t):
            return t.unsqueeze(2).broadcast_to([P, HEADS, HEAD_DIM])

        @block.tensor
        def _(pe):
            def turn(h, m):
                pe.wait_ge(c["m_tok"].sem, c["m_tok"].at(m + 1))
                read = c["m_out"] if h == 0 else c["m_xl"]
                pe.wait_ge(read.sem, read.at(m))
                for t in range(2):
                    last = pe.transpose(ps_p[:, 0, bass.ts(t, P)], xn[h][:, t], ident[:])
                last.then_inc(c["m_t"].sem, 1)

            def project(h, m):
                if h == 0:
                    pe.wait_ge(c["m_xl"].sem, c["m_xl"].at(m + 2))
                else:
                    pe.wait_ge(c["m_xl"].sem, c["m_xl"].at(m + 1))
                    pe.wait_ge(c["m_X"].sem, c["m_X"].at(m))
                    pe.wait_ge(c["m_zs"].sem, c["m_zs"].at(m))
                    pe.wait_ge(c["m_u"].sem, c["m_u"].at(m))
                for t in range(2):
                    lhs = [q[h][:, bass.ts(t, P)] for q in xs]
                    for k, (a, b) in enumerate(((0, 0), (0, 1), (1, 0))):
                        pe.matmul(ps_p[:, t], lhs[a], w["in"][b][:], start=k == 0, stop=k == 2)
                    for k, (a, b) in enumerate(((0, 0), (0, 1), (1, 0))):
                        last = pe.matmul(ps_dt[:, bass.ts(t, HEADS)], lhs[a], w["dt"][b][:], start=k == 0, stop=k == 2)
                last.then_inc(c["m_pj"].sem, 1)

            def project_bc(h, m):
                for r in range(4):
                    pe.wait_ge(c["m_bl"].sem, c["m_bl"].at(4 * m + r - 1))
                    for j in range(4):
                        last = three_pass(pe, ps_c[r % 2][:, j], [t[:, r, bass.ts(j, P)] for t in w["bc"]],
                                          [q[h][:] for q in xs], True, True)
                    last.then_inc(c["m_bc"].sem, 1)

            def sums(h, m):
                pe.wait_ge(c["m_dl"].sem, c["m_dl"].at(m + 1))
                if h:
                    pe.wait_ge(c["m_ee"].sem, c["m_ee"].at(m))
                else:
                    pe.wait_ge(c["m_u"].sem, c["m_u"].at(m + 2))
                for t, tri in ((0, "gt"), (1, "le")):
                    for k in range(2):
                        last = pe.matmul(ps_sum[:, bass.ts(t, HEADS)], consts[tri][:], dAp[k][h][:, t], start=k == 0, stop=k == 1)
                last.then_inc(c["m_sum"].sem, 1)

            def groups(h, m):
                pe.wait_ge(c["m_bl"].sem, c["m_bl"].at(4 * m + (8 if h == 0 else 4)))
                def decay(q):
                    for t in range(2):
                        g = 8 * m + 2 * q + t
                        pe.wait_ge(c["m_rl"].sem, c["m_rl"].at(g + 1))
                        pe.wait_ge(c["m_rh"].sem, c["m_rh"].at(g + 1))
                        pe.wait_ge(c["m_E"].sem, c["m_E"].at(g - 1))
                        out = ps_d[t][:].rearrange("p h l -> p (h l)")
                        pe.matmul(out, consts["gt"][:], rh[t][:].rearrange("p h l -> p (h l)"), start=True, stop=False)
                        pe.matmul(out, consts["gt"][:], rl[t][:].rearrange("p h l -> p (h l)"), start=False, stop=False)
                        pe.matmul(out, consts["ident_r"][:], consts["never"][:].rearrange("p h l -> p (h l)"),
                                  start=False, stop=True).then_inc(c["m_D"].sem, 1)

                def products(q):
                    for t in range(2):
                        pe.wait_ge(c["m_s"].sem, c["m_s"].at(8 * m + 2 * q + t - 1))
                        if t == 0:
                            pe.wait_ge(c["m_off"].sem, c["m_off"].at(4 * m + q))
                        for k in (0, 2, 1, 3):
                            hd = head_of(q, k)
                            j, base = hd // 2, STATE * (hd % 2)
                            rows = slice(base, base + STATE)
                            bs = [s[h][rows, j // 4, j % 4, bass.ts(t, P)] for s in bc]
                            cs = [s[h][rows, 2 + j // 4, j % 4, t * P:SEQ] for s in bc]
                            last = three_pass(pe, ps_c[t][:, k, 0:SEQ - t * P], bs, cs, True, True)
                        last.then_inc(c["m_CB"].sem, 1)

                def outputs(q):
                    if q == 0:
                        pe.wait_ge(c["m_X"].sem, c["m_X"].at(m + 1))
                        pe.wait_ge(c["m_Xd"].sem, c["m_Xd"].at(m + 1))
                        if h:
                            pe.wait_ge(c["m_yt"].sem, c["m_yt"].at(m))
                        else:
                            pe.wait_ge(c["m_ee"].sem, c["m_ee"].at(m + 2))
                    pe.wait_ge(c["m_s"].sem, c["m_s"].at(8 * m + 2 * q + 2))
                    pe.wait_ge(c["m_off"].sem, c["m_off"].at(4 * m + q + 1))
                    for k in range(4):
                        hd = head_of(q, k)
                        col = slice(HEAD_DIM * hd, HEAD_DIM * (hd + 1))
                        for t in range(2):
                            pe.matmul(y_diag[t][:, col], sm[q % 2][t][:, k], xin[h][:, t, col], start=True, stop=True)
                        last = pe.matmul(y_off[:, col], off[q % 2][:, k], xd[h][:, col], start=True, stop=True)
                    last.then_inc(c["m_Y"].sem, 1)

                for q in range(GROUPS):
                    decay(q)
                    products(q)
                    if q:
                        outputs(q - 1)
                outputs(GROUPS - 1)

            def turn_y(h, m):
                pe.wait_ge(c["m_yt"].sem, c["m_yt"].at(m + 1))
                if h == 0:
                    pe.wait_ge(c["m_X"].sem, c["m_X"].at(m + 2))
                    pe.wait_ge(c["m_zs"].sem, c["m_zs"].at(m + 2))
                else:
                    pe.wait_ge(c["m_out"].sem, c["m_out"].at(m))
                for t in range(2):
                    last = pe.transpose(ps_p[:, 0, bass.ts(t, P)], ytok[h][:, t], ident[:])
                last.then_inc(c["m_yT"].sem, 1)

            def project_out(h, m):
                pe.wait_ge(c["m_yl"].sem, c["m_yl"].at(m + 1))
                for t in range(2):
                    for k, (a, b) in enumerate(((0, 0), (0, 1), (1, 0))):
                        last = pe.matmul(ps_p[:, 1, bass.ts(t, P)], yT[a][h][:, bass.ts(t, P)], w["out"][b][:],
                                         start=k == 0, stop=k == 2)
                last.then_inc(c["m_ow"].sem, 1)

            for name, k in credit.items():
                pe.sem_inc(c[name].sem, k)
            with pe.Fori(0, BATCH // 2) as i:
                for h in range(2):
                    turn(h, i * 2 + h)
                for h in range(2):
                    project(h, i * 2 + h)
                    project_bc(h, i * 2 + h)
                for h in range(2):
                    sums(h, i * 2 + h)
                for h in range(2):
                    groups(h, i * 2 + h)
                for h in range(2):
                    turn_y(h, i * 2 + h)
                    project_out(h, i * 2 + h)

        @block.scalar
        def _(act):
            A = nc.scalar.activation

            def take_x(h, m):
                act.wait_ge(c["m_t"].sem, c["m_t"].at(m + 1))
                nc.scalar.copy(xs[0][h][:], ps_p[:, 0]).then_inc(c["m_xh"].sem, 1)

            def gate_dt(h, m):
                act.wait_ge(c["m_pj"].sem, c["m_pj"].at(m + 1))
                A(zs[h][:], ps_p[:, :, P:2 * P], ACT.Silu).then_inc(c["m_zs"].sem, 1)
                act.wait_ge(c["m_na"].sem, c["m_na"].at(m + 1))
                A(na[h][:], na[h][:], ACT.Exp).then_inc(c["m_ex"].sem, 1)
                act.wait_ge(c["m_ex"].sem, c["m_ex"].at(m + 1))
                A(na[h][:], na[h][:], ACT.Ln, bias=1.0).then_inc(c["m_ln"].sem, 1)

            def take_bc(h, m):
                for r in range(4):
                    act.wait_ge(c["m_bc"].sem, c["m_bc"].at(4 * m + r + 1))
                    nc.scalar.copy(bc[0][h][:, r], ps_c[r % 2][:]).then_inc(c["m_bh"].sem, 1)

            def edge(h, m):
                act.wait_ge(c["m_sum"].sem, c["m_sum"].at(m + 1))
                A(ee[h][:], ps_sum.rearrange("p (t h) -> p t h", t=2), ACT.Exp).then_inc(c["m_ee"].sem, 1)

            def groups(h, m):
                for q in range(GROUPS):
                    for t in range(2):
                        g = 8 * m + 2 * q + t
                        act.wait_ge(c["m_D"].sem, c["m_D"].at(g + 1))
                        act.wait_ge(c["m_s"].sem, c["m_s"].at(g - 1))
                        A(ex[t][:], ps_d[t][:], ACT.Exp).then_inc(c["m_E"].sem, 1)
                        if t == 0:
                            act.wait_ge(c["m_CB"].sem, c["m_CB"].at(g + 1))
                            if q >= 2:
                                act.wait_ge(c["m_Y"].sem, c["m_Y"].at(4 * m + q - 1))
                            nc.scalar.copy(off[q % 2][:], ps_c[0][:, :, P:SEQ]).then_inc(c["m_off"].sem, 1)

            def take_y(h, m):
                act.wait_ge(c["m_yT"].sem, c["m_yT"].at(m + 1))
                nc.scalar.copy(yT[0][h][:], ps_p[:, 0]).then_inc(c["m_yh"].sem, 1)

            with act.Fori(0, BATCH // 2) as i:
                for h in range(2):
                    take_x(h, i * 2 + h)
                for h in range(2):
                    gate_dt(h, i * 2 + h)
                    take_bc(h, i * 2 + h)
                for h in range(2):
                    edge(h, i * 2 + h)
                for h in range(2):
                    groups(h, i * 2 + h)
                for h in range(2):
                    take_y(h, i * 2 + h)

        @block.vector
        def _(dve):
            V = nc.vector

            def norm(h, m):
                for j in range(2):
                    last = V.bn_stats(stats[h][:, j], x[:, m * 2 + j])
                last.then_inc(c["m_st"].sem, 1)
                dve.wait_ge(c["m_st"].sem, c["m_st"].at(m + 1))
                dve.sem_inc(spare["dve"], 1)
                for j in range(2):
                    last = V.bn_aggr(mom[h][:, j], stats[h][:, j])
                last.then_inc(c["m_mom"].sem, 1)

            def normed(h, m):
                dve.wait_ge(c["m_rs"].sem, c["m_rs"].at(m + 1))
                for j in range(2):
                    last = V.tensor_scalar(xn[h][:, j], x[:, m * 2 + j], mom[h][:, j, 0:1], rs[h][:, 1, j:j + 1],
                                           ALU.subtract, ALU.mult)
                last.then_inc(c["m_tok"].sem, 1)

            def low_x(h, m):
                dve.wait_ge(c["m_xh"].sem, c["m_xh"].at(m + 1))
                V.tensor_tensor(xs[1][h][:], ps_p[:, 0], xs[0][h][:].bitcast(F32), ALU.subtract).then_inc(c["m_xl"].sem, 1)

            def steps_dt(h, m):
                dve.wait_ge(c["m_pj"].sem, c["m_pj"].at(m + 1))
                V.tensor_tensor(u[h][:], ps_dt.rearrange("p (t h) -> p t h", t=2),
                                v["b_dt"][:].unsqueeze(1).broadcast_to([P, 2, HEADS]), ALU.add).then_inc(c["m_u"].sem, 1)
                dve.wait_ge(c["m_u"].sem, c["m_u"].at(m + 1))
                V.scalar_tensor_tensor(out=na[h][:], in0=u[h][:], scalar=-1.0, in1=u[h][:],
                                       op0=ALU.mult, op1=ALU.min).then_inc(c["m_na"].sem, 1)
                dve.wait_ge(c["m_ln"].sem, c["m_ln"].at(m + 1))
                V.scalar_tensor_tensor(out=dt[h][:], in0=u[h][:], scalar=0.0, in1=na[h][:],
                                       op0=ALU.max, op1=ALU.add).then_inc(c["m_dt"].sem, 1)
                dve.wait_ge(c["m_dt"].sem, c["m_dt"].at(m + 1))
                V.tensor_tensor(dA[h][:], dt[h][:], v["neg_a"][:].unsqueeze(1).broadcast_to([P, 2, HEADS]),
                                ALU.mult).then_inc(c["m_dA"].sem, 1)
                dve.wait_ge(c["m_zs"].sem, c["m_zs"].at(m + 1))
                for t in range(2):
                    last = V.tensor_tensor(by_head(xin[h][:, t]), by_head(ps_p[:, t, 0:P]), spread(dt[h][:, t]), ALU.mult)
                last.then_inc(c["m_X"].sem, 1)
                dve.wait_ge(c["m_dA"].sem, c["m_dA"].at(m + 1))
                V.tensor_copy(dAp[0][h][:], dA[h][:]).then_inc(c["m_dh"].sem, 1)
                dve.wait_ge(c["m_dh"].sem, c["m_dh"].at(m + 1))
                V.tensor_tensor(dAp[1][h][:], dA[h][:], dAp[0][h][:].bitcast(F32), ALU.subtract).then_inc(c["m_dl"].sem, 1)

            def low_bc(h, m):
                for r in range(4):
                    dve.wait_ge(c["m_bh"].sem, c["m_bh"].at(4 * m + r + 1))
                    V.tensor_tensor(bc[1][h][:, r], ps_c[r % 2][:], bc[0][h][:, r].bitcast(F32),
                                    ALU.subtract).then_inc(c["m_bl"].sem, 1)

            def decayed_x(h, m):
                dve.wait_ge(c["m_ee"].sem, c["m_ee"].at(m + 1))
                dve.wait_ge(c["m_X"].sem, c["m_X"].at(m + 1))
                V.tensor_tensor(by_head(xd[h][:]), by_head(xin[h][:, 0]), spread(ee[h][:, 0]), ALU.mult).then_inc(c["m_Xd"].sem, 1)

            def groups(h, m):
                def right(q, t):
                    g = 8 * m + 2 * q + t
                    if q == 0 and t == 0:
                        dve.wait_ge(c["m_dl"].sem, c["m_dl"].at(m + 1))
                    if q or h:
                        dve.wait_ge(c["m_D"].sem, c["m_D"].at(g - 1))
                    for k in range(4):
                        hd = head_of(q, k)
                        last = V.tensor_scalar(rh[t][:, k], consts["le_f"][:], dAp[0][h][:, t, hd:hd + 1].bitcast(F32),
                                               None, ALU.mult)
                    last.then_inc(c["m_rh"].sem, 1)

                def decayed(q, t):
                    g = 8 * m + 2 * q + t
                    dve.wait_ge(c["m_E"].sem, c["m_E"].at(g + 1))
                    dve.wait_ge(c["m_CB"].sem, c["m_CB"].at(g + 1))
                    if t == 0:
                        dve.wait_ge(c["m_off"].sem, c["m_off"].at(4 * m + q + 1))
                    if q >= 2:
                        dve.wait_ge(c["m_Y"].sem, c["m_Y"].at(4 * m + q - 1))
                    V.tensor_tensor(sm[q % 2][t][:], ex[t][:], ps_c[t][:, :, 0:P], ALU.mult).then_inc(c["m_s"].sem, 1)

                right(0, 0)
                right(0, 1)
                for q in range(GROUPS):
                    for t in range(2):
                        if q + 1 < GROUPS:
                            right(q + 1, t)
                        decayed(q, t)

            def gated(h, m):
                dve.wait_ge(c["m_Y"].sem, c["m_Y"].at(4 * m + 4))
                dve.wait_ge(c["m_zs"].sem, c["m_zs"].at(m + 1))
                V.tensor_tensor(by_head(yo[h][:]), by_head(y_off), spread(ee[h][:, 1]), ALU.mult).then_inc(c["m_yo"].sem, 1)
                V.tensor_tensor(ytok[h][:, 0], y_diag[0], zs[h][:, 0], ALU.mult)
                dve.wait_ge(c["m_yo"].sem, c["m_yo"].at(m + 1))
                V.tensor_tensor(yo[h][:], y_diag[1], yo[h][:], ALU.add).then_inc(c["m_yb"].sem, 1)
                dve.wait_ge(c["m_yb"].sem, c["m_yb"].at(m + 1))
                V.tensor_tensor(ytok[h][:, 1], yo[h][:], zs[h][:, 1], ALU.mult).then_inc(c["m_yt"].sem, 1)

            def low_y(h, m):
                dve.wait_ge(c["m_yh"].sem, c["m_yh"].at(m + 1))
                V.tensor_tensor(yT[1][h][:], ps_p[:, 0], yT[0][h][:].bitcast(F32), ALU.subtract).then_inc(c["m_yl"].sem, 1)

            def add_out(h, m):
                dve.wait_ge(c["m_ow"].sem, c["m_ow"].at(m + 1))
                xb = x[:, bass.ts(m, 2)]
                V.tensor_tensor(xb, ps_p[:, 1].rearrange("p (t c) -> p t c", t=2), xb, ALU.add).then_inc(c["m_out"].sem, 1)

            with dve.Fori(0, BATCH // 2) as i:
                for h in range(2):
                    norm(h, i * 2 + h)
                for h in range(2):
                    normed(h, i * 2 + h)
                for h in range(2):
                    low_x(h, i * 2 + h)
                for h in range(2):
                    steps_dt(h, i * 2 + h)
                    low_bc(h, i * 2 + h)
                for h in range(2):
                    decayed_x(h, i * 2 + h)
                for h in range(2):
                    groups(h, i * 2 + h)
                    gated(h, i * 2 + h)
                for h in range(2):
                    low_y(h, i * 2 + h)
                    add_out(h, i * 2 + h)

        @block.gpsimd
        def _(pool):
            G = nc.gpsimd

            def scale(h, m):
                pool.wait_ge(c["m_mom"].sem, c["m_mom"].at(m + 1))
                pool.sem_inc(spare["pool"], 1)
                G.tensor_scalar(rs[h][:, 0], mom[h][:, :, 1], LN_EPS, None, ALU.add).then_inc(c["m_c"].sem, 1)
                pool.wait_ge(c["m_c"].sem, c["m_c"].at(m + 1))
                G.tensor_tensor(rs[h][:, 1], rs[h][:, 0], consts["minus_half"][:, 0:2], ALU.pow).then_inc(c["m_rs"].sem, 1)

            def groups(h, m):
                pool.wait_ge(c["m_dl"].sem, c["m_dl"].at(m + 1))
                for q in range(GROUPS):
                    for t in range(2):
                        if q or h:
                            pool.wait_ge(c["m_D"].sem, c["m_D"].at(8 * m + 2 * q + t - 1))
                        part = dAp[1][h][:, t, 4 * q:4 * q + 4].bitcast(F32).rearrange("p (b a) -> p a b", a=2)
                        G.tensor_tensor(rl[t][:].rearrange("p (a b) l -> p a b l", a=2),
                                        consts["le_f"][:].unsqueeze(1).unsqueeze(1).broadcast_to([P, 2, 2, P]),
                                        part.unsqueeze(3).broadcast_to([P, 2, 2, P]), ALU.mult).then_inc(c["m_rl"].sem, 1)

            with pool.Fori(0, BATCH // 2) as i:
                for h in range(2):
                    scale(h, i * 2 + h)
                for h in range(2):
                    groups(h, i * 2 + h)

    per = {"m_bc": 4, "m_bh": 4, "m_bl": 4, "m_rh": 8, "m_rl": 8, "m_D": 8, "m_E": 8, "m_CB": 8, "m_off": 4, "m_s": 8, "m_Y": 4}
    for name in MAMBA_SEMS:
        c[name].base += per.get(name, 1) * BATCH


def program(nc, a, out):
    with ExitStack() as ctx:
        def sb(name, shape, dt):
            return ctx.enter_context(nc.sbuf_tensor(name, shape, dt))

        def sem(name):
            return ctx.enter_context(nc.semaphore(name))

        x = sb("x", [P, TILES, P], F32)
        xt = [sb(f"xt_{s}", [P, TOKENS], F32R) for s in ("hi", "lo")]
        consts = {
            "ident": sb("ident", [P, P], F32),
            "iota8": sb("iota8", [P, BT, EXPERTS], F32),
            "minus_half": sb("minus_half", [P, BT], F32),
        }
        bias = sb("bias", [P, EXPERTS], F32)
        names = ("a b sil p1 hhi hlo prod row down route xn xt xhi xlo lg lgs lgt gth gates gt gts acc_s ot out "
                 "stats moments veps rstd score gap zero raw0 raw1 raw2 raw3 raw4 raw_hi plain").split()
        counts = {n: Count(sem("s_" + n)) for n in names}
        counts.update({n: Count(sem(n)) for n in RWKV_SEMS})
        counts.update({n: Count(sem(n)) for n in MAMBA_SEMS})
        spare = {n: sem("spare_" + n) for n in ("pe", "act", "dve", "pool")}
        io = sem("io")
        w1 = FfnWeights(sb, "w1", 4)

        x_dram = a["L0_attn_x"].rearrange("b (h p) c -> p (b h) c", p=P)
        out_dram = out.rearrange("b (h p) c -> p (b h) c", p=P)

        def setup():
            made, ones = sem("made"), sem("ones")
            with nc.Block() as block:
                @block.gpsimd
                def _(pool):
                    nc.gpsimd.memset(consts["ident"][:], 0.0).then_inc(ones, 1)
                    nc.gpsimd.memset(consts["minus_half"][:], -0.5)
                    nc.gpsimd.iota(consts["iota8"][:], [[0, BT], [1, EXPERTS]], base=0, channel_multiplier=0,
                                   allow_small_or_imprecise_dtypes=True)
                    pool.wait_ge(ones, 1)
                    nc.gpsimd.affine_select(out=consts["ident"][:], in_=consts["ident"][:],
                                            compare_op=ALU.not_equal, fill=1.0, base=0, pattern=[[-1, P]],
                                            channel_multiplier=1).then_inc(made, 1)

                @block.sync
                def _(sp):
                    sp.dma_start(x[:], x_dram).then_inc(io, 16)
                    sp.dma_start(bias[:], a["L1_ffn_expert_bias"].rearrange("(a e) -> a e", a=1).broadcast_to(
                        [P, EXPERTS])).then_inc(io, 16)
                    sp.wait_ge(io, 32)

        def ffn_jobs(w, gate, up, down, e_up, e_down, router):
            S = w.shared
            jobs = [((S, 2, P), [(lambda r: r[:, :, 0], gate), (lambda r: r[:, :, 1], up)]) + tuple(t[:, 0:S] for t in w.up),
                    ((S, P), [(lambda r: r[:], down)]) + tuple(t[:, 0:S] for t in w.down)]
            for h in range(2):
                s = slice(S + 4 * h, S + 4 * h + 4)
                jobs.append(((4, 2, P), [(lambda r: r[:].rearrange("p e a c -> p e (a c)"), e_up[:, 4 * h:4 * h + 4])])
                            + tuple(t[:, s] for t in w.up))
            jobs.append(((EXPERTS, P), [(lambda r: r[:], e_down)]) + tuple(t[:, S:S + EXPERTS] for t in w.down))
            return jobs

        def router_job(w, name, router):
            s, d = sem(f"{name}_s"), sem(f"{name}_d")
            with nc.sbuf_tensor(f"{name}_raw", [P, P], F32) as raw, nc.Block() as block:
                @block.vector
                def _(dve):
                    nc.vector.memset(raw[:], 0.0).then_inc(s, 1)
                    dve.wait_ge(d, 16)
                    nc.vector.tensor_copy(w.router[0][:], raw[:]).then_inc(s, 1)
                    dve.wait_ge(s, 2)
                    nc.vector.tensor_tensor(w.router[1][:], raw[:], w.router[0][:].bitcast(F32), ALU.subtract)

                @block.sync
                def _(sp):
                    sp.wait_ge(s, 1)
                    sp.dma_start(raw[:, 0:EXPERTS], router).then_inc(d, 16)

        def ps(name, shape, dt):
            return nc.psum_tensor(name, shape, dt)

        def scoped(name, shape, dt):
            return nc.sbuf_tensor(name, shape, dt)

        def rwkv_stage():
            with ExitStack() as scope:
                def keep(name, shape, dt):
                    return scope.enter_context(nc.sbuf_tensor(name, shape, dt))

                w = {n: [keep(f"rw_{n}{s}", [P, k, P], F32R) for s in ("hi", "lo")]
                     for n, k in (("tm", 3), ("cm", 4), ("cp", 4))}
                names = {"w": "time_decay", "u": "time_first", "g1": "g1", "b1": "b1", "g2": "g2", "b2": "b2", "tmk": "tmk",
                         "tmv": "tmv", "tmr": "tmr", "cmk": "cmk", "cmr": "cmr"}
                vec = keep("rw_vec", [P, len(names) + 6], F32)
                v = {n: vec[:, k:k + 1] for k, n in enumerate(list(names) + ["omk", "omv", "omr", "omck", "omcr", "nuh"])}
                vectors = []
                for n, full in names.items():
                    d = a["L0_attn_" + full]
                    d = d.rearrange("(p q) -> p q", q=1) if len(d.shape) == 1 else d.rearrange("q r p -> p (q r)")
                    vectors.append((v[n], d))
                split_phase(nc, counts, scoped, "rw", [
                    ((3, P), [(lambda r: r[:].rearrange("p q c -> p (q c)"), a["L0_attn_W_tm"])]) + tuple(t[:] for t in w["tm"]),
                    ((4, P), [(lambda r: r[:].rearrange("p q c -> p (q c)"), a["L0_attn_W_cm"])]) + tuple(t[:] for t in w["cm"]),
                    ((4, P), [(lambda r: r[:], a["L0_attn_W_cp"].rearrange("(q p) c -> p q c", p=P))]) + tuple(t[:] for t in w["cp"]),
                ], vectors)
                with nc.Block() as block:
                    @block.vector
                    def _(dve):
                        for dst, src in (("omk", "tmk"), ("omv", "tmv"), ("omr", "tmr"), ("omck", "cmk"), ("omcr", "cmr")):
                            nc.vector.tensor_scalar(v[dst], v[src], -1.0, 1.0, ALU.mult, ALU.add)
                        nc.vector.tensor_scalar(v["nuh"], v["u"], -0.5, None, ALU.mult)
                rwkv_phase(nc, counts, spare, scoped, ps, x, xt, consts, w, v)

        def mamba_stage():
            with ExitStack() as scope:
                def keep(name, shape, dt):
                    return scope.enter_context(nc.sbuf_tensor(name, shape, dt))

                w = {n: [keep(f"mb_w{n}{s}", shape, F32R) for s in ("hi", "lo")]
                     for n, shape in (("in", [P, 2 * P]), ("dt", [P, HEADS]), ("bc", [P, 4, 4 * P]), ("out", [P, P]))}
                v = {"b_dt": keep("mb_bdt", [P, HEADS], F32), "neg_a": keep("mb_nega", [P, HEADS], F32)}
                a_log = keep("mb_alog", [P, HEADS], F32)
                a_exp = keep("mb_aexp", [P, HEADS], F32)
                tri = {"gt_f": keep("mb_gtf", [P, P], F32), "le_f": keep("mb_lef", [P, P], F32)}
                cm = dict(consts)
                cm.update(tri)
                for n, shape in (("gt", [P, P]), ("le", [P, P]), ("ident_r", [P, P]), ("never", [P, 4, P])):
                    cm[n] = keep("mb_" + n, shape, F32R)
                jobs = []
                for k, name in enumerate(("L1_attn_W_B", "L1_attn_W_C")):
                    jobs.append(((2, 4 * P), [(lambda r: r[:].rearrange("p r c -> p (r c)"), a[name])])
                                + tuple(t[:, 2 * k:2 * k + 2] for t in w["bc"]))
                for n, name, width in (("in", "L1_attn_W_in", 2 * P), ("dt", "L1_attn_W_dt", HEADS), ("out", "L1_attn_W_out", P)):
                    jobs.append(((width,), [(lambda r: r[:], a[name])]) + tuple(t[:] for t in w[n]))
                row = [P, HEADS]
                split_phase(nc, counts, scoped, "mb", jobs, [
                    (v["b_dt"][:], a["L1_attn_b_dt"].rearrange("(q e) -> q e", q=1).broadcast_to(row)),
                    (a_log[:], a["L1_attn_A_log"].rearrange("(q e) -> q e", q=1).broadcast_to(row))])
                made, done = sem("mb_made"), sem("mb_done")
                with nc.Block() as block:
                    @block.gpsimd
                    def _(pool):
                        G = nc.gpsimd
                        G.memset(cm["gt_f"][:], 1.0)
                        G.memset(cm["le_f"][:], 1.0).then_inc(made, 1)
                        pool.wait_ge(made, 1)
                        G.affine_select(out=cm["gt_f"][:], in_=cm["gt_f"][:], compare_op=ALU.is_gt, fill=0.0, base=0,
                                        pattern=[[-1, P]], channel_multiplier=1)
                        G.affine_select(out=cm["le_f"][:], in_=cm["le_f"][:], compare_op=ALU.is_ge, fill=0.0, base=0,
                                        pattern=[[1, P]], channel_multiplier=-1).then_inc(made, 1)

                    @block.scalar
                    def _(act):
                        nc.scalar.activation(a_exp[:], a_log[:], ACT.Exp).then_inc(done, 1)

                    @block.vector
                    def _(dve):
                        V = nc.vector
                        dve.wait_ge(done, 1)
                        V.tensor_scalar(v["neg_a"][:], a_exp[:], -1.0, None, ALU.mult)
                        V.tensor_copy(cm["ident_r"][:], consts["ident"][:])
                        dve.wait_ge(made, 2)
                        V.tensor_copy(cm["gt"][:], cm["gt_f"][:])
                        V.tensor_copy(cm["le"][:], cm["le_f"][:])
                        for k in range(4):
                            V.tensor_scalar(cm["never"][:, k], cm["gt_f"][:], -1e30, None, ALU.mult)
                mamba_phase(nc, counts, spare, scoped, ps, x, cm, w, v)

        setup()
        split_phase(nc, counts, scoped, "w1", ffn_jobs(
            w1, a["L1_ffn_shared_w1"].rearrange("d (s i) -> d s i", i=P), a["L1_ffn_shared_w2"].rearrange("d (s i) -> d s i", i=P),
            a["L1_ffn_shared_w3"].rearrange("(s i) c -> i s c", i=P), a["L1_ffn_w12"].rearrange("e d r -> d e r"),
            a["L1_ffn_w3"].rearrange("e r d -> r e d"), None), [])
        router_job(w1, "router1", a["L1_ffn_router_w"])
        w0 = None
        with ExitStack() as inner:
            if "ffn0" in STAGES:
                w0 = FfnWeights(lambda n, s, d: inner.enter_context(nc.sbuf_tensor(n, s, d)), "w0", 2)
                split_phase(nc, counts, scoped, "w0", ffn_jobs(
                    w0, a["L0_ffn_gate_w"].rearrange("d (s i) -> d s i", i=P), a["L0_ffn_up_w"].rearrange("d (s i) -> d s i", i=P),
                    a["L0_ffn_down_w"].rearrange("(s i) c -> i s c", i=P), a["L0_ffn_fc1_w"].rearrange("e d r -> d e r"),
                    a["L0_ffn_fc2_w"].rearrange("e i c -> i e c"), None), [])
                router_job(w0, "router0", a["L0_ffn_w_router"])
            for k, stage in enumerate(STAGES):
                if stage == "mamba":
                    inner.close()
                    mamba_stage()
                if stage == "ffn0":
                    ffn_phase(nc, f"p{k}", counts, spare, scoped, ps, x, xt, consts, w0, True, None)
                if stage == "rwkv":
                    rwkv_stage()
                if stage == "ffn1":
                    ffn_phase(nc, f"p{k}", counts, spare, scoped, ps, x, xt, consts, w1, False, bias)

        with nc.Block() as block:
            @block.sync
            def _(sp):
                sp.dma_start(out_dram, x[:]).then_inc(io, 16)
                sp.wait_ge(io, 48)


_INS = ["L0_attn_x", "L0_attn_time_decay", "L0_attn_time_first", "L0_attn_W_tm", "L0_attn_g1", "L0_attn_b1",
        "L0_attn_tmk", "L0_attn_tmv", "L0_attn_tmr", "L0_attn_W_cm", "L0_attn_W_cp", "L0_attn_g2", "L0_attn_b2",
        "L0_attn_cmk", "L0_attn_cmr", "L0_ffn_w_router", "L0_ffn_fc1_w", "L0_ffn_fc2_w", "L0_ffn_gate_w",
        "L0_ffn_up_w", "L0_ffn_down_w", "L1_attn_W_in", "L1_attn_W_dt", "L1_attn_b_dt", "L1_attn_W_B",
        "L1_attn_W_C", "L1_attn_W_out", "L1_attn_A_log", "L1_ffn_w12", "L1_ffn_w3", "L1_ffn_shared_w1",
        "L1_ffn_shared_w2", "L1_ffn_shared_w3", "L1_ffn_router_w", "L1_ffn_expert_bias"]
_TURNED = {"L1_attn_W_in", "L1_attn_W_dt", "L1_attn_W_B", "L1_attn_W_C", "L1_attn_W_out", "L1_ffn_w12", "L1_ffn_w3",
           "L1_ffn_shared_w1", "L1_ffn_shared_w2", "L1_ffn_shared_w3", "L1_ffn_router_w"}


def kernel(**inputs):
    import numpy as _np
    import concourse.bacc as _bacc
    from concourse import mybir as _mybir
    from concourse.bass_utils import run_bass_kernel_spmd as _run

    nc = _bacc.Bacc("TRN2", target_bir_lowering=False, num_devices=1)
    arrays, aps = {}, {}
    for name in _INS:
        v = _np.asarray(inputs[name])
        if name in _TURNED:
            v = _np.swapaxes(v, -1, -2)
        v = _np.ascontiguousarray(v)
        arrays[f"in_{name}_dram"] = v
        aps[name] = nc.dram_tensor(f"in_{name}_dram", v.shape, _mybir.dt.from_np(v.dtype), kind="ExternalInput").ap()
    out = nc.dram_tensor("out_0_dram", (BATCH, SEQ, P), F32, kind="ExternalOutput").ap()
    program(nc, aps, out)
    r = _run(nc, [arrays], core_ids=[0])
    return r.results[0]["out_0_dram"]
```

```python
from contextlib import ExitStack

import concourse.bass as bass
from concourse import mybir

ALU = mybir.AluOpType
ACT = mybir.ActivationFunctionType
F32 = mybir.dt.float32
F32R = mybir.dt.float32r
BF16 = mybir.dt.bfloat16
U32 = mybir.dt.uint32

P = 128
BATCH, SEQ = 8, 256
TOKENS = BATCH * SEQ
TILES = TOKENS // P
BT = 4
BLK = BT * P
NBLK = TILES // BT
EXPERTS = 8
LN_EPS = 1e-5

STAGES = ("ffn0", "rwkv", "ffn0", "ffn1", "mamba", "ffn1")


class Count:

    def __init__(self, sem):
        self.sem = sem
        self.base = 0

    def at(self, value):
        least = value if isinstance(value, int) else value.min_val
        assert least + self.base > 0
        return value + self.base


class FfnWeights:

    def __init__(self, sb, tag, shared):
        self.shared = shared
        self.units = shared + EXPERTS
        self.up = [sb(f"{tag}_up{s}", [P, self.units, 2, P], F32R) for s in ("hi", "lo")]
        self.down = [sb(f"{tag}_down{s}", [P, self.units, P], F32R) for s in ("hi", "lo")]
        self.router = [sb(f"{tag}_router{s}", [P, P], F32R) for s in ("hi", "lo")]


def split_phase(nc, c, sb, tag, jobs, extra):
    with ExitStack() as ctx:
        raws = [ctx.enter_context(sb(f"{tag}_rawbuf{k}", [P] + list(j[0]), F32)) for k, j in enumerate(jobs)]
        block = ctx.enter_context(nc.Block())

        @block.sync
        def _(sp):
            for k, (shape, parts, hi, lo) in enumerate(jobs):
                for view, source in parts:
                    sp.dma_start(view(raws[k]), source).then_inc(c[f"raw{k}"].sem, 16)
            for dst, source in extra:
                sp.dma_start(dst, source).then_inc(c["plain"].sem, 16)
            if extra:
                sp.wait_ge(c["plain"].sem, c["plain"].at(16 * len(extra)))

        @block.scalar
        def _(act):
            for k, (shape, parts, hi, lo) in enumerate(jobs):
                act.wait_ge(c[f"raw{k}"].sem, c[f"raw{k}"].at(16 * len(parts)))
                nc.scalar.copy(hi, raws[k][:]).then_inc(c["raw_hi"].sem, 1)

        @block.vector
        def _(dve):
            for k, (shape, parts, hi, lo) in enumerate(jobs):
                dve.wait_ge(c["raw_hi"].sem, c["raw_hi"].at(k + 1))
                nc.vector.tensor_tensor(lo, raws[k][:], hi.bitcast(F32), ALU.subtract)

    for k, (shape, parts, hi, lo) in enumerate(jobs):
        c[f"raw{k}"].base += 16 * len(parts)
    c["raw_hi"].base += len(jobs)
    c["plain"].base += 16 * len(extra)


def three_pass(pe, out, weights, moving, start, stop):
    pe.matmul(out, weights[0], moving[0], start=start, stop=False)
    pe.matmul(out, weights[0], moving[1], start=False, stop=False)
    return pe.matmul(out, weights[1], moving[0], start=False, stop=stop)


def ffn_phase(nc, tag, counts, spare, sb, ps, x, xt, consts, w, softmax, expert_bias):
    U, S = w.units, w.shared
    LEAD = 3
    HR = 5 if U % 5 == 0 else 4
    DVE_SLOTS = (0, 1, 3, 6, 7)
    PE_SLOTS = (2, 4, 5, 8)
    ACT_SLOTS = (2, 4, 6 if softmax else 5)
    xhi, xlo = xt
    c = counts
    credit = {"down": HR, "sil": 2, "p1": 2, "hhi": 2, "hlo": 2, "prod": 2, "row": 1, "acc_s": 1, "ot": 1, "out": 2}
    for name, k in credit.items():
        c[name].base += k
    with ExitStack() as ctx:
        def tile(name, shape, dt=F32):
            return ctx.enter_context(sb(f"{tag}_{name}", shape, dt))

        stats = tile("stats", [P, BT, 6])
        moments = tile("moments", [P, BT, 2])
        veps = tile("veps", [P, BT])
        rstd = tile("rstd", [P, BT])
        xn = tile("xn", [P, BT, P])
        logits_t = tile("logits_t", [EXPERTS, BLK])
        key = tile("key", [P, BT, EXPERTS])
        th = tile("th", [P, BT, EXPERTS])
        score = tile("score", [P, BT, EXPERTS])
        top = tile("top", [P, BT, 8])
        topi = tile("topi", [P, BT, 8], U32)
        hot = tile("hot", [P, 2, BT, EXPERTS])
        gap = tile("gap", [P, BT])
        gth = tile("gth", [P, BT])
        g12 = tile("g12", [P, 2, BT])
        hot1 = tile("hot1", [P, BT, EXPERTS])
        gates = tile("gates", [P, BT * EXPERTS * 32])
        gates_t = tile("gates_t", [P, 2, BLK])
        gate_row = tile("gate_row", [P, 2, BLK])
        sil = tile("sil", [P, 2, BLK])
        p1 = tile("p1", [P, 2, BLK])
        prod = tile("prod", [P, 2, BLK])
        hhi = tile("hhi", [P, HR, BLK], F32R)
        hlo = tile("hlo", [P, HR, BLK], F32R)
        acc_s = tile("acc_s", [P, BLK])
        ps_a = ctx.enter_context(ps(f"{tag}_ps_a", [P, 2, BLK], F32))
        ps_b = ctx.enter_context(ps(f"{tag}_ps_b", [P, 2, BLK], F32))
        ps_acc = ctx.enter_context(ps(f"{tag}_ps_acc", [P, BLK], F32))
        ps_t = ctx.enter_context(ps(f"{tag}_ps_t", [P, BLK], F32))
        ps_l = ctx.enter_context(ps(f"{tag}_ps_l", [P, BLK], F32))
        block = ctx.enter_context(nc.Block())
        gates_w = gates[:].rearrange("p (j e s) -> p j e s", j=BT, s=32)[:, :, :, 0]
        rank = consts["iota8"]

        def src(g):
            return prod[:, g % 2, :]

        @block.tensor
        def _(pe):
            def up(n, u):
                if u == 0:
                    pe.wait_ge(c["xlo"].sem, c["xlo"].at(n + 1))
                g = n * U + u
                xs = [xhi[:, bass.ts(n, BLK)], xlo[:, bass.ts(n, BLK)]]
                pe.wait_ge(c["sil"].sem, c["sil"].at(g - 1))
                three_pass(pe, ps_a[:, u % 2], [t[:, u, 0] for t in w.up], xs, True, True).then_inc(c["a"].sem, 1)
                pe.wait_ge(c["p1"].sem, c["p1"].at(g - 1))
                three_pass(pe, ps_b[:, u % 2], [t[:, u, 1] for t in w.up], xs, True, True).then_inc(c["b"].sem, 1)

            def down(n, u):
                g = n * U + u
                if u == 0:
                    pe.wait_ge(c["acc_s"].sem, c["acc_s"].at(n))
                pe.wait_ge(c["hlo"].sem, c["hlo"].at(g + 1))
                three_pass(pe, ps_acc[:], [t[:, u] for t in w.down], [hhi[:, u % HR], hlo[:, u % HR]],
                           u == 0, u == U - 1).then_inc(c["down"].sem, 1)

            def head(n, step):
                if step == 0:
                    pe.wait_ge(c["xn"].sem, c["xn"].at(n + 1))
                    for j in range(BT):
                        last = pe.transpose(ps_t[:, bass.ts(j, P)], xn[:, j], consts["ident"][:])
                    last.then_inc(c["xt"].sem, 1)
                if step == 1:
                    pe.wait_ge(c["xlo"].sem, c["xlo"].at(n + 1))
                    xs = [xhi[:, bass.ts(n, BLK)], xlo[:, bass.ts(n, BLK)]]
                    pe.wait_ge(c["out"].sem, c["out"].at(n - 1))
                    three_pass(pe, ps_l[:], [t[:] for t in w.router], xs, True, True).then_inc(c["lg"].sem, 1)
                if step == 2:
                    pe.wait_ge(c["lgs"].sem, c["lgs"].at(n + 1))
                    pe.sem_inc(spare["pe"], 1)
                    for j in range(BT):
                        last = pe.transpose(ps_t[:, bass.ts(j, EXPERTS)], logits_t[:, bass.ts(j, P)],
                                            consts["ident"][0:EXPERTS, 0:EXPERTS])
                    last.then_inc(c["lgt"].sem, 1)
                if step == 3:
                    pe.wait_ge(c["gates"].sem, c["gates"].at(n + 1))
                    for h, bank in enumerate((ps_t, ps_l)):
                        for j in range(BT):
                            last = pe.transpose(bank[:, bass.ts(j, P)], gates[:, (2 * j + h) * P:(2 * j + h + 1) * P],
                                                consts["ident"][:])
                    last.then_inc(c["gt"].sem, 1)

            def final(n):
                pe.wait_ge(c["acc_s"].sem, c["acc_s"].at(n + 1))
                pe.wait_ge(c["gts"].sem, c["gts"].at(n + 2 if has_next(n) else NBLK))
                for j in range(BT):
                    last = pe.transpose(ps_l[:, bass.ts(j, P)], acc_s[:, bass.ts(j, P)], consts["ident"][:])
                last.then_inc(c["ot"].sem, 1)

            def has_next(n):
                return not isinstance(n, int) or n + 1 < NBLK

            def body(n, more):
                for p in range(U):
                    u = p + LEAD
                    if u < U:
                        up(n, u)
                    elif more:
                        up(n + 1, u - U)
                    if p < U - 1:
                        down(n, p)
                    if p == U - 2:
                        down(n, U - 1)
                    if more and p in PE_SLOTS:
                        head(n + 1, PE_SLOTS.index(p))
                final(n)

            for name, k in credit.items():
                pe.sem_inc(c[name].sem, k)
            for step in range(4):
                head(0, step)
            for u in range(LEAD):
                up(0, u)
            with pe.Fori(0, NBLK - 1) as n:
                body(n, True)
            body(NBLK - 1, False)

        @block.scalar
        def _(act):
            def unit(n, u):
                g = n * U + u
                act.wait_ge(c["a"].sem, c["a"].at(g + 1))
                act.wait_ge(c["p1"].sem, c["p1"].at(g - 1))
                nc.scalar.activation(sil[:, u % 2], ps_a[:, u % 2], ACT.Silu).then_inc(c["sil"].sem, 1)

            def high(n, u):
                g = n * U + u
                if u < S:
                    act.wait_ge(c["p1"].sem, c["p1"].at(g + 1))
                else:
                    act.wait_ge(c["prod"].sem, c["prod"].at(n * EXPERTS + u - S + 1))
                act.wait_ge(c["down"].sem, c["down"].at(g + 1 - HR))
                nc.scalar.copy(hhi[:, u % HR], src(u)).then_inc(c["hhi"].sem, 1)

            def head(n, step):
                if step == 0:
                    act.wait_ge(c["xt"].sem, c["xt"].at(n + 1))
                    nc.scalar.copy(xhi[:, bass.ts(n, BLK)], ps_t[:]).then_inc(c["xhi"].sem, 1)
                if step == 1:
                    act.wait_ge(c["lg"].sem, c["lg"].at(n + 1))
                    nc.scalar.copy(logits_t[:], ps_l[0:EXPERTS, :]).then_inc(c["lgs"].sem, 1)
                if step == 2:
                    if softmax:
                        act.wait_ge(c["gap"].sem, c["gap"].at(n + 1))
                        nc.scalar.activation(gth[:], gap[:], ACT.Tanh, scale=0.5).then_inc(c["gth"].sem, 1)
                    else:
                        act.wait_ge(c["lgt"].sem, c["lgt"].at(n + 1))
                        nc.scalar.activation(th[:], ps_t[:, 0:BT * EXPERTS].rearrange("p (j e) -> p j e", j=BT),
                                             ACT.Tanh, scale=0.5).then_inc(c["gth"].sem, 1)

            def gates_out(n):
                act.wait_ge(c["gt"].sem, c["gt"].at(n + 1))
                act.wait_ge(c["row"].sem, c["row"].at(n * EXPERTS))
                nc.scalar.copy(gates_t[:, 0], ps_t[:])
                nc.scalar.copy(gates_t[:, 1], ps_l[:]).then_inc(c["gts"].sem, 1)

            def final(n):
                act.wait_ge(c["down"].sem, c["down"].at((n + 1) * U))
                act.wait_ge(c["ot"].sem, c["ot"].at(n))
                nc.scalar.copy(acc_s[:], ps_acc[:]).then_inc(c["acc_s"].sem, 1)

            def body(n, more):
                for p in range(U):
                    u = p + LEAD
                    if u < U:
                        unit(n, u)
                        high(n, u - 1)
                    elif more:
                        unit(n + 1, u - U)
                        if u == U:
                            high(n, U - 1)
                        else:
                            high(n + 1, u - U - 1)
                    elif u == U:
                        high(n, U - 1)
                    if more and p in ACT_SLOTS:
                        head(n + 1, ACT_SLOTS.index(p))
                if more:
                    gates_out(n + 1)
                final(n)

            for step in range(3):
                head(0, step)
            gates_out(0)
            for u in range(LEAD):
                unit(0, u)
                if u >= 1:
                    high(0, u - 1)
            with act.Fori(0, NBLK - 1) as n:
                body(n, True)
            body(NBLK - 1, False)

        @block.vector
        def _(dve):
            def unit(n, u):
                g = n * U + u
                dve.wait_ge(c["sil"].sem, c["sil"].at(g + 1))
                dve.wait_ge(c["b"].sem, c["b"].at(g + 1))
                if u < S:
                    dst = src(u)
                    dve.wait_ge(c["hhi"].sem, c["hhi"].at(g - 1))
                    dve.wait_ge(c["hlo"].sem, c["hlo"].at(g - 1))
                else:
                    dst = p1[:, u % 2]
                    dve.wait_ge(c["prod"].sem, c["prod"].at(n * EXPERTS + u - S - 1))
                nc.vector.tensor_tensor(dst, sil[:, u % 2], ps_b[:, u % 2], ALU.mult).then_inc(c["p1"].sem, 1)

            def low(n, u):
                g = n * U + u
                dve.wait_ge(c["hhi"].sem, c["hhi"].at(g + 1))
                nc.vector.tensor_tensor(hlo[:, u % HR], src(u), hhi[:, u % HR].bitcast(F32),
                                        ALU.subtract).then_inc(c["hlo"].sem, 1)

            def head(n, step):
                if step == 0:
                    for j in range(BT):
                        last = nc.vector.bn_stats(stats[:, j], x[:, n * BT + j])
                    last.then_inc(c["stats"].sem, 1)
                    dve.wait_ge(c["stats"].sem, c["stats"].at(n + 1))
                    dve.sem_inc(spare["dve"], 1)
                    for j in range(BT):
                        last = nc.vector.bn_aggr(moments[:, j], stats[:, j])
                    last.then_inc(c["moments"].sem, 1)
                if step == 1:
                    dve.wait_ge(c["rstd"].sem, c["rstd"].at(n + 1))
                    dve.wait_ge(c["moments"].sem, c["moments"].at(n + 1))
                    for j in range(BT):
                        last = nc.vector.tensor_scalar(xn[:, j], x[:, n * BT + j], moments[:, j, 0:1], rstd[:, j:j + 1],
                                                       ALU.subtract, ALU.mult)
                    last.then_inc(c["xn"].sem, 1)
                if step == 2:
                    dve.wait_ge(c["xhi"].sem, c["xhi"].at(n + 1))
                    nc.vector.tensor_tensor(xlo[:, bass.ts(n, BLK)], ps_t[:], xhi[:, bass.ts(n, BLK)].bitcast(F32),
                                            ALU.subtract).then_inc(c["xlo"].sem, 1)
                if step == 3:
                    k0 = 5 * n
                    if softmax:
                        dve.wait_ge(c["lgt"].sem, c["lgt"].at(n + 1))
                        nc.vector.tensor_copy(key[:], ps_t[:, 0:BT * EXPERTS].rearrange(
                            "p (j e) -> p j e", j=BT)).then_inc(c["route"].sem, 1)
                        dve.wait_ge(c["route"].sem, c["route"].at(k0 + 1))
                        dve.sem_inc(spare["dve"], 1)
                    else:
                        dve.wait_ge(c["gth"].sem, c["gth"].at(n + 1))
                        nc.vector.tensor_scalar(score[:], th[:], 0.5, 0.5, ALU.mult, ALU.add).then_inc(c["score"].sem, 1)
                        dve.wait_ge(c["score"].sem, c["score"].at(n + 1))
                        nc.vector.tensor_tensor(key[:], score[:], expert_bias[:].unsqueeze(1).broadcast_to([P, BT, EXPERTS]),
                                                ALU.add).then_inc(c["route"].sem, 1)
                        dve.wait_ge(c["route"].sem, c["route"].at(k0 + 1))
                        dve.sem_inc(spare["dve"], 1)
                    for j in range(BT):
                        last = nc.vector.max(top[:, j], key[:, j])
                    last.then_inc(c["route"].sem, 1)
                    dve.wait_ge(c["route"].sem, c["route"].at(k0 + 2))
                    dve.sem_inc(spare["dve"], 1)
                    for j in range(BT):
                        last = nc.vector.max_index(topi[:, j], top[:, j], key[:, j])
                    last.then_inc(c["route"].sem, 1)
                    if softmax:
                        nc.vector.tensor_tensor(gap[:], top[:, :, 0], top[:, :, 1], ALU.subtract).then_inc(c["gap"].sem, 1)
                    dve.wait_ge(c["route"].sem, c["route"].at(k0 + 3))
                    for k in range(2):
                        last = nc.vector.tensor_tensor(hot[:, k], rank[:], topi[:, :, k:k + 1].broadcast_to([P, BT, EXPERTS]),
                                                       ALU.is_equal)
                    last.then_inc(c["route"].sem, 1)
                if step == 4:
                    k0 = 5 * n
                    if softmax:
                        dve.wait_ge(c["gth"].sem, c["gth"].at(n + 1))
                        nc.vector.tensor_scalar(g12[:, 0], gth[:], 0.5, 0.5, ALU.mult, ALU.add)
                        nc.vector.tensor_scalar(g12[:, 1], gth[:], -0.5, 0.5, ALU.mult, ALU.add).then_inc(c["score"].sem, 1)
                        dve.wait_ge(c["score"].sem, c["score"].at(n + 1))
                        dve.wait_ge(c["route"].sem, c["route"].at(k0 + 4))
                        nc.vector.tensor_tensor(score[:], hot[:, 0], g12[:, 0].unsqueeze(2).broadcast_to([P, BT, EXPERTS]),
                                                ALU.mult)
                        nc.vector.tensor_tensor(hot1[:], hot[:, 1], g12[:, 1].unsqueeze(2).broadcast_to([P, BT, EXPERTS]),
                                                ALU.mult).then_inc(c["route"].sem, 1)
                        dve.wait_ge(c["route"].sem, c["route"].at(k0 + 5))
                        nc.vector.tensor_tensor(gates_w, score[:], hot1[:], ALU.add).then_inc(c["gates"].sem, 1)
                    else:
                        dve.wait_ge(c["route"].sem, c["route"].at(k0 + 4))
                        nc.vector.tensor_tensor(hot1[:], hot[:, 0], hot[:, 1], ALU.add).then_inc(c["route"].sem, 1)
                        dve.wait_ge(c["route"].sem, c["route"].at(k0 + 5))
                        nc.vector.tensor_tensor(gates_w, score[:], hot1[:], ALU.mult).then_inc(c["gates"].sem, 1)

            def final(n):
                dve.wait_ge(c["ot"].sem, c["ot"].at(n + 1))
                xb = x[:, bass.ts(n, BT)]
                nc.vector.scalar_tensor_tensor(out=xb, in0=ps_l[:].rearrange("p (j c) -> p j c", j=BT), scalar=0.5,
                                               in1=xb, op0=ALU.mult, op1=ALU.add).then_inc(c["out"].sem, 1)

            def body(n, more):
                for p in range(U):
                    u = p + LEAD
                    if u < U:
                        unit(n, u)
                        low(n, u - 1)
                    elif more:
                        unit(n + 1, u - U)
                        if u == U:
                            low(n, U - 1)
                        else:
                            low(n + 1, u - U - 1)
                    elif u == U:
                        low(n, U - 1)
                    if more and p in DVE_SLOTS:
                        head(n + 1, DVE_SLOTS.index(p))
                final(n)

            nc.vector.memset(gates[:], 0.0).then_inc(c["zero"].sem, 1)
            dve.wait_ge(c["zero"].sem, c["zero"].at(1))
            for step in range(5):
                head(0, step)
            for u in range(LEAD):
                unit(0, u)
                if u >= 1:
                    low(0, u - 1)
            with dve.Fori(0, NBLK - 1) as n:
                body(n, True)
            body(NBLK - 1, False)

        @block.gpsimd
        def _(pool):
            def row(n, e):
                g = n * EXPERTS + e
                if e == 0:
                    pool.wait_ge(c["gts"].sem, c["gts"].at(n + 1))
                pool.wait_ge(c["prod"].sem, c["prod"].at(g - 1 if e else g))
                pool.sem_inc(spare["pool"], 1)
                q = 32 * (e % 4)
                nc.gpsimd.partition_broadcast(gate_row[:, e % 2], gates_t[q:q + 1, e // 4], P).then_inc(c["row"].sem, 1)

            def weigh(n, e):
                g = n * EXPERTS + e
                u = S + e
                pool.wait_ge(c["row"].sem, c["row"].at(g + min(2, EXPERTS - e)))
                pool.wait_ge(c["p1"].sem, c["p1"].at(n * U + u + 1))
                pool.wait_ge(c["hlo"].sem, c["hlo"].at(n * U + u - 1))
                nc.gpsimd.tensor_tensor(src(u), p1[:, u % 2], gate_row[:, e % 2], ALU.mult).then_inc(c["prod"].sem, 1)

            def head(n):
                pool.wait_ge(c["moments"].sem, c["moments"].at(n + 1))
                pool.sem_inc(spare["pool"], 1)
                nc.gpsimd.tensor_scalar(veps[:], moments[:, :, 1], LN_EPS, None, ALU.add).then_inc(c["veps"].sem, 1)
                pool.wait_ge(c["veps"].sem, c["veps"].at(n + 1))
                nc.gpsimd.tensor_tensor(rstd[:], veps[:], consts["minus_half"][:], ALU.pow).then_inc(c["rstd"].sem, 1)

            def body(n, more):
                for e in range(EXPERTS):
                    if e == 0:
                        row(n, 0)
                    if e == 1 and more:
                        pool.wait_ge(c["rstd"].sem, c["rstd"].at(n + 2))
                        pool.sem_inc(spare["pool"], 1)
                    if e + 1 < EXPERTS:
                        row(n, e + 1)
                    weigh(n, e)
                    if e == 0 and more:
                        head(n + 1)

            head(0)
            with pool.Fori(0, NBLK - 1) as n:
                body(n, True)
            body(NBLK - 1, False)

    per = {"a": U, "b": U, "sil": U, "p1": U, "hhi": U, "hlo": U, "prod": EXPERTS, "row": EXPERTS, "route": 5}
    for name in ("xn", "xt", "xhi", "xlo", "lg", "lgs", "lgt", "gth", "gates", "gt", "gts", "acc_s", "ot", "out",
                 "stats", "moments", "veps", "rstd", "score"):
        per[name] = 1
    if softmax:
        per["gap"] = 1
    for name, k in per.items():
        c[name].base += k * NBLK
    c["down"].base += U * NBLK
    c["zero"].base += 1


def rwkv_phase(nc, counts, spare, sb, ps, x, xt, consts, w, v):
    LOW = -1e38
    NS = BLK // SEQ
    T1 = SEQ + 1
    c = counts
    credit = {"r_out": 1}
    for name, k in credit.items():
        c[name].base += k
    with ExitStack() as ctx:
        def tiles(name, shape, dt=F32):
            return [ctx.enter_context(sb(f"rw_{name}{h}", shape, dt)) for h in range(2)]

        stats = tiles("stats", [P, BT, 6])
        mom = tiles("mom", [P, BT, 2])
        rs = tiles("rs", [P, 7, BT])
        ytok = tiles("ytok", [P, BT, P])
        ztok = tiles("ztok", [P, BT, P])
        y0 = tiles("y0", [P, NS, T1])
        zf = tiles("zf", [P, BLK])
        xpk, xpv, xpr = tiles("xpk", [P, BLK]), tiles("xpv", [P, BLK]), tiles("xpr", [P, BLK])
        key, val = tiles("key", [P, NS, SEQ]), tiles("val", [P, NS, SEQ])
        rg = tiles("rg", [P, NS, SEQ])
        mx, bb, aa, x2 = (tiles(n, [P, NS, T1]) for n in ("mx", "bb", "aa", "x2"))
        t1, t2, t3, t4 = (tiles(n, [P, NS, SEQ]) for n in ("t1", "t2", "t3", "t4"))
        sq = tiles("sq", [P, BLK])
        shi, slo = tiles("shi", [P, 2, BLK], F32R), tiles("slo", [P, 2, BLK], F32R)
        b1 = ctx.enter_context(ps("rw_b1", [P, BLK], F32))
        b2 = ctx.enter_context(ps("rw_b2", [P, BLK], F32))
        ba, bv, bc = ([ctx.enter_context(ps(f"rw_{n}{h}", [P, BLK], F32)) for h in range(2)] for n in ("ba", "bv", "bc"))
        block = ctx.enter_context(nc.Block())
        ident = consts["ident"]

        def seqs(bank):
            return bank[:].rearrange("p (b t) -> p b t", b=NS)

        def tok(bank):
            return bank[:].rearrange("p (j c) -> p j c", j=BT)

        def mid(buf):
            return buf[:, :, 1:T1]

        def prev(buf):
            return buf[:, :, 0:SEQ]

        def blk(t, m):
            return t[:, bass.ts(m, BLK)]

        def w_row():
            return v["w"].broadcast_to([P, SEQ])

        @block.tensor
        def _(pe):
            def turn_ln(h, m):
                pe.wait_ge(c["r_tok"].sem, c["r_tok"].at(m + 1))
                if h == 0:
                    pe.wait_ge(c["r_out"].sem, c["r_out"].at(m))
                else:
                    pe.wait_ge(c["r_zf"].sem, c["r_zf"].at(m))
                for src, bank in ((ytok, b1), (ztok, b2)):
                    for j in range(BT):
                        last = pe.transpose(bank[:, bass.ts(j, P)], src[h][:, j], ident[:])
                last.then_inc(c["r_tt"].sem, 1)

            def kvr(h, m):
                pe.wait_ge(c["r_zl"].sem, c["r_zl"].at(m + 1))
                for q, bank in enumerate((ba[h], bv[h], bc[h])):
                    three_pass(pe, bank[:], [t[:, q] for t in w["tm"]], [blk(xt[0], m), blk(xt[1], m)],
                               True, True).then_inc(c["r_kvr"].sem, 1)

            def turn_x2(h, m):
                pe.wait_ge(c["r_x2"].sem, c["r_x2"].at(m + 1))
                if h == 0:
                    pe.wait_ge(c["r_zf"].sem, c["r_zf"].at(m + 2))
                else:
                    pe.wait_ge(c["r_tok2"].sem, c["r_tok2"].at(m))
                for j in range(BT):
                    b, s = j // 2, j % 2
                    last = pe.transpose(b1[:, bass.ts(j, P)], x2[h][:, b, 1 + s * P:1 + (s + 1) * P], ident[:])
                last.then_inc(c["r_t2"].sem, 1)

            def turn_ln2(h, m):
                pe.wait_ge(c["r_tok2"].sem, c["r_tok2"].at(m + 1))
                if h == 1:
                    pe.wait_ge(c["r_zf2"].sem, c["r_zf2"].at(m))
                for j in range(BT):
                    last = pe.transpose(b2[:, bass.ts(j, P)], ztok[h][:, j], ident[:])
                last.then_inc(c["r_t3"].sem, 1)

            def channel(h, m):
                pe.wait_ge(c["r_zl2"].sem, c["r_zl2"].at(m + 1))
                xs = [blk(xt[0], m), blk(xt[1], m)]

                def grow(j):
                    if j >= 2:
                        pe.wait_ge(c["r_kx"].sem, c["r_kx"].at(4 * m + j - 1))
                    three_pass(pe, (ba[h], bv[h])[j % 2][:], [t[:, j] for t in w["cm"]], xs, True, True).then_inc(c["r_kk"].sem, 1)

                def shrink(j):
                    pe.wait_ge(c["r_sl"].sem, c["r_sl"].at(4 * m + j + 1))
                    three_pass(pe, bc[h][:], [t[:, j] for t in w["cp"]], [shi[h][:, j % 2], slo[h][:, j % 2]],
                               j == 0, j == 3).then_inc(c["r_vv"].sem, 1)

                grow(0)
                grow(1)
                for j in range(4):
                    if j + 2 < 4:
                        grow(j + 2)
                    shrink(j)

            def turn_out(h, m):
                pe.wait_ge(c["r_o"].sem, c["r_o"].at(m + 1))
                if h == 0:
                    pe.wait_ge(c["r_tok2"].sem, c["r_tok2"].at(m + 2))
                else:
                    pe.wait_ge(c["r_out"].sem, c["r_out"].at(m))
                for j in range(BT):
                    b, s = j // 2, j % 2
                    last = pe.transpose(b1[:, bass.ts(j, P)], t4[h][:, b, s * P:(s + 1) * P], ident[:])
                last.then_inc(c["r_ot"].sem, 1)

            for name, k in credit.items():
                pe.sem_inc(c[name].sem, k)
            with pe.Fori(0, NBLK // 2) as i:
                for h in range(2):
                    turn_ln(h, i * 2 + h)
                for h in range(2):
                    kvr(h, i * 2 + h)
                for h in range(2):
                    turn_x2(h, i * 2 + h)
                for h in range(2):
                    turn_ln2(h, i * 2 + h)
                for h in range(2):
                    channel(h, i * 2 + h)
                for h in range(2):
                    turn_out(h, i * 2 + h)

        @block.scalar
        def _(act):
            A = nc.scalar.activation

            def take_ln(h, m):
                act.wait_ge(c["r_tt"].sem, c["r_tt"].at(m + 1))
                nc.scalar.copy(mid(y0[h]), seqs(b1))
                nc.scalar.copy(y0[h][:, :, 0:1], seqs(b1)[:, :, 0:1]).then_inc(c["r_y0"].sem, 1)
                A(zf[h][:], b2[:], ACT.Identity, bias=v["b1"], scale=v["g1"]).then_inc(c["r_zf"].sem, 1)
                act.wait_ge(c["r_zf"].sem, c["r_zf"].at(m + 1))
                act.sem_inc(spare["act"], 1)
                nc.scalar.copy(blk(xt[0], m), zf[h][:]).then_inc(c["r_zh"].sem, 1)

            def mixes(h, m):
                act.wait_ge(c["r_y0"].sem, c["r_y0"].at(m + 1))
                for q, dst in enumerate((xpk, xpv, xpr)):
                    last = A(dst[h][:].rearrange("p (b t) -> p b t", b=NS), prev(y0[h]), ACT.Copy, scale=v["om" + "kvr"[q]])
                last.then_inc(c["r_xp"].sem, 1)

            def decays(h, m):
                act.wait_ge(c["r_dm"].sem, c["r_dm"].at(m + 1))
                A(t1[h][:], t1[h][:], ACT.Exp, bias=v["w"])
                act.wait_ge(c["r_dk"].sem, c["r_dk"].at(m + 1))
                A(t2[h][:], t2[h][:], ACT.Exp).then_inc(c["r_d"].sem, 1)

            def logs(h, m):
                act.wait_ge(c["r_B"].sem, c["r_B"].at(m + 1))
                A(t3[h][:], t3[h][:], ACT.Ln).then_inc(c["r_ln"].sem, 1)

            def factors(h, m):
                act.wait_ge(c["r_a1"].sem, c["r_a1"].at(m + 1))
                A(t1[h][:], t1[h][:], ACT.Exp, bias=v["w"])
                act.wait_ge(c["r_a2"].sem, c["r_a2"].at(m + 1))
                A(t2[h][:], t2[h][:], ACT.Exp).then_inc(c["r_e"].sem, 1)

            def weights(h, m):
                act.wait_ge(c["r_r"].sem, c["r_r"].at(m + 1))
                A(rg[h][:], rg[h][:], ACT.Tanh, scale=0.5).then_inc(c["r_tr"].sem, 1)
                act.wait_ge(c["r_du"].sem, c["r_du"].at(m + 1))
                A(t3[h][:], t3[h][:], ACT.Tanh, bias=v["nuh"], scale=0.5).then_inc(c["r_th"].sem, 1)

            def take_ln2(h, m):
                act.wait_ge(c["r_t3"].sem, c["r_t3"].at(m + 1))
                A(zf[h][:], b2[:], ACT.Identity, bias=v["b2"], scale=v["g2"]).then_inc(c["r_zf2"].sem, 1)
                act.wait_ge(c["r_zf2"].sem, c["r_zf2"].at(m + 1))
                act.sem_inc(spare["act"], 1)
                nc.scalar.copy(blk(xt[0], m), zf[h][:]).then_inc(c["r_zh2"].sem, 1)

            def mixes2(h, m):
                act.wait_ge(c["r_x2w"].sem, c["r_x2w"].at(m + 1))
                A(xpk[h][:].rearrange("p (b t) -> p b t", b=NS), prev(x2[h]), ACT.Copy, scale=v["omck"])
                A(xpr[h][:].rearrange("p (b t) -> p b t", b=NS), prev(x2[h]), ACT.Copy, scale=v["omcr"]).then_inc(c["r_xp2"].sem, 1)

            def gate(h, m):
                act.wait_ge(c["r_rr"].sem, c["r_rr"].at(m + 1))
                A(rg[h][:].rearrange("p b t -> p (b t)"), xpr[h][:], ACT.Tanh, scale=0.5).then_inc(c["r_tr2"].sem, 1)

            def square_hi(h, m):
                for j in range(4):
                    act.wait_ge(c["r_sq"].sem, c["r_sq"].at(4 * m + j + 1))
                    if j >= 2:
                        act.wait_ge(c["r_vv"].sem, c["r_vv"].at(4 * m + j - 1))
                    nc.scalar.copy(shi[h][:, j % 2], sq[h][:]).then_inc(c["r_sh"].sem, 1)

            with act.Fori(0, NBLK // 2) as i:
                for h in range(2):
                    take_ln(h, i * 2 + h)
                for h in range(2):
                    mixes(h, i * 2 + h)
                for h in range(2):
                    decays(h, i * 2 + h)
                for h in range(2):
                    logs(h, i * 2 + h)
                for h in range(2):
                    factors(h, i * 2 + h)
                for h in range(2):
                    weights(h, i * 2 + h)
                for h in range(2):
                    mixes2(h, i * 2 + h)
                for h in range(2):
                    take_ln2(h, i * 2 + h)
                for h in range(2):
                    gate(h, i * 2 + h)
                for h in range(2):
                    square_hi(h, i * 2 + h)

        @block.vector
        def _(dve):
            V = nc.vector

            def ln_stats(h, m):
                for j in range(BT):
                    last = V.bn_stats(stats[h][:, j], x[:, m * BT + j])
                last.then_inc(c["r_st"].sem, 1)
                dve.wait_ge(c["r_st"].sem, c["r_st"].at(m + 1))
                dve.sem_inc(spare["dve"], 1)
                for j in range(BT):
                    last = V.bn_aggr(mom[h][:, j], stats[h][:, j])
                last.then_inc(c["r_mom"].sem, 1)

            def ln_apply(h, m):
                dve.wait_ge(c["r_rs"].sem, c["r_rs"].at(m + 1))
                for j in range(BT):
                    V.tensor_scalar(ytok[h][:, j], x[:, m * BT + j], mom[h][:, j, 0:1], rs[h][:, 1, j:j + 1],
                                    ALU.subtract, ALU.mult)
                    last = V.tensor_scalar(ztok[h][:, j], x[:, m * BT + j], mom[h][:, j, 0:1], rs[h][:, 6, j:j + 1],
                                           ALU.subtract, ALU.mult)
                last.then_inc(c["r_tok"].sem, 1)

            def low(h, m):
                dve.wait_ge(c["r_zh"].sem, c["r_zh"].at(m + 1))
                V.tensor_tensor(blk(xt[1], m), zf[h][:], blk(xt[0], m).bitcast(F32), ALU.subtract).then_inc(c["r_zl"].sem, 1)

            def mix(h, m):
                for q, (bank, xp, dst, name) in enumerate(((ba, xpk, key, "k"), (bv, xpv, val, "v"), (bc, xpr, rg, "r"))):
                    dve.wait_ge(c["r_kvr"].sem, c["r_kvr"].at(3 * m + q + 1))
                    dve.wait_ge(c["r_xp"].sem, c["r_xp"].at(m + 1))
                    V.scalar_tensor_tensor(out=dst[h][:], in0=seqs(bank[h]), scalar=v["tm" + name],
                                           in1=xp[h][:].rearrange("p (b t) -> p b t", b=NS),
                                           op0=ALU.mult, op1=ALU.add).then_inc(c["r_" + name].sem, 1)

            def running_max(h, m):
                dve.wait_ge(c["r_k"].sem, c["r_k"].at(m + 1))
                for b in range(NS):
                    last = V.tensor_tensor_scan(mx[h][:, b, 1:T1], w_row(), key[h][:, b], LOW, ALU.add, ALU.max)
                last.then_inc(c["r_M"].sem, 1)

            def max_step(h, m):
                dve.wait_ge(c["r_M"].sem, c["r_M"].at(m + 1))
                V.tensor_tensor(t1[h][:], prev(mx[h]), mid(mx[h]), ALU.subtract).then_inc(c["r_dm"].sem, 1)

            def sums(h, m):
                dve.wait_ge(c["r_d"].sem, c["r_d"].at(m + 1))
                for b in range(NS):
                    last = V.tensor_tensor_scan(t3[h][:, b], t1[h][:, b], t2[h][:, b], 0.0, ALU.mult, ALU.add)
                last.then_inc(c["r_B"].sem, 1)

            def log_state(h, m):
                dve.wait_ge(c["r_ln"].sem, c["r_ln"].at(m + 1))
                V.tensor_tensor(mid(bb[h]), mid(mx[h]), t3[h][:], ALU.add).then_inc(c["r_bb"].sem, 1)

            def peaks(h, m):
                dve.wait_ge(c["r_bb"].sem, c["r_bb"].at(m + 1))
                V.scalar_tensor_tensor(out=t4[h][:], in0=prev(bb[h]), scalar=v["w"], in1=key[h][:],
                                       op0=ALU.add, op1=ALU.max).then_inc(c["r_pm"].sem, 1)

            def peak_gap(h, m):
                dve.wait_ge(c["r_pm"].sem, c["r_pm"].at(m + 1))
                V.tensor_tensor(t1[h][:], prev(bb[h]), t4[h][:], ALU.subtract).then_inc(c["r_a1"].sem, 1)

            def numerator(h, m):
                dve.wait_ge(c["r_e"].sem, c["r_e"].at(m + 1))
                dve.wait_ge(c["r_v"].sem, c["r_v"].at(m + 1))
                V.tensor_tensor(t2[h][:], t2[h][:], val[h][:], ALU.mult).then_inc(c["r_ev"].sem, 1)

            def numerator_scan(h, m):
                dve.wait_ge(c["r_ev"].sem, c["r_ev"].at(m + 1))
                for b in range(NS):
                    last = V.tensor_tensor_scan(aa[h][:, b, 1:T1], t1[h][:, b], t2[h][:, b], 0.0, ALU.mult, ALU.add)
                last.then_inc(c["r_aa"].sem, 1)

            def diff(h, m):
                dve.wait_ge(c["r_aa"].sem, c["r_aa"].at(m + 1))
                V.tensor_tensor(t1[h][:], prev(aa[h]), val[h][:], ALU.subtract).then_inc(c["r_q"].sem, 1)

            def blend1(h, m):
                dve.wait_ge(c["r_q"].sem, c["r_q"].at(m + 1))
                dve.wait_ge(c["r_th"].sem, c["r_th"].at(m + 1))
                V.scalar_tensor_tensor(out=t1[h][:], in0=t3[h][:], scalar=1.0, in1=t1[h][:],
                                       op0=ALU.add, op1=ALU.mult).then_inc(c["r_q2"].sem, 1)

            def blend2(h, m):
                dve.wait_ge(c["r_q2"].sem, c["r_q2"].at(m + 1))
                V.scalar_tensor_tensor(out=t2[h][:], in0=t1[h][:], scalar=0.5, in1=val[h][:],
                                       op0=ALU.mult, op1=ALU.add).then_inc(c["r_y"].sem, 1)

            def receptance(h, m):
                dve.wait_ge(c["r_y"].sem, c["r_y"].at(m + 1))
                dve.wait_ge(c["r_tr"].sem, c["r_tr"].at(m + 1))
                V.scalar_tensor_tensor(out=t1[h][:], in0=rg[h][:], scalar=1.0, in1=t2[h][:],
                                       op0=ALU.add, op1=ALU.mult).then_inc(c["r_ry"].sem, 1)

            def add_x(h, m):
                dve.wait_ge(c["r_ry"].sem, c["r_ry"].at(m + 1))
                V.scalar_tensor_tensor(out=mid(x2[h]), in0=t1[h][:], scalar=0.5, in1=mid(y0[h]),
                                       op0=ALU.mult, op1=ALU.add).then_inc(c["r_x2"].sem, 1)

            def wrap_x(h, m):
                dve.wait_ge(c["r_x2"].sem, c["r_x2"].at(m + 1))
                V.tensor_copy(x2[h][:, :, 0:1], x2[h][:, :, SEQ:T1]).then_inc(c["r_x2w"].sem, 1)

            def ln2_stats(h, m):
                dve.wait_ge(c["r_t2"].sem, c["r_t2"].at(m + 1))
                for j in range(BT):
                    last = V.bn_stats(stats[h][:, j], b1[:, bass.ts(j, P)])
                last.then_inc(c["r_st2"].sem, 1)
                dve.wait_ge(c["r_st2"].sem, c["r_st2"].at(m + 1))
                dve.sem_inc(spare["dve"], 1)
                for j in range(BT):
                    last = V.bn_aggr(mom[h][:, j], stats[h][:, j])
                last.then_inc(c["r_mom2"].sem, 1)
                dve.wait_ge(c["r_rs2"].sem, c["r_rs2"].at(m + 1))
                for j in range(BT):
                    last = V.tensor_scalar(ztok[h][:, j], b1[:, bass.ts(j, P)], mom[h][:, j, 0:1], rs[h][:, 1, j:j + 1],
                                           ALU.subtract, ALU.mult)
                last.then_inc(c["r_tok2"].sem, 1)

            def low2(h, m):
                dve.wait_ge(c["r_zh2"].sem, c["r_zh2"].at(m + 1))
                V.tensor_tensor(blk(xt[1], m), zf[h][:], blk(xt[0], m).bitcast(F32), ALU.subtract).then_inc(c["r_zl2"].sem, 1)
                dve.wait_ge(c["r_xp2"].sem, c["r_xp2"].at(m + 1))
                V.scalar_tensor_tensor(out=xpr[h][:], in0=zf[h][:], scalar=v["cmr"], in1=xpr[h][:],
                                       op0=ALU.mult, op1=ALU.add).then_inc(c["r_rr"].sem, 1)

            def channel(h, m):
                for j in range(4):
                    dve.wait_ge(c["r_kk"].sem, c["r_kk"].at(4 * m + j + 1))
                    if j >= 1:
                        dve.wait_ge(c["r_sl"].sem, c["r_sl"].at(4 * m + j))
                    V.scalar_tensor_tensor(out=xpv[h][:], in0=(ba[h], bv[h])[j % 2][:], scalar=v["cmk"], in1=xpk[h][:],
                                           op0=ALU.mult, op1=ALU.add).then_inc(c["r_kx"].sem, 1)
                    dve.wait_ge(c["r_kx"].sem, c["r_kx"].at(4 * m + j + 1))
                    V.scalar_tensor_tensor(out=sq[h][:], in0=xpv[h][:], scalar=0.0, in1=xpv[h][:],
                                           op0=ALU.max, op1=ALU.mult).then_inc(c["r_sq"].sem, 1)
                    dve.wait_ge(c["r_sh"].sem, c["r_sh"].at(4 * m + j + 1))
                    V.tensor_tensor(slo[h][:, j % 2], sq[h][:], shi[h][:, j % 2].bitcast(F32),
                                    ALU.subtract).then_inc(c["r_sl"].sem, 1)

            def gated(h, m):
                dve.wait_ge(c["r_vv"].sem, c["r_vv"].at(4 * m + 4))
                dve.wait_ge(c["r_tr2"].sem, c["r_tr2"].at(m + 1))
                V.scalar_tensor_tensor(out=t1[h][:], in0=rg[h][:], scalar=1.0, in1=seqs(bc[h]),
                                       op0=ALU.add, op1=ALU.mult).then_inc(c["r_g"].sem, 1)
                dve.wait_ge(c["r_g"].sem, c["r_g"].at(m + 1))
                V.scalar_tensor_tensor(out=t4[h][:], in0=t1[h][:], scalar=0.5, in1=mid(x2[h]),
                                       op0=ALU.mult, op1=ALU.add).then_inc(c["r_o"].sem, 1)

            def add_out(h, m):
                dve.wait_ge(c["r_ot"].sem, c["r_ot"].at(m + 1))
                xb = x[:, bass.ts(m, BT)]
                V.tensor_tensor(xb, tok(b1), xb, ALU.add).then_inc(c["r_out"].sem, 1)

            for h in range(2):
                V.memset(mx[h][:, :, 0:1], LOW)
                V.memset(bb[h][:, :, 0:1], LOW)
                last = V.memset(aa[h][:, :, 0:1], 0.0)
            last.then_inc(c["r_pad"].sem, 1)
            dve.wait_ge(c["r_pad"].sem, c["r_pad"].at(1))
            with dve.Fori(0, NBLK // 2) as i:
                for h in range(2):
                    ln_stats(h, i * 2 + h)
                for h in range(2):
                    ln_apply(h, i * 2 + h)
                for h in range(2):
                    low(h, i * 2 + h)
                for h in range(2):
                    mix(h, i * 2 + h)
                for h in range(2):
                    running_max(h, i * 2 + h)
                for h in range(2):
                    max_step(h, i * 2 + h)
                for h in range(2):
                    sums(h, i * 2 + h)
                for h in range(2):
                    log_state(h, i * 2 + h)
                for h in range(2):
                    peaks(h, i * 2 + h)
                for h in range(2):
                    peak_gap(h, i * 2 + h)
                for h in range(2):
                    numerator(h, i * 2 + h)
                for h in range(2):
                    numerator_scan(h, i * 2 + h)
                for h in range(2):
                    diff(h, i * 2 + h)
                for h in range(2):
                    blend1(h, i * 2 + h)
                for h in range(2):
                    blend2(h, i * 2 + h)
                for h in range(2):
                    receptance(h, i * 2 + h)
                for h in range(2):
                    add_x(h, i * 2 + h)
                for h in range(2):
                    wrap_x(h, i * 2 + h)
                for h in range(2):
                    ln2_stats(h, i * 2 + h)
                for h in range(2):
                    low2(h, i * 2 + h)
                for h in range(2):
                    channel(h, i * 2 + h)
                for h in range(2):
                    gated(h, i * 2 + h)
                for h in range(2):
                    add_out(h, i * 2 + h)

        @block.gpsimd
        def _(pool):
            G = nc.gpsimd
            half = consts["minus_half"]

            def ln_scale(h, m):
                r, var = rs[h], mom[h][:, :, 1]
                pool.wait_ge(c["r_mom"].sem, c["r_mom"].at(m + 1))
                pool.sem_inc(spare["pool"], 1)
                G.tensor_scalar(r[:, 0], var, LN_EPS, None, ALU.add).then_inc(c["r_c1"].sem, 1)
                pool.wait_ge(c["r_c1"].sem, c["r_c1"].at(6 * m + 1))
                G.tensor_tensor(r[:, 1], r[:, 0], half[:], ALU.pow).then_inc(c["r_c1"].sem, 1)
                pool.wait_ge(c["r_c1"].sem, c["r_c1"].at(6 * m + 2))
                G.tensor_tensor(r[:, 2], r[:, 1], r[:, 1], ALU.mult).then_inc(c["r_c1"].sem, 1)
                pool.wait_ge(c["r_c1"].sem, c["r_c1"].at(6 * m + 3))
                G.tensor_tensor(r[:, 3], r[:, 2], var, ALU.mult).then_inc(c["r_c1"].sem, 1)
                pool.wait_ge(c["r_c1"].sem, c["r_c1"].at(6 * m + 4))
                pool.sem_inc(spare["pool"], 1)
                G.tensor_scalar(r[:, 4], r[:, 3], LN_EPS, None, ALU.add).then_inc(c["r_c1"].sem, 1)
                pool.wait_ge(c["r_c1"].sem, c["r_c1"].at(6 * m + 5))
                G.tensor_tensor(r[:, 5], r[:, 4], half[:], ALU.pow).then_inc(c["r_c1"].sem, 1)
                pool.wait_ge(c["r_c1"].sem, c["r_c1"].at(6 * m + 6))
                G.tensor_tensor(r[:, 6], r[:, 5], r[:, 1], ALU.mult).then_inc(c["r_rs"].sem, 1)

            def below_max(h, m):
                pool.wait_ge(c["r_M"].sem, c["r_M"].at(m + 1))
                G.tensor_tensor(t2[h][:], key[h][:], mid(mx[h]), ALU.subtract).then_inc(c["r_dk"].sem, 1)

            def below_peak(h, m):
                pool.wait_ge(c["r_pm"].sem, c["r_pm"].at(m + 1))
                G.tensor_tensor(t2[h][:], key[h][:], t4[h][:], ALU.subtract).then_inc(c["r_a2"].sem, 1)

            def bonus(h, m):
                pool.wait_ge(c["r_bb"].sem, c["r_bb"].at(m + 1))
                G.tensor_tensor(t3[h][:], prev(bb[h]), key[h][:], ALU.subtract).then_inc(c["r_du"].sem, 1)

            def ln2_scale(h, m):
                r = rs[h]
                pool.wait_ge(c["r_mom2"].sem, c["r_mom2"].at(m + 1))
                pool.sem_inc(spare["pool"], 1)
                G.tensor_scalar(r[:, 0], mom[h][:, :, 1], LN_EPS, None, ALU.add).then_inc(c["r_c2"].sem, 1)
                pool.wait_ge(c["r_c2"].sem, c["r_c2"].at(m + 1))
                G.tensor_tensor(r[:, 1], r[:, 0], half[:], ALU.pow).then_inc(c["r_rs2"].sem, 1)

            with pool.Fori(0, NBLK // 2) as i:
                for h in range(2):
                    ln_scale(h, i * 2 + h)
                for h in range(2):
                    below_max(h, i * 2 + h)
                for h in range(2):
                    below_peak(h, i * 2 + h)
                for h in range(2):
                    bonus(h, i * 2 + h)
                for h in range(2):
                    ln2_scale(h, i * 2 + h)

    per = {"r_kvr": 3, "r_kk": 4, "r_vv": 4, "r_kx": 4, "r_sq": 4, "r_sh": 4, "r_sl": 4, "r_c1": 6}
    for name in RWKV_SEMS:
        if name != "r_pad":
            c[name].base += per.get(name, 1) * NBLK


RWKV_SEMS = ("r_st r_mom r_rs r_tok r_tt r_y0 r_zf r_zh r_zl r_xp r_kvr r_k r_v r_r r_M r_dm r_dk r_d r_B r_ln r_bb r_pm "
             "r_a1 r_a2 r_e r_ev r_aa r_du r_tr r_th r_q r_q2 r_y r_ry r_x2 r_x2w r_t2 r_st2 r_mom2 r_rs2 r_tok2 r_t3 "
             "r_zf2 r_zh2 r_zl2 r_xp2 r_rr r_tr2 r_kk r_kx r_sq r_sh r_sl r_vv r_g r_o r_ot r_out r_c1 r_c2 r_pad").split()


HEADS, STATE, HEAD_DIM = 16, 64, 8

MAMBA_SEMS = ("m_st m_mom m_c m_rs m_tok m_t m_xh m_xl m_pj m_xr m_u m_na m_ex m_ln m_dt m_dA m_dh m_dl m_zs m_sum m_ee "
              "m_bc m_bh m_rh m_rl m_D m_E m_CB m_off m_read m_xp m_xd m_Y m_yc m_sel m_yo m_yb m_yt m_yT m_yh m_yl m_ow "
              "m_out").split()


def mamba_input(nc, counts, spare, sb, ps, x, xt, consts, w, v, keep):
    c = counts
    credit = {"m_xl": 2, "m_xr": 2, "m_zs": 2, "m_u": 2, "m_pj": 2}
    for name, k in credit.items():
        c[name].base += k
    with ExitStack() as ctx:
        def tiles(name, shape, dt=F32):
            return [ctx.enter_context(sb(f"mi_{name}{h}", shape, dt)) for h in range(2)]

        stats, mom = tiles("stats", [P, BT, 6]), tiles("mom", [P, BT, 2])
        rs = tiles("rs", [P, 2, BT])
        xn = tiles("xn", [P, BT, P])
        xs = [tiles("xs" + p, [P, BLK], F32R) for p in ("hi", "lo")]
        ps_t = [ctx.enter_context(ps(f"mi_t{h}", [P, BT, P], F32)) for h in range(2)]
        ps_in = [ctx.enter_context(ps(f"mi_in{h}", [P, BT, 2 * P], F32)) for h in range(2)]
        ps_dt = [ctx.enter_context(ps(f"mi_dt{h}", [P, BT, HEADS], F32)) for h in range(2)]
        block = ctx.enter_context(nc.Block())

        @block.tensor
        def _(pe):
            def turn(h, n):
                pe.wait_ge(c["m_tok"].sem, c["m_tok"].at(n + 1))
                pe.wait_ge(c["m_xl"].sem, c["m_xl"].at(n - 1))
                for t in range(BT):
                    last = pe.transpose(ps_t[h][:, t], xn[h][:, t], consts["ident"][:])
                last.then_inc(c["m_t"].sem, 1)

            def project(h, n):
                pe.wait_ge(c["m_xl"].sem, c["m_xl"].at(n + 1))
                pe.wait_ge(c["m_xr"].sem, c["m_xr"].at(n - 1))
                pe.wait_ge(c["m_zs"].sem, c["m_zs"].at(n - 1))
                pe.wait_ge(c["m_u"].sem, c["m_u"].at(n - 1))
                for t in range(BT):
                    lhs = [q[h][:, bass.ts(t, P)] for q in xs]
                    three_pass(pe, ps_in[h][:, t], lhs, [q[:] for q in w["in"]], True, True)
                for t in range(BT):
                    lhs = [q[h][:, bass.ts(t, P)] for q in xs]
                    last = three_pass(pe, ps_dt[h][:, t], lhs, [q[:] for q in w["dt"]], True, True)
                last.then_inc(c["m_pj"].sem, 1)

            for name, k in credit.items():
                pe.sem_inc(c[name].sem, k)
            with pe.Fori(0, NBLK // 2) as i:
                for h in range(2):
                    turn(h, i * 2 + h)
                for h in range(2):
                    project(h, i * 2 + h)

        @block.scalar
        def _(act):
            def take_x(h, n):
                act.wait_ge(c["m_t"].sem, c["m_t"].at(n + 1))
                act.wait_ge(c["m_pj"].sem, c["m_pj"].at(n - 1))
                nc.scalar.copy(xs[0][h][:], ps_t[h][:].rearrange("p j c -> p (j c)"))
                act.sem_inc(spare["act"], 1)
                nc.scalar.copy(xt[0][:, bass.ts(n, BLK)], ps_t[h][:].rearrange("p j c -> p (j c)")).then_inc(c["m_xh"].sem, 1)

            def take_in(h, n):
                act.wait_ge(c["m_pj"].sem, c["m_pj"].at(n + 1))
                act.sem_inc(spare["act"], 1)
                nc.scalar.copy(keep["xraw"][:, bass.ts(n, BT)], ps_in[h][:, :, 0:P]).then_inc(c["m_xr"].sem, 1)
                nc.scalar.activation(keep["zs"][:, bass.ts(n, BT)], ps_in[h][:, :, P:2 * P], ACT.Silu).then_inc(c["m_zs"].sem, 1)

            with act.Fori(0, NBLK // 2) as i:
                for h in range(2):
                    take_x(h, i * 2 + h)
                for h in range(2):
                    take_in(h, i * 2 + h)

        @block.vector
        def _(dve):
            V = nc.vector

            def norm(h, n):
                for j in range(BT):
                    last = V.bn_stats(stats[h][:, j], x[:, n * BT + j])
                last.then_inc(c["m_st"].sem, 1)
                dve.wait_ge(c["m_st"].sem, c["m_st"].at(n + 1))
                dve.sem_inc(spare["dve"], 1)
                for j in range(BT):
                    last = V.bn_aggr(mom[h][:, j], stats[h][:, j])
                last.then_inc(c["m_mom"].sem, 1)

            def normed(h, n):
                dve.wait_ge(c["m_rs"].sem, c["m_rs"].at(n + 1))
                for j in range(BT):
                    last = V.tensor_scalar(xn[h][:, j], x[:, n * BT + j], mom[h][:, j, 0:1], rs[h][:, 1, j:j + 1],
                                           ALU.subtract, ALU.mult)
                last.then_inc(c["m_tok"].sem, 1)

            def low_x(h, n):
                dve.wait_ge(c["m_xh"].sem, c["m_xh"].at(n + 1))
                for lo in (xt[1][:, bass.ts(n, BLK)], xs[1][h][:]):
                    last = V.tensor_tensor(lo, ps_t[h][:].rearrange("p j c -> p (j c)"), xs[0][h][:].bitcast(F32), ALU.subtract)
                last.then_inc(c["m_xl"].sem, 1)

            def take_dt(h, n):
                dve.wait_ge(c["m_pj"].sem, c["m_pj"].at(n + 1))
                V.tensor_tensor(keep["u"][:, bass.ts(n, BT)], ps_dt[h][:], v["b_dt"][:].unsqueeze(1).broadcast_to([P, BT, HEADS]),
                                ALU.add).then_inc(c["m_u"].sem, 1)

            with dve.Fori(0, NBLK // 2) as i:
                for h in range(2):
                    norm(h, i * 2 + h)
                for h in range(2):
                    normed(h, i * 2 + h)
                for h in range(2):
                    low_x(h, i * 2 + h)
                for h in range(2):
                    take_dt(h, i * 2 + h)

        @block.gpsimd
        def _(pool):
            def scale(h, n):
                pool.wait_ge(c["m_mom"].sem, c["m_mom"].at(n + 1))
                pool.sem_inc(spare["pool"], 1)
                nc.gpsimd.tensor_scalar(rs[h][:, 0], mom[h][:, :, 1], LN_EPS, None, ALU.add).then_inc(c["m_c"].sem, 1)
                pool.wait_ge(c["m_c"].sem, c["m_c"].at(n + 1))
                nc.gpsimd.tensor_tensor(rs[h][:, 1], rs[h][:, 0], consts["minus_half"][:], ALU.pow).then_inc(c["m_rs"].sem, 1)

            with pool.Fori(0, NBLK // 2) as i:
                for h in range(2):
                    scale(h, i * 2 + h)

    for name in ("m_st", "m_mom", "m_c", "m_rs", "m_tok", "m_t", "m_xh", "m_xl", "m_pj", "m_xr", "m_u", "m_zs"):
        c[name].base += NBLK


def mamba_phase(nc, counts, spare, sb, ps, x, xt, consts, w, v, keep):
    c = counts
    credit = {"m_out": 1, "m_E": 2, "m_yc": 1}
    for name, k in credit.items():
        c[name].base += k
    GROUPS = HEADS // 4
    PIECES = (0, 2, 1, 3)
    USES = 3 * GROUPS
    with ExitStack() as ctx:
        def one(name, shape, dt=F32):
            return ctx.enter_context(sb(f"mb_{name}", shape, dt))

        def tiles(name, shape, dt=F32):
            return [one(f"{name}{h}", shape, dt) for h in range(2)]

        u = keep["u"]
        na = one("na", [P, TILES, HEADS])
        dt, dA = u, na
        dAp = [one("dA" + p, [P, TILES, HEADS], F32R) for p in ("hi", "lo")]
        ee = one("ee", [P, 2, BATCH, HEADS])
        xp, xd = tiles("xp", [P, 2, HEADS, 32]), tiles("xd", [P, HEADS, 32])
        yo, ytok = one("yo", [P, P]), one("ytok", [P, 2, P])
        bc = [tiles("bc" + p, [P, 4, 4, SEQ], F32R) for p in ("hi", "lo")]
        yt = one("yt", [P, 3, P])
        yT = [one("yT" + p, [P, SEQ], F32R) for p in ("hi", "lo")]
        rh, rl = tiles("rh", [P, 4, P], F32R), tiles("rl", [P, 4, P], F32R)
        sm = [tiles(f"sm{q}", [P, 4, P]) for q in range(2)]
        off = tiles("off", [P, 4, P])
        ps_d = [ctx.enter_context(ps(f"mb_d{t}", [P, 4, P], F32)) for t in range(2)]
        ps_c = [ctx.enter_context(ps(f"mb_c{t}", [P, 4, SEQ], F32)) for t in range(2)]
        ps_yt = ctx.enter_context(ps("mb_pyt", [P, 4, P], F32))
        ps_y = ctx.enter_context(ps("mb_y", [P, 4, P], F32))
        ps_sum = ps_y[:, 0:2].rearrange("p t (m h) -> p t m h", h=HEADS)
        ps_turn = ps_y[:, 0:2].rearrange("p t c -> p (t c)")
        block = ctx.enter_context(nc.Block())
        ident = consts["ident"]

        def head_of(q, k):
            return 4 * q + 2 * (k % 2) + k // 2

        def by_head(t):
            return t.rearrange("p (r j d) -> p r j d", j=4, d=HEAD_DIM)

        def turned(t):
            return t.rearrange("p (j r d) -> p r j d", j=4, d=HEAD_DIM)

        def spread(t):
            return t.rearrange("p (r j) -> p r j", j=4).unsqueeze(3).broadcast_to([P, GROUPS, 4, HEAD_DIM])

        def columns(t, r):
            return t[:, 4 * r:4 * r + 4, HEAD_DIM * r:HEAD_DIM * r + HEAD_DIM]

        def use(m, q, j, more=True):
            return m * USES + (4 + (3 if more else 2) * q + j)

        def half(q, j, more=True):
            return ps_c[((3 if more else 2) * q + j) % 2]

        @block.tensor
        def _(pe):
            def piece(h, m, k, bank):
                for j in range(4):
                    last = three_pass(pe, bank[:, j], [t[:, PIECES[k], bass.ts(j, P)] for t in w["bc"]],
                                      [q[:, bass.ts(m, SEQ)] for q in xt], True, True)
                last.then_inc(c["m_bc"].sem, 1)

            def decay(h, m, q):
                for t in range(2):
                    g = m * 8 + (2 * q + t)
                    pe.wait_ge(c["m_rl"].sem, c["m_rl"].at(g + 1))
                    pe.wait_ge(c["m_rh"].sem, c["m_rh"].at(g + 1))
                    pe.wait_ge(c["m_E"].sem, c["m_E"].at(g - 1))
                    out = ps_d[t][:].rearrange("p h l -> p (h l)")
                    pe.matmul(out, consts["gt"][:], rh[t][:].rearrange("p h l -> p (h l)"), start=True, stop=False)
                    pe.matmul(out, consts["gt"][:], rl[t][:].rearrange("p h l -> p (h l)"), start=False, stop=False)
                    pe.matmul(out, consts["ident_r"][:], consts["never"][:].unsqueeze(1).broadcast_to([P, 4, P]),
                              start=False, stop=True).then_inc(c["m_D"].sem, 1)

            def products(h, m, q, more):
                for t in range(2):
                    pe.wait_ge(c["m_read"].sem, c["m_read"].at(use(m, q, t, more) - 1))
                    for k in (0, 2, 1, 3):
                        hd = head_of(q, k)
                        rows = slice(STATE * (hd % 2), STATE * (hd % 2) + STATE)
                        r, j = hd // 2 // 4, hd // 2 % 4
                        B = [p[h][rows, r, j, bass.ts(t, P)] for p in bc]
                        C = [p[h][rows, 2 + r, j, t * P:SEQ] for p in bc]
                        last = three_pass(pe, half(q, t, more)[:, k, 0:SEQ - t * P], B, C, True, True)
                    last.then_inc(c["m_CB"].sem, 1)

            def outputs(h, m, q, more=True):
                if q == 0:
                    pe.wait_ge(c["m_xd"].sem, c["m_xd"].at(m + 1))
                    pe.wait_ge(c["m_yc"].sem, c["m_yc"].at(m))
                pe.wait_ge(c["m_read"].sem, c["m_read"].at(use(m, q, 1, more) + 1))
                pe.wait_ge(c["m_off"].sem, c["m_off"].at(m * 4 + (q + 1)))
                for part in range(3):
                    for k in range(4):
                        hd = head_of(q, k)
                        lhs = xd[h][:, hd] if part == 2 else xp[h][:, part, hd]
                        rhs = off[q % 2][:, k] if part == 2 else sm[q % 2][part][:, k]
                        rows = slice(32 * (hd % 4), 32 * (hd % 4) + 32)
                        last = pe.matmul(ps_yt[rows, part], lhs, rhs, start=q == 0 and part == 0,
                                         stop=q == GROUPS - 1 and part == 2)
                last.then_inc(c["m_Y"].sem, 1)

            def to_tokens(h, m):
                pe.wait_ge(c["m_yc"].sem, c["m_yc"].at(m + 1))
                pe.wait_ge(c["m_out"].sem, c["m_out"].at(m))
                pe.wait_ge(c["m_ee"].sem, c["m_ee"].at(1))
                for part in range(3):
                    last = pe.transpose(ps_y[:, part], yt[:, part], ident[:])
                last.then_inc(c["m_sel"].sem, 1)

            def turn_y(h, m):
                pe.wait_ge(c["m_yt"].sem, c["m_yt"].at(m + 1))
                for t in range(2):
                    last = pe.transpose(ps_y[:, t], ytok[:, t], ident[:])
                last.then_inc(c["m_yT"].sem, 1)

            def project_out(h, m):
                pe.wait_ge(c["m_yl"].sem, c["m_yl"].at(m + 1))
                for t in range(2):
                    last = three_pass(pe, ps_y[:, 2 + t], [q[:, bass.ts(t, P)] for q in yT], [q[:] for q in w["out"]],
                                      True, True)
                last.then_inc(c["m_ow"].sem, 1)

            def section(h, m, first=False, more=True):
                for q in range(GROUPS):
                    decay(h, m, q)
                    products(h, m, q, more)
                    if q == 1 and not first:
                        to_tokens(1 - h, m - 1)
                    if q:
                        outputs(h, m, q - 1, more)
                    elif not first:
                        outputs(1 - h, m - 1, GROUPS - 1)
                    if q == 3 and not first:
                        turn_y(1 - h, m - 1)
                    if more:
                        pe.wait_ge(c["m_read"].sem, c["m_read"].at(use(m, q, 2) - 1))
                        piece(1 - h, m + 1, q, half(q, 2))
                if not first:
                    project_out(1 - h, m - 1)

            for name, k in credit.items():
                pe.sem_inc(c[name].sem, k)
            for k in range(4):
                if k >= 2:
                    pe.wait_ge(c["m_read"].sem, c["m_read"].at(k - 1))
                piece(0, 0, k, ps_c[k % 2])
            pe.wait_ge(c["m_dl"].sem, c["m_dl"].at(1))
            for t, tri in ((0, "gt"), (1, "le")):
                for k in range(2):
                    part = dAp[k][:].rearrange("p (m t) h -> p t m h", t=2)[:, t]
                    last = pe.matmul(ps_sum[:, t], consts[tri][:], part, start=k == 0, stop=k == 1)
            last.then_inc(c["m_sum"].sem, 1)
            section(0, 0, first=True)
            with pe.Fori(0, BATCH // 2 - 1) as i:
                section(1, i * 2 + 1)
                section(0, i * 2 + 2)
            section(1, BATCH - 1, more=False)
            outputs(1, BATCH - 1, GROUPS - 1, more=False)
            to_tokens(1, BATCH - 1)
            turn_y(1, BATCH - 1)
            project_out(1, BATCH - 1)

        @block.scalar
        def _(act):
            A = nc.scalar.activation

            def take_bc(h, m, k, bank):
                act.wait_ge(c["m_bc"].sem, c["m_bc"].at(m * 4 + (k + 1)))
                nc.scalar.copy(bc[0][h][:, PIECES[k]], bank[:]).then_inc(c["m_bh"].sem, 1)

            def take_yt(h, m):
                act.wait_ge(c["m_Y"].sem, c["m_Y"].at(m * 4 + 4))
                nc.scalar.copy(yt[:], ps_yt[:, 0:3]).then_inc(c["m_yc"].sem, 1)

            def take_y(h, m):
                act.wait_ge(c["m_yT"].sem, c["m_yT"].at(m + 1))
                nc.scalar.copy(yT[0][:], ps_turn).then_inc(c["m_yh"].sem, 1)

            def section(h, m, first=False, more=True):
                for q in range(GROUPS):
                    for t in range(2):
                        g = m * 8 + (2 * q + t)
                        act.wait_ge(c["m_D"].sem, c["m_D"].at(g + 1))
                        if q >= 2 or not first:
                            act.wait_ge(c["m_Y"].sem, c["m_Y"].at(m * 4 + (q - 1)))
                        A(sm[q % 2][t][:], ps_d[t][:], ACT.Exp).then_inc(c["m_E"].sem, 1)
                        if t == 0:
                            act.wait_ge(c["m_CB"].sem, c["m_CB"].at(g + 1))
                            nc.scalar.copy(off[q % 2][:], half(q, 0, more)[:, :, P:SEQ]).then_inc(c["m_off"].sem, 1)
                    if q == 0 and not first:
                        take_yt(1 - h, m - 1)
                    if q == 3 and not first:
                        take_y(1 - h, m - 1)
                    if more:
                        take_bc(1 - h, m + 1, q, half(q, 2))

            act.wait_ge(c["m_na"].sem, c["m_na"].at(1))
            A(na[:], na[:], ACT.Exp).then_inc(c["m_ex"].sem, 1)
            act.wait_ge(c["m_ex"].sem, c["m_ex"].at(1))
            A(na[:], na[:], ACT.Ln, bias=1.0).then_inc(c["m_ln"].sem, 1)
            for k in range(4):
                take_bc(0, 0, k, ps_c[k % 2])
            act.wait_ge(c["m_sum"].sem, c["m_sum"].at(1))
            A(ee[:], ps_sum, ACT.Exp).then_inc(c["m_ee"].sem, 1)
            section(0, 0, first=True)
            with act.Fori(0, BATCH // 2 - 1) as i:
                section(1, i * 2 + 1)
                section(0, i * 2 + 2)
            section(1, BATCH - 1, more=False)
            take_yt(1, BATCH - 1)
            take_y(1, BATCH - 1)

        @block.vector
        def _(dve):
            V = nc.vector

            def low_bc(h, m, k, bank):
                dve.wait_ge(c["m_bh"].sem, c["m_bh"].at(m * 4 + (k + 1)))
                V.tensor_tensor(bc[1][h][:, PIECES[k]], bank[:], bc[0][h][:, PIECES[k]].bitcast(F32),
                                ALU.subtract).then_inc(c["m_read"].sem, 1)

            def right(m, q, t, first=False):
                g = m * 8 + (2 * q + t)
                if not first:
                    dve.wait_ge(c["m_D"].sem, c["m_D"].at(g - 1))
                for k in range(4):
                    hd = head_of(q, k)
                    last = V.tensor_scalar(rh[t][:, k], consts["le_f"][:], dAp[0][:, m * 2 + t, hd:hd + 1].bitcast(F32),
                                           None, ALU.mult)
                last.then_inc(c["m_rh"].sem, 1)

            def decayed(m, q, t, more):
                g = m * 8 + (2 * q + t)
                dve.wait_ge(c["m_E"].sem, c["m_E"].at(g + 1))
                dve.wait_ge(c["m_CB"].sem, c["m_CB"].at(g + 1))
                if t == 0:
                    dve.wait_ge(c["m_off"].sem, c["m_off"].at(m * 4 + (q + 1)))
                V.tensor_tensor(sm[q % 2][t][:], sm[q % 2][t][:], half(q, t, more)[:, :, 0:P], ALU.mult).then_inc(c["m_read"].sem, 1)

            def gated(h, m):
                dve.wait_ge(c["m_sel"].sem, c["m_sel"].at(m + 1))
                zs = keep["zs"]
                V.tensor_tensor(by_head(yo[:]), turned(ps_y[:, 2]), spread(ee[:, 1, m]), ALU.mult).then_inc(c["m_yo"].sem, 1)
                V.tensor_tensor(by_head(ytok[:, 0]), turned(ps_y[:, 0]), by_head(zs[:, m * 2]), ALU.mult)
                dve.wait_ge(c["m_yo"].sem, c["m_yo"].at(m + 1))
                V.tensor_tensor(by_head(yo[:]), turned(ps_y[:, 1]), by_head(yo[:]), ALU.add).then_inc(c["m_yb"].sem, 1)
                dve.wait_ge(c["m_yb"].sem, c["m_yb"].at(m + 1))
                V.tensor_tensor(ytok[:, 1], yo[:], zs[:, m * 2 + 1], ALU.mult).then_inc(c["m_yt"].sem, 1)

            def low_y(h, m):
                dve.wait_ge(c["m_yh"].sem, c["m_yh"].at(m + 1))
                V.tensor_tensor(yT[1][:], ps_turn, yT[0][:].bitcast(F32), ALU.subtract).then_inc(c["m_yl"].sem, 1)

            def add_out(h, m):
                dve.wait_ge(c["m_ow"].sem, c["m_ow"].at(m + 1))
                xb = x[:, bass.ts(m, 2)]
                V.tensor_tensor(xb, ps_y[:, 2:4], xb, ALU.add).then_inc(c["m_out"].sem, 1)

            def section(h, m, first=False, more=True):
                for q in range(GROUPS):
                    for t in range(2):
                        if q + 1 < GROUPS:
                            right(m, q + 1, t)
                        elif more:
                            right(m + 1, 0, t)
                        decayed(m, q, t, more)
                    if q == 2 and not first:
                        gated(1 - h, m - 1)
                    if q == 3 and not first:
                        low_y(1 - h, m - 1)
                    if more:
                        low_bc(1 - h, m + 1, q, half(q, 2))
                if not first:
                    add_out(1 - h, m - 1)

            V.scalar_tensor_tensor(out=na[:], in0=u[:], scalar=-1.0, in1=u[:], op0=ALU.mult, op1=ALU.min).then_inc(c["m_na"].sem, 1)
            dve.wait_ge(c["m_ln"].sem, c["m_ln"].at(1))
            V.scalar_tensor_tensor(out=dt[:], in0=u[:], scalar=0.0, in1=na[:], op0=ALU.max, op1=ALU.add).then_inc(c["m_dt"].sem, 1)
            dve.wait_ge(c["m_dt"].sem, c["m_dt"].at(1))
            V.tensor_tensor(dA[:], dt[:], v["neg_a"][:].unsqueeze(1).broadcast_to([P, TILES, HEADS]), ALU.mult).then_inc(c["m_dA"].sem, 1)
            dve.wait_ge(c["m_dA"].sem, c["m_dA"].at(1))
            V.tensor_copy(dAp[0][:], dA[:]).then_inc(c["m_dh"].sem, 1)
            dve.wait_ge(c["m_dh"].sem, c["m_dh"].at(1))
            V.tensor_tensor(dAp[1][:], dA[:], dAp[0][:].bitcast(F32), ALU.subtract).then_inc(c["m_dl"].sem, 1)
            for k in range(4):
                if k < 2:
                    right(0, 0, k, first=True)
                low_bc(0, 0, k, ps_c[k % 2])
            section(0, 0, first=True)
            with dve.Fori(0, BATCH // 2 - 1) as i:
                section(1, i * 2 + 1)
                section(0, i * 2 + 2)
            section(1, BATCH - 1, more=False)
            gated(1, BATCH - 1)
            low_y(1, BATCH - 1)
            add_out(1, BATCH - 1)

        @block.gpsimd
        def _(pool):
            G = nc.gpsimd

            def inputs(h, m, used):
                if used:
                    pool.wait_ge(c["m_Y"].sem, c["m_Y"].at(m * 4 - 4))
                for t in range(2):
                    xin = keep["xraw"][:, m * 2 + t].rearrange("p (h d) -> p h d", d=HEAD_DIM)
                    for r in range(GROUPS):
                        s = slice(4 * r, 4 * r + 4)
                        last = G.tensor_tensor(columns(xp[h][:, t], r), xin[:, s],
                                               dt[:, m * 2 + t, s].unsqueeze(2).broadcast_to([P, 4, HEAD_DIM]), ALU.mult)
                last.then_inc(c["m_xp"].sem, 1)
                pool.wait_ge(c["m_xp"].sem, c["m_xp"].at(m + 1))
                for r in range(GROUPS):
                    last = G.tensor_tensor(columns(xd[h], r), columns(xp[h][:, 0], r),
                                           ee[:, 0, m, 4 * r:4 * r + 4].unsqueeze(2).broadcast_to([P, 4, HEAD_DIM]), ALU.mult)
                last.then_inc(c["m_xd"].sem, 1)

            def section(h, m, first=False, more=True):
                for q in range(GROUPS):
                    for t in range(2):
                        if q or not first:
                            pool.wait_ge(c["m_D"].sem, c["m_D"].at(m * 8 + (2 * q + t - 1)))
                        part = dAp[1][:, m * 2 + t, 4 * q:4 * q + 4].bitcast(F32).rearrange("p (b a) -> p a b", a=2)
                        G.tensor_tensor(rl[t][:].rearrange("p (a b) l -> p a b l", a=2),
                                        consts["le_f"][:].unsqueeze(1).unsqueeze(1).broadcast_to([P, 2, 2, P]),
                                        part.unsqueeze(3).broadcast_to([P, 2, 2, P]), ALU.mult).then_inc(c["m_rl"].sem, 1)
                    if q == 0 and first:
                        pool.wait_ge(c["m_ee"].sem, c["m_ee"].at(1))
                        inputs(0, m, False)
                    if q == 2 and more:
                        inputs(1 - h, m + 1, not first)

            for h in range(2):
                G.memset(xp[h][:], 0.0)
                last = G.memset(xd[h][:], 0.0)
            last.then_inc(c["zero"].sem, 1)
            pool.wait_ge(c["zero"].sem, c["zero"].at(1))
            pool.wait_ge(c["m_dl"].sem, c["m_dl"].at(1))
            section(0, 0, first=True)
            with pool.Fori(0, BATCH // 2 - 1) as i:
                section(1, i * 2 + 1)
                section(0, i * 2 + 2)
            section(1, BATCH - 1, more=False)

    for name in ("m_na", "m_ex", "m_ln", "m_dt", "m_dA", "m_dh", "m_dl", "m_sum", "m_ee", "zero"):
        c[name].base += 1
    for name, k in {"m_bc": 4, "m_bh": 4, "m_rh": 8, "m_rl": 8, "m_D": 8, "m_E": 8, "m_CB": 8, "m_off": 4, "m_read": USES,
                    "m_xp": 1, "m_xd": 1, "m_Y": 4, "m_yc": 1, "m_sel": 1, "m_yo": 1, "m_yb": 1, "m_yt": 1, "m_yT": 1,
                    "m_yh": 1, "m_yl": 1, "m_ow": 1, "m_out": 1}.items():
        c[name].base += k * BATCH


def program(nc, a, out):
    with ExitStack() as ctx:
        def sb(name, shape, dt):
            return ctx.enter_context(nc.sbuf_tensor(name, shape, dt))

        def sem(name):
            return ctx.enter_context(nc.semaphore(name))

        x = sb("x", [P, TILES, P], F32)
        xt = [sb(f"xt_{s}", [P, TOKENS], F32R) for s in ("hi", "lo")]
        consts = {
            "ident": sb("ident", [P, P], F32),
            "iota8": sb("iota8", [P, BT, EXPERTS], F32),
            "minus_half": sb("minus_half", [P, BT], F32),
        }
        bias = sb("bias", [P, EXPERTS], F32)
        names = ("a b sil p1 hhi hlo prod row down route xn xt xhi xlo lg lgs lgt gth gates gt gts acc_s ot out "
                 "stats moments veps rstd score gap zero raw0 raw1 raw2 raw3 raw4 raw_hi plain").split()
        counts = {n: Count(sem("s_" + n)) for n in names}
        counts.update({n: Count(sem(n)) for n in RWKV_SEMS})
        counts.update({n: Count(sem(n)) for n in MAMBA_SEMS})
        spare = {n: sem("spare_" + n) for n in ("pe", "act", "dve", "pool")}
        io = sem("io")
        w1 = FfnWeights(sb, "w1", 4)

        x_dram = a["L0_attn_x"].rearrange("b (h p) c -> p (b h) c", p=P)
        out_dram = out.rearrange("b (h p) c -> p (b h) c", p=P)

        def setup():
            made, ones = sem("made"), sem("ones")
            with nc.Block() as block:
                @block.gpsimd
                def _(pool):
                    nc.gpsimd.memset(consts["ident"][:], 0.0).then_inc(ones, 1)
                    nc.gpsimd.memset(consts["minus_half"][:], -0.5)
                    nc.gpsimd.iota(consts["iota8"][:], [[0, BT], [1, EXPERTS]], base=0, channel_multiplier=0,
                                   allow_small_or_imprecise_dtypes=True)
                    pool.wait_ge(ones, 1)
                    nc.gpsimd.affine_select(out=consts["ident"][:], in_=consts["ident"][:],
                                            compare_op=ALU.not_equal, fill=1.0, base=0, pattern=[[-1, P]],
                                            channel_multiplier=1).then_inc(made, 1)

                @block.sync
                def _(sp):
                    sp.dma_start(x[:], x_dram).then_inc(io, 16)
                    sp.dma_start(bias[:], a["L1_ffn_expert_bias"].rearrange("(a e) -> a e", a=1).broadcast_to(
                        [P, EXPERTS])).then_inc(io, 16)
                    sp.wait_ge(io, 32)

        def ffn_jobs(w, gate, up, down, e_up, e_down, router):
            S = w.shared
            jobs = [((S, 2, P), [(lambda r: r[:, :, 0], gate), (lambda r: r[:, :, 1], up)]) + tuple(t[:, 0:S] for t in w.up),
                    ((S, P), [(lambda r: r[:], down)]) + tuple(t[:, 0:S] for t in w.down)]
            for h in range(2):
                s = slice(S + 4 * h, S + 4 * h + 4)
                jobs.append(((4, 2, P), [(lambda r: r[:].rearrange("p e a c -> p e (a c)"), e_up[:, 4 * h:4 * h + 4])])
                            + tuple(t[:, s] for t in w.up))
            jobs.append(((EXPERTS, P), [(lambda r: r[:], e_down)]) + tuple(t[:, S:S + EXPERTS] for t in w.down))
            return jobs

        def router_job(w, name, router):
            s, d = sem(f"{name}_s"), sem(f"{name}_d")
            with nc.sbuf_tensor(f"{name}_raw", [P, P], F32) as raw, nc.Block() as block:
                @block.vector
                def _(dve):
                    nc.vector.memset(raw[:], 0.0).then_inc(s, 1)
                    dve.wait_ge(d, 16)
                    nc.vector.tensor_copy(w.router[0][:], raw[:]).then_inc(s, 1)
                    dve.wait_ge(s, 2)
                    nc.vector.tensor_tensor(w.router[1][:], raw[:], w.router[0][:].bitcast(F32), ALU.subtract)

                @block.sync
                def _(sp):
                    sp.wait_ge(s, 1)
                    sp.dma_start(raw[:, 0:EXPERTS], router).then_inc(d, 16)

        def ps(name, shape, dt):
            return nc.psum_tensor(name, shape, dt)

        def scoped(name, shape, dt):
            return nc.sbuf_tensor(name, shape, dt)

        def rwkv_stage():
            with ExitStack() as scope:
                def keep(name, shape, dt):
                    return scope.enter_context(nc.sbuf_tensor(name, shape, dt))

                w = {n: [keep(f"rw_{n}{s}", [P, k, P], F32R) for s in ("hi", "lo")]
                     for n, k in (("tm", 3), ("cm", 4), ("cp", 4))}
                names = {"w": "time_decay", "u": "time_first", "g1": "g1", "b1": "b1", "g2": "g2", "b2": "b2", "tmk": "tmk",
                         "tmv": "tmv", "tmr": "tmr", "cmk": "cmk", "cmr": "cmr"}
                vec = keep("rw_vec", [P, len(names) + 6], F32)
                v = {n: vec[:, k:k + 1] for k, n in enumerate(list(names) + ["omk", "omv", "omr", "omck", "omcr", "nuh"])}
                vectors = []
                for n, full in names.items():
                    d = a["L0_attn_" + full]
                    d = d.rearrange("(p q) -> p q", q=1) if len(d.shape) == 1 else d.rearrange("q r p -> p (q r)")
                    vectors.append((v[n], d))
                split_phase(nc, counts, scoped, "rw", [
                    ((3, P), [(lambda r: r[:].rearrange("p q c -> p (q c)"), a["L0_attn_W_tm"])]) + tuple(t[:] for t in w["tm"]),
                    ((4, P), [(lambda r: r[:].rearrange("p q c -> p (q c)"), a["L0_attn_W_cm"])]) + tuple(t[:] for t in w["cm"]),
                    ((4, P), [(lambda r: r[:], a["L0_attn_W_cp"].rearrange("(q p) c -> p q c", p=P))]) + tuple(t[:] for t in w["cp"]),
                ], vectors)
                with nc.Block() as block:
                    @block.vector
                    def _(dve):
                        for dst, src in (("omk", "tmk"), ("omv", "tmv"), ("omr", "tmr"), ("omck", "cmk"), ("omcr", "cmr")):
                            nc.vector.tensor_scalar(v[dst], v[src], -1.0, 1.0, ALU.mult, ALU.add)
                        nc.vector.tensor_scalar(v["nuh"], v["u"], -0.5, None, ALU.mult)
                rwkv_phase(nc, counts, spare, scoped, ps, x, xt, consts, w, v)

        def mamba_stage():
            with ExitStack() as scope:
                def keep(name, shape, dt):
                    return scope.enter_context(nc.sbuf_tensor(name, shape, dt))

                w = {n: [keep(f"mb_w{n}{s}", shape, F32R) for s in ("hi", "lo")]
                     for n, shape in (("in", [P, 2 * P]), ("dt", [P, HEADS]), ("bc", [P, 4, 4 * P]), ("out", [P, P]))}
                v = {"b_dt": keep("mb_bdt", [P, HEADS], F32), "neg_a": keep("mb_nega", [P, HEADS], F32)}
                a_log = keep("mb_alog", [P, HEADS], F32)
                a_exp = keep("mb_aexp", [P, HEADS], F32)
                tri = {"gt_f": keep("mb_gtf", [P, P], F32), "le_f": keep("mb_lef", [P, P], F32)}
                cm = dict(consts)
                cm.update(tri)
                for n, shape in (("gt", [P, P]), ("le", [P, P]), ("ident_r", [P, P]), ("never", [P, P])):
                    cm[n] = keep("mb_" + n, shape, F32R)
                jobs = []
                for k, name in enumerate(("L1_attn_W_B", "L1_attn_W_C")):
                    jobs.append(((2, 4 * P), [(lambda r: r[:].rearrange("p r c -> p (r c)"), a[name])])
                                + tuple(t[:, 2 * k:2 * k + 2] for t in w["bc"]))
                for n, name, width in (("in", "L1_attn_W_in", 2 * P), ("dt", "L1_attn_W_dt", HEADS), ("out", "L1_attn_W_out", P)):
                    jobs.append(((width,), [(lambda r: r[:], a[name])]) + tuple(t[:] for t in w[n]))
                row = [P, HEADS]
                split_phase(nc, counts, scoped, "mb", jobs, [
                    (v["b_dt"][:], a["L1_attn_b_dt"].rearrange("(q e) -> q e", q=1).broadcast_to(row)),
                    (a_log[:], a["L1_attn_A_log"].rearrange("(q e) -> q e", q=1).broadcast_to(row))])
                made, done = sem("mb_made"), sem("mb_done")
                with nc.Block() as block:
                    @block.gpsimd
                    def _(pool):
                        G = nc.gpsimd
                        G.memset(cm["gt_f"][:], 1.0)
                        G.memset(cm["le_f"][:], 1.0).then_inc(made, 1)
                        pool.wait_ge(made, 1)
                        G.affine_select(out=cm["gt_f"][:], in_=cm["gt_f"][:], compare_op=ALU.is_gt, fill=0.0, base=0,
                                        pattern=[[-1, P]], channel_multiplier=1)
                        G.affine_select(out=cm["le_f"][:], in_=cm["le_f"][:], compare_op=ALU.is_ge, fill=0.0, base=0,
                                        pattern=[[1, P]], channel_multiplier=-1).then_inc(made, 1)

                    @block.scalar
                    def _(act):
                        nc.scalar.activation(a_exp[:], a_log[:], ACT.Exp).then_inc(done, 1)

                    @block.vector
                    def _(dve):
                        V = nc.vector
                        dve.wait_ge(done, 1)
                        V.tensor_scalar(v["neg_a"][:], a_exp[:], -1.0, None, ALU.mult)
                        V.tensor_copy(cm["ident_r"][:], consts["ident"][:])
                        dve.wait_ge(made, 2)
                        V.tensor_copy(cm["gt"][:], cm["gt_f"][:])
                        V.tensor_copy(cm["le"][:], cm["le_f"][:])
                        V.tensor_scalar(cm["never"][:], cm["gt_f"][:], -1e30, None, ALU.mult)
                kept = {"xraw": keep("mb_xraw", [P, TILES, P], F32), "zs": keep("mb_zs", [P, TILES, P], F32),
                        "u": keep("mb_u", [P, TILES, HEADS], F32)}
                mamba_input(nc, counts, spare, scoped, ps, x, xt, consts, w, v, kept)
                mamba_phase(nc, counts, spare, scoped, ps, x, xt, cm, w, v, kept)

        setup()
        split_phase(nc, counts, scoped, "w1", ffn_jobs(
            w1, a["L1_ffn_shared_w1"].rearrange("d (s i) -> d s i", i=P), a["L1_ffn_shared_w2"].rearrange("d (s i) -> d s i", i=P),
            a["L1_ffn_shared_w3"].rearrange("(s i) c -> i s c", i=P), a["L1_ffn_w12"].rearrange("e d r -> d e r"),
            a["L1_ffn_w3"].rearrange("e r d -> r e d"), None), [])
        router_job(w1, "router1", a["L1_ffn_router_w"])
        w0 = None
        with ExitStack() as inner:
            if "ffn0" in STAGES:
                w0 = FfnWeights(lambda n, s, d: inner.enter_context(nc.sbuf_tensor(n, s, d)), "w0", 2)
                split_phase(nc, counts, scoped, "w0", ffn_jobs(
                    w0, a["L0_ffn_gate_w"].rearrange("d (s i) -> d s i", i=P), a["L0_ffn_up_w"].rearrange("d (s i) -> d s i", i=P),
                    a["L0_ffn_down_w"].rearrange("(s i) c -> i s c", i=P), a["L0_ffn_fc1_w"].rearrange("e d r -> d e r"),
                    a["L0_ffn_fc2_w"].rearrange("e i c -> i e c"), None), [])
                router_job(w0, "router0", a["L0_ffn_w_router"])
            for k, stage in enumerate(STAGES):
                if stage == "mamba":
                    inner.close()
                    mamba_stage()
                if stage == "ffn0":
                    ffn_phase(nc, f"p{k}", counts, spare, scoped, ps, x, xt, consts, w0, True, None)
                if stage == "rwkv":
                    rwkv_stage()
                if stage == "ffn1":
                    ffn_phase(nc, f"p{k}", counts, spare, scoped, ps, x, xt, consts, w1, False, bias)

        with nc.Block() as block:
            @block.sync
            def _(sp):
                sp.dma_start(out_dram, x[:]).then_inc(io, 16)
                sp.wait_ge(io, 48)


_INS = ["L0_attn_x", "L0_attn_time_decay", "L0_attn_time_first", "L0_attn_W_tm", "L0_attn_g1", "L0_attn_b1",
        "L0_attn_tmk", "L0_attn_tmv", "L0_attn_tmr", "L0_attn_W_cm", "L0_attn_W_cp", "L0_attn_g2", "L0_attn_b2",
        "L0_attn_cmk", "L0_attn_cmr", "L0_ffn_w_router", "L0_ffn_fc1_w", "L0_ffn_fc2_w", "L0_ffn_gate_w",
        "L0_ffn_up_w", "L0_ffn_down_w", "L1_attn_W_in", "L1_attn_W_dt", "L1_attn_b_dt", "L1_attn_W_B",
        "L1_attn_W_C", "L1_attn_W_out", "L1_attn_A_log", "L1_ffn_w12", "L1_ffn_w3", "L1_ffn_shared_w1",
        "L1_ffn_shared_w2", "L1_ffn_shared_w3", "L1_ffn_router_w", "L1_ffn_expert_bias"]
_TURNED = {"L1_attn_W_in", "L1_attn_W_dt", "L1_attn_W_B", "L1_attn_W_C", "L1_attn_W_out", "L1_ffn_w12", "L1_ffn_w3",
           "L1_ffn_shared_w1", "L1_ffn_shared_w2", "L1_ffn_shared_w3", "L1_ffn_router_w"}


def kernel(**inputs):
    import numpy as _np
    import concourse.bacc as _bacc
    from concourse import mybir as _mybir
    from concourse.bass_utils import run_bass_kernel_spmd as _run

    nc = _bacc.Bacc("TRN2", target_bir_lowering=False, num_devices=1)
    arrays, aps = {}, {}
    for name in _INS:
        v = _np.asarray(inputs[name])
        if name in _TURNED:
            v = _np.swapaxes(v, -1, -2)
        v = _np.ascontiguousarray(v)
        arrays[f"in_{name}_dram"] = v
        aps[name] = nc.dram_tensor(f"in_{name}_dram", v.shape, _mybir.dt.from_np(v.dtype), kind="ExternalInput").ap()
    out = nc.dram_tensor("out_0_dram", (BATCH, SEQ, P), F32, kind="ExternalOutput").ap()
    program(nc, aps, out)
    r = _run(nc, [arrays], core_ids=[0])
    return r.results[0]["out_0_dram"]
```

```python
from contextlib import ExitStack

import concourse.bass as bass
from concourse import mybir

ALU = mybir.AluOpType
ACT = mybir.ActivationFunctionType
F32 = mybir.dt.float32
F32R = mybir.dt.float32r
BF16 = mybir.dt.bfloat16
U32 = mybir.dt.uint32

P = 128
BATCH, SEQ = 8, 256
TOKENS = BATCH * SEQ
TILES = TOKENS // P
BT = 4
BLK = BT * P
NBLK = TILES // BT
EXPERTS = 8
LN_EPS = 1e-5

STAGES = ("ffn0", "rwkv", "ffn0", "ffn1", "mamba", "ffn1")


class Count:

    def __init__(self, sem):
        self.sem = sem
        self.base = 0

    def at(self, value):
        least = value if isinstance(value, int) else value.min_val
        assert least + self.base > 0
        return value + self.base


class FfnWeights:

    def __init__(self, sb, tag, shared):
        self.shared = shared
        self.units = shared + EXPERTS
        self.up = [sb(f"{tag}_up{s}", [P, self.units, 2, P], F32R) for s in ("hi", "lo")]
        self.down = [sb(f"{tag}_down{s}", [P, self.units, P], F32R) for s in ("hi", "lo")]
        self.router = [sb(f"{tag}_router{s}", [P, EXPERTS], F32R) for s in ("hi", "lo")]


class RawWeights:

    def __init__(self, sb, c, tag, jobs, extra=(), one_semaphore=True, raws=None):
        self.jobs, self.extra = jobs, extra
        self.raws = raws or [sb(f"{tag}_rawbuf{k}", [P] + list(j[0]), F32)[:] for k, j in enumerate(jobs)]
        loads = [16 * len(j[1]) for j in jobs]
        if one_semaphore:
            self.arrived = [(c[f"{tag}_raw"], sum(loads) + 16 * len(extra))] * len(jobs)
        else:
            self.arrived = [(c[f"raw{k}"], n) for k, n in enumerate(loads)]

    def load(self, sp):
        for (shape, parts, hi, lo), raw, (count, total) in zip(self.jobs, self.raws, self.arrived):
            for view, source in parts:
                sp.dma_start(view(raw), source).then_inc(count.sem, 16)
        for dst, source in self.extra:
            sp.dma_start(dst, source).then_inc(self.arrived[0][0].sem, 16)


def split_jobs(sets):
    return [(job, raw, arrived) for s in sets for job, raw, arrived in zip(s.jobs, s.raws, s.arrived)]


def split_hi(nc, act, c, job):
    (shape, parts, hi, lo), raw, (count, total) = job
    act.wait_ge(count.sem, count.at(total))
    nc.scalar.copy(hi, raw).then_inc(c["raw_hi"].sem, 1)


def split_lo(nc, dve, c, job, k):
    (shape, parts, hi, lo), raw, arrived = job
    dve.wait_ge(c["raw_hi"].sem, c["raw_hi"].at(k + 1))
    nc.vector.tensor_tensor(lo, raw, hi.bitcast(F32), ALU.subtract).then_inc(c["raw_lo"].sem, 1)


def three_pass(pe, out, weights, moving, start, stop):
    pe.matmul(out, weights[0], moving[0], start=start, stop=False)
    pe.matmul(out, weights[0], moving[1], start=False, stop=False)
    return pe.matmul(out, weights[1], moving[0], start=False, stop=stop)


class Start:

    def __init__(self, nc, c, norm, x, xt, ident, half):
        self.nc, self.c, self.norm, self.x, self.xt, self.ident, self.half = (
            nc, c, norm, x, xt, ident, half)

    def stats(self, dve):
        c, norm = self.c, self.norm
        for j in range(BT):
            last = self.nc.vector.bn_stats(norm["stats"][:, j], self.x[:, j])
        last.then_inc(c["stats"].sem, 1)
        dve.wait_ge(c["stats"].sem, c["stats"].at(NBLK + 1))
        for j in range(BT):
            last = self.nc.vector.bn_aggr(norm["moments"][:, j], norm["stats"][:, j])
        last.then_inc(c["moments"].sem, 1)

    def scale(self, pool):
        c, norm = self.c, self.norm
        pool.wait_ge(c["moments"].sem, c["moments"].at(NBLK + 1))
        self.nc.gpsimd.tensor_scalar(norm["veps"][:], norm["moments"][:, :, 1], LN_EPS, None, ALU.add).then_inc(c["veps"].sem, 1)
        pool.wait_ge(c["veps"].sem, c["veps"].at(NBLK + 1))
        self.nc.gpsimd.tensor_tensor(norm["rstd"][:], norm["veps"][:], self.half[:, 0:BT], ALU.pow).then_inc(c["rstd"].sem, 1)

    def apply(self, dve):
        c, norm = self.c, self.norm
        dve.wait_ge(c["rstd"].sem, c["rstd"].at(NBLK + 1))
        for j in range(BT):
            last = self.nc.vector.tensor_scalar(norm["xn"][:, j], self.x[:, j], norm["moments"][:, j, 0:1],
                                                norm["rstd"][:, j:j + 1], ALU.subtract, ALU.mult)
        last.then_inc(c["xn"].sem, 1)

    def turn(self, pe, bank):
        c = self.c
        pe.wait_ge(c["xn"].sem, c["xn"].at(NBLK + 1))
        for j in range(BT):
            last = pe.transpose(bank[:, bass.ts(j, P)], self.norm["xn"][:, j], self.ident[:])
        last.then_inc(c["xt"].sem, 1)

    def high(self, act, bank):
        c = self.c
        act.wait_ge(c["xt"].sem, c["xt"].at(NBLK + 1))
        self.nc.scalar.copy(self.xt[0][:, 0:BLK], bank).then_inc(c["xhi"].sem, 1)

    def low(self, dve, bank):
        c = self.c
        dve.wait_ge(c["xhi"].sem, c["xhi"].at(NBLK + 1))
        self.nc.vector.tensor_tensor(self.xt[1][:, 0:BLK], bank, self.xt[0][:, 0:BLK].bitcast(F32),
                                     ALU.subtract).then_inc(c["xlo"].sem, 1)


def ffn_phase(nc, tag, counts, spare, sb, ps, x, xt, consts, w, softmax, expert_bias, gate_dram, norm,
              loads=(), splits=(), out_dram=None, begun=False, start_next=False):
    splits = split_jobs(splits)
    U, S = w.units, w.shared
    LEAD = 3
    ROWS = 4
    HR = 5 if U % 5 == 0 else 4
    DVE_SLOTS = {1: 2, 4: 3, 5: 4}
    PE_SLOTS = {1: 0, 2: 1, 3: 2, 6 if softmax else 7: 3}
    ACT_SLOTS = {1: 0, 2: 1, 4 if softmax else 3: 2, 6 if softmax else 7: 3}
    NORM_SLOTS = {U - 4: 0, U - 1: 1}
    NORM_EXPERT = EXPERTS - 1
    xhi, xlo = xt
    c = counts
    credit = {"down": HR, "sil": 2, "p1": 2, "hhi": 2, "hlo": 2, "prod": 4, "acc_s": 1, "ot": 1, "out": 2, "gts": 1, "store": 1, "xt": 1}
    for name, k in credit.items():
        c[name].base += k
    with ExitStack() as ctx:
        def tile(name, shape, dt=F32):
            return ctx.enter_context(sb(f"{tag}_{name}", shape, dt))

        stats, moments, veps, rstd, xn = (norm[n] for n in ("stats", "moments", "veps", "rstd", "xn"))
        start = Start(nc, c, norm, x, xt, consts["ident"], consts["minus_half"])
        logits_t = tile("logits_t", [EXPERTS, BLK])
        key = tile("key", [P, BT, EXPERTS])
        th = tile("th", [P, BT, EXPERTS])
        score = tile("score", [P, BT, EXPERTS])
        top = tile("top", [P, BT, 8])
        topi = tile("topi", [P, BT, 8], U32)
        hot = tile("hot", [P, 2, BT, EXPERTS])
        gap = tile("gap", [P, BT])
        gth = tile("gth", [P, BT])
        g12 = tile("g12", [P, 2, BT])
        hot1 = tile("hot1", [P, BT, EXPERTS])
        gates = tile("gates", [P, EXPERTS, BT])
        gates_t = tile("gates_t", [EXPERTS * BT, P])
        gate_row = tile("gate_row", [P, ROWS, BLK])
        sil = tile("sil", [P, 2, BLK])
        p1 = tile("p1", [P, 2, BLK])
        prod = tile("prod", [P, 2, BLK])
        hhi = tile("hhi", [P, HR, BLK], F32R)
        hlo = tile("hlo", [P, HR, BLK], F32R)
        acc_s = tile("acc_s", [P, BLK])
        ps_a = ctx.enter_context(ps(f"{tag}_ps_a", [P, 2, BLK], F32))
        ps_b = ctx.enter_context(ps(f"{tag}_ps_b", [P, 2, BLK], F32))
        ps_acc = ctx.enter_context(ps(f"{tag}_ps_acc", [P, BLK], F32))
        ps_t = ctx.enter_context(ps(f"{tag}_ps_t", [P, BLK], F32))
        ps_l = ctx.enter_context(ps(f"{tag}_ps_l", [P, BLK], F32))
        block = ctx.enter_context(nc.Block())
        gates_w = gates[:].rearrange("p e j -> p j e")
        rank = consts["iota8"]

        def src(g):
            return prod[:, g % 2, :]

        @block.tensor
        def _(pe):
            def up(n, u):
                if u == 0:
                    pe.wait_ge(c["xlo"].sem, c["xlo"].at(n + 1))
                g = n * U + u
                xs = [xhi[:, bass.ts(n, BLK)], xlo[:, bass.ts(n, BLK)]]
                pe.wait_ge(c["sil"].sem, c["sil"].at(g - 1))
                three_pass(pe, ps_a[:, u % 2], [t[:, u, 0] for t in w.up], xs, True, True).then_inc(c["a"].sem, 1)
                pe.wait_ge(c["p1"].sem, c["p1"].at(g - 1))
                three_pass(pe, ps_b[:, u % 2], [t[:, u, 1] for t in w.up], xs, True, True).then_inc(c["b"].sem, 1)

            def down(n, u):
                g = n * U + u
                if u == 0:
                    pe.wait_ge(c["acc_s"].sem, c["acc_s"].at(n))
                pe.wait_ge(c["hlo"].sem, c["hlo"].at(g + 1))
                three_pass(pe, ps_acc[:], [t[:, u] for t in w.down], [hhi[:, u % HR], hlo[:, u % HR]],
                           u == 0, u == U - 1).then_inc(c["down"].sem, 1)

            def head(n, step):
                if step == 0:
                    pe.wait_ge(c["xn"].sem, c["xn"].at(n + 1))
                    pe.wait_ge(c["gts"].sem, c["gts"].at(n))
                    for j in range(BT):
                        last = pe.transpose(ps_t[:, bass.ts(j, P)], xn[:, j], consts["ident"][:])
                    last.then_inc(c["xt"].sem, 1)
                if step == 1:
                    pe.wait_ge(c["xlo"].sem, c["xlo"].at(n + 1))
                    xs = [xhi[:, bass.ts(n, BLK)], xlo[:, bass.ts(n, BLK)]]
                    pe.wait_ge(c["out"].sem, c["out"].at(n - 1))
                    three_pass(pe, ps_l[0:EXPERTS, :], [t[:] for t in w.router], xs, True, True).then_inc(c["lg"].sem, 1)
                if step == 2:
                    pe.wait_ge(c["lgs"].sem, c["lgs"].at(n + 1))
                    pe.sem_inc(spare["pe"], 1)
                    for j in range(BT):
                        last = pe.transpose(ps_t[:, bass.ts(j, EXPERTS)], logits_t[:, bass.ts(j, P)],
                                            consts["ident"][0:EXPERTS, 0:EXPERTS])
                    last.then_inc(c["lgt"].sem, 1)
                if step == 3:
                    pe.wait_ge(c["gates"].sem, c["gates"].at(n + 1))
                    pe.transpose(ps_t[0:EXPERTS * BT, 0:P], gates[:].rearrange("p e j -> p (e j)"),
                                 consts["ident"][:]).then_inc(c["gt"].sem, 1)

            def final(n):
                pe.wait_ge(c["acc_s"].sem, c["acc_s"].at(n + 1))
                pe.wait_ge(c["lgs"].sem, c["lgs"].at(n + 2 if has_next(n) else NBLK))
                for j in range(BT):
                    last = pe.transpose(ps_l[:, bass.ts(j, P)], acc_s[:, bass.ts(j, P)], consts["ident"][:])
                last.then_inc(c["ot"].sem, 1)

            def has_next(n):
                return not isinstance(n, int) or n + 1 < NBLK

            def body(n, more):
                for p in range(U):
                    u = p + LEAD
                    if u < U:
                        up(n, u)
                    elif more:
                        up(n + 1, u - U)
                    if p < U - 1:
                        down(n, p)
                    if p == U - 2:
                        down(n, U - 1)
                    if more and p in PE_SLOTS:
                        head(n + 1, PE_SLOTS[p])
                    if start_next and not more and p == 6:
                        pe.wait_ge(c["gts"].sem, c["gts"].at(NBLK))
                        start.turn(pe, ps_t)
                final(n)

            for name, k in credit.items():
                pe.sem_inc(c[name].sem, k)
            if not begun:
                head(0, 0)
            head(0, 1)
            up(0, 0)
            head(0, 2)
            up(0, 1)
            head(0, 3)
            up(0, 2)
            with pe.Fori(0, NBLK - 1) as n:
                body(n, True)
            body(NBLK - 1, False)

        @block.scalar
        def _(act):
            def unit(n, u):
                g = n * U + u
                act.wait_ge(c["a"].sem, c["a"].at(g + 1))
                act.wait_ge(c["p1"].sem, c["p1"].at(g - 1))
                nc.scalar.activation(sil[:, u % 2], ps_a[:, u % 2], ACT.Silu).then_inc(c["sil"].sem, 1)

            def high(n, u):
                g = n * U + u
                if u < S:
                    act.wait_ge(c["p1"].sem, c["p1"].at(g + 1))
                else:
                    act.wait_ge(c["prod"].sem, c["prod"].at(n * EXPERTS + u - S + 1))
                act.wait_ge(c["down"].sem, c["down"].at(g + 1 - HR))
                nc.scalar.copy(hhi[:, u % HR], src(u)).then_inc(c["hhi"].sem, 1)

            def head(n, step):
                if step == 0:
                    act.wait_ge(c["xt"].sem, c["xt"].at(n + 1))
                    nc.scalar.copy(xhi[:, bass.ts(n, BLK)], ps_t[:]).then_inc(c["xhi"].sem, 1)
                if step == 1:
                    act.wait_ge(c["lg"].sem, c["lg"].at(n + 1))
                    nc.scalar.copy(logits_t[:], ps_l[0:EXPERTS, :]).then_inc(c["lgs"].sem, 1)
                if step == 2:
                    if softmax:
                        act.wait_ge(c["gap"].sem, c["gap"].at(n + 1))
                        nc.scalar.activation(gth[:], gap[:], ACT.Tanh, scale=0.5).then_inc(c["gth"].sem, 1)
                    else:
                        act.wait_ge(c["lgt"].sem, c["lgt"].at(n + 1))
                        nc.scalar.activation(th[:], ps_t[:, 0:BT * EXPERTS].rearrange("p (j e) -> p j e", j=BT),
                                             ACT.Tanh, scale=0.5).then_inc(c["gth"].sem, 1)
                if step == 3:
                    act.wait_ge(c["gt"].sem, c["gt"].at(n + 1))
                    act.wait_ge(c["store"].sem, c["store"].at(n))
                    nc.scalar.copy(gates_t[:], ps_t[0:EXPERTS * BT, 0:P]).then_inc(c["gts"].sem, 1)

            def final(n):
                act.wait_ge(c["down"].sem, c["down"].at((n + 1) * U))
                act.wait_ge(c["ot"].sem, c["ot"].at(n))
                nc.scalar.copy(acc_s[:], ps_acc[:]).then_inc(c["acc_s"].sem, 1)

            def body(n, more):
                for p in range(U):
                    u = p + LEAD
                    if p == U - 1 and more:
                        final(n)
                    if u < U:
                        unit(n, u)
                        high(n, u - 1)
                    elif more:
                        unit(n + 1, u - U)
                        if u == U:
                            high(n, U - 1)
                        else:
                            high(n + 1, u - U - 1)
                    elif u == U:
                        high(n, U - 1)
                    if more and p in ACT_SLOTS:
                        head(n + 1, ACT_SLOTS[p])
                    if not more and p < len(splits):
                        split_hi(nc, act, c, splits[p])
                    if start_next and not more and p == 7:
                        start.high(act, ps_t[:])
                if not more:
                    final(n)

            if not begun:
                head(0, 0)
            head(0, 1)
            unit(0, 0)
            head(0, 2)
            unit(0, 1)
            high(0, 0)
            head(0, 3)
            unit(0, 2)
            high(0, 1)
            with act.Fori(0, NBLK - 1) as n:
                body(n, True)
            body(NBLK - 1, False)

        @block.vector
        def _(dve):
            def unit(n, u):
                g = n * U + u
                dve.wait_ge(c["sil"].sem, c["sil"].at(g + 1))
                dve.wait_ge(c["b"].sem, c["b"].at(g + 1))
                if u < S:
                    dst = src(u)
                    dve.wait_ge(c["hhi"].sem, c["hhi"].at(g - 1))
                    dve.wait_ge(c["hlo"].sem, c["hlo"].at(g - 1))
                else:
                    dst = p1[:, u % 2]
                    dve.wait_ge(c["prod"].sem, c["prod"].at(n * EXPERTS + u - S - 1))
                nc.vector.tensor_tensor(dst, sil[:, u % 2], ps_b[:, u % 2], ALU.mult).then_inc(c["p1"].sem, 1)

            def low(n, u):
                g = n * U + u
                dve.wait_ge(c["hhi"].sem, c["hhi"].at(g + 1))
                nc.vector.tensor_tensor(hlo[:, u % HR], src(u), hhi[:, u % HR].bitcast(F32),
                                        ALU.subtract).then_inc(c["hlo"].sem, 1)

            def head(n, step):
                if step == 0:
                    for j in range(BT):
                        last = nc.vector.bn_stats(stats[:, j], x[:, n * BT + j])
                    last.then_inc(c["stats"].sem, 1)
                    dve.wait_ge(c["stats"].sem, c["stats"].at(n + 1))
                    dve.sem_inc(spare["dve"], 1)
                    for j in range(BT):
                        last = nc.vector.bn_aggr(moments[:, j], stats[:, j])
                    last.then_inc(c["moments"].sem, 1)
                if step == 1:
                    dve.wait_ge(c["rstd"].sem, c["rstd"].at(n + 1))
                    dve.wait_ge(c["moments"].sem, c["moments"].at(n + 1))
                    dve.wait_ge(c["xt"].sem, c["xt"].at(n))
                    for j in range(BT):
                        last = nc.vector.tensor_scalar(xn[:, j], x[:, n * BT + j], moments[:, j, 0:1], rstd[:, j:j + 1],
                                                       ALU.subtract, ALU.mult)
                    last.then_inc(c["xn"].sem, 1)
                if step == 2:
                    dve.wait_ge(c["xhi"].sem, c["xhi"].at(n + 1))
                    nc.vector.tensor_tensor(xlo[:, bass.ts(n, BLK)], ps_t[:], xhi[:, bass.ts(n, BLK)].bitcast(F32),
                                            ALU.subtract).then_inc(c["xlo"].sem, 1)
                if step == 3:
                    k0 = 5 * n
                    if softmax:
                        dve.wait_ge(c["lgt"].sem, c["lgt"].at(n + 1))
                        nc.vector.tensor_copy(key[:], ps_t[:, 0:BT * EXPERTS].rearrange(
                            "p (j e) -> p j e", j=BT)).then_inc(c["route"].sem, 1)
                        dve.wait_ge(c["route"].sem, c["route"].at(k0 + 1))
                        dve.sem_inc(spare["dve"], 1)
                    else:
                        dve.wait_ge(c["gth"].sem, c["gth"].at(n + 1))
                        nc.vector.tensor_scalar(score[:], th[:], 0.5, 0.5, ALU.mult, ALU.add).then_inc(c["score"].sem, 1)
                        dve.wait_ge(c["score"].sem, c["score"].at(n + 1))
                        nc.vector.tensor_tensor(key[:], score[:], expert_bias[:].unsqueeze(1).broadcast_to([P, BT, EXPERTS]),
                                                ALU.add).then_inc(c["route"].sem, 1)
                        dve.wait_ge(c["route"].sem, c["route"].at(k0 + 1))
                        dve.sem_inc(spare["dve"], 1)
                    for j in range(BT):
                        last = nc.vector.max(top[:, j], key[:, j])
                    last.then_inc(c["route"].sem, 1)
                    dve.wait_ge(c["route"].sem, c["route"].at(k0 + 2))
                    dve.sem_inc(spare["dve"], 1)
                    for j in range(BT):
                        last = nc.vector.max_index(topi[:, j], top[:, j], key[:, j])
                    last.then_inc(c["route"].sem, 1)
                    if softmax:
                        nc.vector.tensor_tensor(gap[:], top[:, :, 0], top[:, :, 1], ALU.subtract).then_inc(c["gap"].sem, 1)
                    dve.wait_ge(c["route"].sem, c["route"].at(k0 + 3))
                    for k in range(2):
                        last = nc.vector.tensor_tensor(hot[:, k], rank[:], topi[:, :, k:k + 1].broadcast_to([P, BT, EXPERTS]),
                                                       ALU.is_equal)
                    last.then_inc(c["route"].sem, 1)
                if step == 4:
                    k0 = 5 * n
                    if softmax:
                        dve.wait_ge(c["gth"].sem, c["gth"].at(n + 1))
                        nc.vector.tensor_scalar(g12[:, 0], gth[:], 0.5, 0.5, ALU.mult, ALU.add)
                        nc.vector.tensor_scalar(g12[:, 1], gth[:], -0.5, 0.5, ALU.mult, ALU.add).then_inc(c["score"].sem, 1)
                        dve.wait_ge(c["score"].sem, c["score"].at(n + 1))
                        dve.wait_ge(c["route"].sem, c["route"].at(k0 + 4))
                        nc.vector.tensor_tensor(score[:], hot[:, 0], g12[:, 0].unsqueeze(2).broadcast_to([P, BT, EXPERTS]),
                                                ALU.mult)
                        nc.vector.tensor_tensor(hot1[:], hot[:, 1], g12[:, 1].unsqueeze(2).broadcast_to([P, BT, EXPERTS]),
                                                ALU.mult).then_inc(c["route"].sem, 1)
                        dve.wait_ge(c["route"].sem, c["route"].at(k0 + 5))
                        nc.vector.tensor_tensor(gates_w, score[:], hot1[:], ALU.add).then_inc(c["gates"].sem, 1)
                    else:
                        dve.wait_ge(c["route"].sem, c["route"].at(k0 + 4))
                        nc.vector.tensor_tensor(hot1[:], hot[:, 0], hot[:, 1], ALU.add).then_inc(c["route"].sem, 1)
                        dve.wait_ge(c["route"].sem, c["route"].at(k0 + 5))
                        nc.vector.tensor_tensor(gates_w, score[:], hot1[:], ALU.mult).then_inc(c["gates"].sem, 1)

            def final(n):
                dve.wait_ge(c["ot"].sem, c["ot"].at(n + 1))
                xb = x[:, bass.ts(n, BT)]
                nc.vector.scalar_tensor_tensor(out=xb, in0=ps_l[:].rearrange("p (j c) -> p j c", j=BT), scalar=0.5,
                                               in1=xb, op0=ALU.mult, op1=ALU.add).then_inc(c["out"].sem, 1)

            def body(n, more, ahead):
                for p in range(U):
                    u = p + LEAD
                    if u < U:
                        unit(n, u)
                        low(n, u - 1)
                    elif more:
                        unit(n + 1, u - U)
                        if u == U:
                            low(n, U - 1)
                        else:
                            low(n + 1, u - U - 1)
                    elif u == U:
                        low(n, U - 1)
                    if more and p in DVE_SLOTS:
                        head(n + 1, DVE_SLOTS[p])
                    if ahead and p in NORM_SLOTS:
                        head(n + 2, NORM_SLOTS[p])
                    if not more and p < len(splits):
                        split_lo(nc, dve, c, splits[p], p)
                    if start_next and not more:
                        if p == 2:
                            dve.wait_ge(c["out"].sem, c["out"].at(1))
                            start.stats(dve)
                        if p == 4:
                            dve.wait_ge(c["xt"].sem, c["xt"].at(NBLK))
                            start.apply(dve)
                        if p == 8:
                            start.low(dve, ps_t[:])
                final(n)

            for step in range(4):
                if step == 3 or not begun:
                    head(0, step)
                if step == 2:
                    head(1, 0)
            unit(0, 0)
            head(0, 4)
            head(1, 1)
            unit(0, 1)
            low(0, 0)
            unit(0, 2)
            low(0, 1)
            with dve.Fori(0, NBLK - 2) as n:
                body(n, True, True)
            body(NBLK - 2, True, False)
            body(NBLK - 1, False, False)

        @block.gpsimd
        def _(pool):
            def weigh(n, e):
                g = n * EXPERTS + e
                u = S + e
                row = c[f"row{e % ROWS}"]
                pool.wait_ge(row.sem, row.at(n * (16 * EXPERTS // ROWS) + 16 * (e // ROWS + 1)))
                pool.wait_ge(c["p1"].sem, c["p1"].at(n * U + u + 1))
                pool.wait_ge(c["hlo"].sem, c["hlo"].at(n * U + u - 1))
                nc.gpsimd.tensor_tensor(src(u), p1[:, u % 2], gate_row[:, e % ROWS], ALU.mult).then_inc(c["prod"].sem, 1)

            def head(n):
                pool.wait_ge(c["moments"].sem, c["moments"].at(n + 1))
                pool.sem_inc(spare["pool"], 1)
                nc.gpsimd.tensor_scalar(veps[:], moments[:, :, 1], LN_EPS, None, ALU.add).then_inc(c["veps"].sem, 1)
                pool.wait_ge(c["veps"].sem, c["veps"].at(n + 1))
                nc.gpsimd.tensor_tensor(rstd[:], veps[:], consts["minus_half"][:, 0:BT], ALU.pow).then_inc(c["rstd"].sem, 1)

            def body(n, ahead):
                for e in range(EXPERTS):
                    weigh(n, e)
                    if e == NORM_EXPERT and ahead:
                        head(n + 2)
                    if start_next and e == 3 and isinstance(n, int) and n == NBLK - 1:
                        start.scale(pool)

            if not begun:
                head(0)
            head(1)
            with pool.Fori(0, NBLK - 2) as n:
                body(n, True)
            body(NBLK - 2, False)
            body(NBLK - 1, False)

        @block.sync
        def _(sp):
            def rows(n):
                sp.wait_ge(c["gts"].sem, c["gts"].at(n + 1))
                sp.dma_start(gate_dram[bass.ts(n, EXPERTS * BT)], gates_t[:]).then_inc(c["stored"].sem, 16)
                sp.wait_ge(c["stored"].sem, c["stored"].at(n * 16 + 16))
                sp.sem_inc(c["store"].sem, 1)
                for e in range(EXPERTS):
                    sp.wait_ge(c["prod"].sem, c["prod"].at(n * EXPERTS + (e + 1 - ROWS)))
                    source = gate_dram[bass.ds(n * (EXPERTS * BT) + e * BT, BT)].rearrange("(q j) t -> q (j t)", q=1)
                    sp.dma_start(gate_row[:, e % ROWS], source.broadcast_to([P, BLK])).then_inc(c[f"row{e % ROWS}"].sem, 16)

            rows(0)
            for later in loads:
                later.load(sp)
            with sp.Fori(1, NBLK) as n:
                rows(n)
                if out_dram is not None:
                    sp.wait_ge(c["out"].sem, c["out"].at(n))
                    sp.dma_start(out_dram[:, bass.ts(n - 1, BT)], x[:, bass.ts(n - 1, BT)]).then_inc(c["io"].sem, 16)
            if out_dram is not None:
                sp.wait_ge(c["out"].sem, c["out"].at(NBLK))
                last = slice((NBLK - 1) * BT, NBLK * BT)
                sp.dma_start(out_dram[:, last], x[:, last]).then_inc(c["io"].sem, 16)
                sp.wait_ge(c["io"].sem, c["io"].at(16 * NBLK))

    per = {"store": 1, "stored": 16, "row0": 32, "row1": 32, "row2": 32, "row3": 32, "a": U, "b": U, "sil": U, "p1": U, "hhi": U, "hlo": U, "prod": EXPERTS, "route": 5}
    for name in ("xn", "xt", "xhi", "xlo", "lg", "lgs", "lgt", "gth", "gates", "gt", "gts", "acc_s", "ot", "out",
                 "stats", "moments", "veps", "rstd", "score"):
        per[name] = 1
    if softmax:
        per["gap"] = 1
    for name, k in per.items():
        c[name].base += k * NBLK
    c["down"].base += U * NBLK
    c["raw_hi"].base += len(splits)
    c["raw_lo"].base += len(splits)


def rwkv_phase(nc, counts, spare, sb, ps, x, xt, consts, w, v):
    LOW = -1e38
    NS = BLK // SEQ
    T1 = SEQ + 1
    c = counts
    credit = {"r_out": 1}
    for name, k in credit.items():
        c[name].base += k
    with ExitStack() as ctx:
        def tiles(name, shape, dt=F32):
            return [ctx.enter_context(sb(f"rw_{name}{h}", shape, dt)) for h in range(2)]

        stats1 = ctx.enter_context(sb("rw_stats_all", [P, TILES, 6], F32))
        mom1 = ctx.enter_context(sb("rw_mom_all", [P, TILES, 2], F32))
        rs1 = ctx.enter_context(sb("rw_rs_all", [P, 5, TILES], F32))
        stats = tiles("stats", [P, BT, 6])
        mom = tiles("mom", [P, BT, 2])
        rs = tiles("rs", [P, 2, BT])
        ytok = tiles("ytok", [P, BT, P])
        ztok = tiles("ztok", [P, BT, P])
        y0 = tiles("y0", [P, NS, T1])
        zf = tiles("zf", [P, BLK])
        xpk, xpv, xpr = tiles("xpk", [P, BLK]), tiles("xpv", [P, BLK]), tiles("xpr", [P, BLK])
        key, val = tiles("key", [P, NS, SEQ]), tiles("val", [P, NS, SEQ])
        rg = tiles("rg", [P, NS, SEQ])
        mx, bb, aa, x2 = (tiles(n, [P, NS, T1]) for n in ("mx", "bb", "aa", "x2"))
        t1, t2, t3, t4 = (tiles(n, [P, NS, SEQ]) for n in ("t1", "t2", "t3", "t4"))
        sq = tiles("sq", [P, BLK])
        shi, slo = tiles("shi", [P, 2, BLK], F32R), tiles("slo", [P, 2, BLK], F32R)
        b1 = ctx.enter_context(ps("rw_b1", [P, BLK], F32))
        b2 = ctx.enter_context(ps("rw_b2", [P, BLK], F32))
        ba, bv, bc = ([ctx.enter_context(ps(f"rw_{n}{h}", [P, BLK], F32)) for h in range(2)] for n in ("ba", "bv", "bc"))
        turned = ((b1, b2), (ba[1], bv[1]))
        sqs = [(sq[h][:], t2[h][:].rearrange("p b t -> p (b t)")) for h in range(2)]
        block = ctx.enter_context(nc.Block())
        ident = consts["ident"]

        def seqs(bank):
            return bank[:].rearrange("p (b t) -> p b t", b=NS)

        def tok(bank):
            return bank[:].rearrange("p (j c) -> p j c", j=BT)

        def mid(buf):
            return buf[:, :, 1:T1]

        def prev(buf):
            return buf[:, :, 0:SEQ]

        def blk(t, m):
            return t[:, bass.ts(m, BLK)]

        def slot(i, j, h):
            return i * 8 + (2 * j + h + 1)

        def w_row():
            return v["w"].broadcast_to([P, SEQ])

        @block.tensor
        def _(pe):
            def turn_ln(h, m):
                pe.wait_ge(c["r_tok"].sem, c["r_tok"].at(m + 1))
                if h == 0:
                    pe.wait_ge(c["r_out"].sem, c["r_out"].at(m))
                for src, bank in zip((ytok, ztok), turned[h]):
                    for j in range(BT):
                        last = pe.transpose(bank[:, bass.ts(j, P)], src[h][:, j], ident[:])
                last.then_inc(c["r_tt"].sem, 1)

            def kvr(h, m):
                pe.wait_ge(c["r_zl"].sem, c["r_zl"].at(m + 1))
                for q, bank in enumerate((ba[h], bv[h], bc[h])):
                    three_pass(pe, bank[:], [t[:, q] for t in w["tm"]], [blk(xt[0], m), blk(xt[1], m)],
                               True, True).then_inc(c["r_kvr"].sem, 1)

            def turn_x2(h, m):
                pe.wait_ge(c["r_x2"].sem, c["r_x2"].at(m + 1))
                for j in range(BT):
                    b, s = j // 2, j % 2
                    last = pe.transpose(ba[h][:, bass.ts(j, P)], x2[h][:, b, 1 + s * P:1 + (s + 1) * P], ident[:])
                last.then_inc(c["r_t2"].sem, 1)

            def turn_ln2(h, m):
                pe.wait_ge(c["r_tok2"].sem, c["r_tok2"].at(m + 1))
                for j in range(BT):
                    last = pe.transpose(bv[h][:, bass.ts(j, P)], ztok[h][:, j], ident[:])
                last.then_inc(c["r_t3"].sem, 1)

            def channel(i):
                def grow(j):
                    for h in range(2):
                        if j == 0:
                            pe.wait_ge(c["r_zl2"].sem, c["r_zl2"].at(i * 2 + h + 1))
                        if j >= 2:
                            pe.wait_ge(c["r_kx"].sem, c["r_kx"].at(slot(i, j - 2, h)))
                        xs = [blk(xt[0], i * 2 + h), blk(xt[1], i * 2 + h)]
                        three_pass(pe, (ba[h], bv[h])[j % 2][:], [t[:, j] for t in w["cm"]], xs, True, True).then_inc(c["r_kk"].sem, 1)

                def shrink(j):
                    for h in range(2):
                        pe.wait_ge(c["r_sl"].sem, c["r_sl"].at(slot(i, j, h)))
                        three_pass(pe, bc[h][:], [t[:, j] for t in w["cp"]], [shi[h][:, j % 2], slo[h][:, j % 2]],
                                   j == 0, j == 3).then_inc(c["r_vv"].sem, 1)

                grow(0)
                grow(1)
                for j in range(4):
                    if j + 2 < 4:
                        grow(j + 2)
                    shrink(j)

            def turn_out(h, m):
                pe.wait_ge(c["r_o"].sem, c["r_o"].at(m + 1))
                for j in range(BT):
                    b, s = j // 2, j % 2
                    last = pe.transpose((b1, b2)[h][:, bass.ts(j, P)], t4[h][:, b, s * P:(s + 1) * P], ident[:])
                last.then_inc(c["r_ot"].sem, 1)

            for name, k in credit.items():
                pe.sem_inc(c[name].sem, k)
            with pe.Fori(0, NBLK // 2) as i:
                for h in range(2):
                    turn_ln(h, i * 2 + h)
                for h in range(2):
                    kvr(h, i * 2 + h)
                for h in range(2):
                    turn_x2(h, i * 2 + h)
                for h in range(2):
                    turn_ln2(h, i * 2 + h)
                channel(i)
                for h in range(2):
                    turn_out(h, i * 2 + h)

        @block.scalar
        def _(act):
            A = nc.scalar.activation

            def take_ln(h, m):
                act.wait_ge(c["r_tt"].sem, c["r_tt"].at(m + 1))
                nc.scalar.copy(mid(y0[h]), seqs(turned[h][0]))
                nc.scalar.copy(y0[h][:, :, 0:1], seqs(turned[h][0])[:, :, 0:1]).then_inc(c["r_y0"].sem, 1)
                A(zf[h][:], turned[h][1][:], ACT.Identity, bias=v["b1"], scale=v["g1"]).then_inc(c["r_zf"].sem, 1)
                act.wait_ge(c["r_zf"].sem, c["r_zf"].at(m + 1))
                act.sem_inc(spare["act"], 1)
                nc.scalar.copy(blk(xt[0], m), zf[h][:]).then_inc(c["r_zh"].sem, 1)

            def mixes(i):
                for q, dst in enumerate((xpk, xpv, xpr)):
                    for h in range(2):
                        act.wait_ge(c["r_y0"].sem, c["r_y0"].at(i * 2 + h + 1))
                        A(dst[h][:].rearrange("p (b t) -> p b t", b=NS), prev(y0[h]), ACT.Copy,
                          scale=v["om" + "kvr"[q]]).then_inc(c["r_xp"].sem, 1)

            def decays(h, m):
                act.wait_ge(c["r_dm"].sem, c["r_dm"].at(m + 1))
                A(t1[h][:], t1[h][:], ACT.Exp, bias=v["w"])
                act.wait_ge(c["r_dk"].sem, c["r_dk"].at(m + 1))
                A(t2[h][:], t2[h][:], ACT.Exp).then_inc(c["r_d"].sem, 1)

            def logs(h, m):
                act.wait_ge(c["r_B"].sem, c["r_B"].at(m + 1))
                A(t3[h][:], t3[h][:], ACT.Ln).then_inc(c["r_ln"].sem, 1)

            def factors(h, m):
                act.wait_ge(c["r_a1"].sem, c["r_a1"].at(m + 1))
                A(t1[h][:], t1[h][:], ACT.Exp, bias=v["w"])
                act.wait_ge(c["r_a2"].sem, c["r_a2"].at(m + 1))
                A(t2[h][:], t2[h][:], ACT.Exp).then_inc(c["r_e"].sem, 1)

            def weights(h, m):
                act.wait_ge(c["r_r"].sem, c["r_r"].at(m + 1))
                A(rg[h][:], rg[h][:], ACT.Tanh, scale=0.5).then_inc(c["r_tr"].sem, 1)
                act.wait_ge(c["r_du"].sem, c["r_du"].at(m + 1))
                A(t3[h][:], t3[h][:], ACT.Tanh, bias=v["nuh"], scale=0.5).then_inc(c["r_th"].sem, 1)

            def take_ln2(h, m):
                act.wait_ge(c["r_t3"].sem, c["r_t3"].at(m + 1))
                A(zf[h][:], bv[h][:], ACT.Identity, bias=v["b2"], scale=v["g2"]).then_inc(c["r_zf2"].sem, 1)
                act.wait_ge(c["r_zf2"].sem, c["r_zf2"].at(m + 1))
                act.sem_inc(spare["act"], 1)
                nc.scalar.copy(blk(xt[0], m), zf[h][:]).then_inc(c["r_zh2"].sem, 1)

            def mixes2(h, m):
                act.wait_ge(c["r_x2w"].sem, c["r_x2w"].at(m + 1))
                A(xpk[h][:].rearrange("p (b t) -> p b t", b=NS), prev(x2[h]), ACT.Copy, scale=v["omck"])
                A(xpr[h][:].rearrange("p (b t) -> p b t", b=NS), prev(x2[h]), ACT.Copy, scale=v["omcr"]).then_inc(c["r_xp2"].sem, 1)

            def gate(h, m):
                act.wait_ge(c["r_rr"].sem, c["r_rr"].at(m + 1))
                A(rg[h][:].rearrange("p b t -> p (b t)"), xpr[h][:], ACT.Tanh, scale=0.5).then_inc(c["r_tr2"].sem, 1)

            def square_hi(i):
                for j in range(4):
                    for h in range(2):
                        act.wait_ge(c["r_sq"].sem, c["r_sq"].at(slot(i, j, h)))
                        if j >= 2:
                            act.wait_ge(c["r_vv"].sem, c["r_vv"].at(slot(i, j - 2, h)))
                        nc.scalar.copy(shi[h][:, j % 2], sqs[h][j % 2]).then_inc(c["r_sh"].sem, 1)

            with act.Fori(0, NBLK // 2) as i:
                for h in range(2):
                    take_ln(h, i * 2 + h)
                mixes(i)
                for h in range(2):
                    decays(h, i * 2 + h)
                for h in range(2):
                    logs(h, i * 2 + h)
                for h in range(2):
                    factors(h, i * 2 + h)
                for h in range(2):
                    weights(h, i * 2 + h)
                for h in range(2):
                    mixes2(h, i * 2 + h)
                for h in range(2):
                    take_ln2(h, i * 2 + h)
                for h in range(2):
                    gate(h, i * 2 + h)
                square_hi(i)

        @block.vector
        def _(dve):
            V = nc.vector

            def ln_stats():
                for j in range(TILES):
                    last = V.bn_stats(stats1[:, j], x[:, j])
                last.then_inc(c["r_st"].sem, 1)
                dve.wait_ge(c["r_st"].sem, c["r_st"].at(1))
                dve.sem_inc(spare["dve"], 1)
                for j in range(TILES):
                    last = V.bn_aggr(mom1[:, j], stats1[:, j])
                last.then_inc(c["r_mom"].sem, 1)

            def ln_apply(h, m):
                dve.wait_ge(c["r_rs"].sem, c["r_rs"].at(m + 1))
                for j in range(BT):
                    t = m * BT + j
                    V.tensor_scalar(ytok[h][:, j], x[:, t], mom1[:, t, 0:1], rs1[:, 1, bass.ds(t, 1)], ALU.subtract, ALU.mult)
                    last = V.tensor_scalar(ztok[h][:, j], x[:, t], mom1[:, t, 0:1], rs1[:, 4, bass.ds(t, 1)],
                                           ALU.subtract, ALU.mult)
                last.then_inc(c["r_tok"].sem, 1)

            def low(h, m):
                dve.wait_ge(c["r_zh"].sem, c["r_zh"].at(m + 1))
                V.tensor_tensor(blk(xt[1], m), zf[h][:], blk(xt[0], m).bitcast(F32), ALU.subtract).then_inc(c["r_zl"].sem, 1)

            def mix(name, h, i):
                m = i * 2 + h
                q, bank, xp, dst = {"k": (0, ba, xpk, key), "v": (1, bv, xpv, val), "r": (2, bc, xpr, rg)}[name]
                dve.wait_ge(c["r_kvr"].sem, c["r_kvr"].at(3 * m + q + 1))
                dve.wait_ge(c["r_xp"].sem, c["r_xp"].at(i * 6 + (2 * q + h + 1)))
                V.scalar_tensor_tensor(out=dst[h][:], in0=seqs(bank[h]), scalar=v["tm" + name],
                                       in1=xp[h][:].rearrange("p (b t) -> p b t", b=NS),
                                       op0=ALU.mult, op1=ALU.add).then_inc(c["r_" + name].sem, 1)

            def running_max(h, m):
                dve.wait_ge(c["r_k"].sem, c["r_k"].at(m + 1))
                for b in range(NS):
                    last = V.tensor_tensor_scan(mx[h][:, b, 1:T1], w_row(), key[h][:, b], LOW, ALU.add, ALU.max)
                last.then_inc(c["r_M"].sem, 1)

            def max_step(h, m):
                dve.wait_ge(c["r_M"].sem, c["r_M"].at(m + 1))
                V.tensor_tensor(t1[h][:], prev(mx[h]), mid(mx[h]), ALU.subtract).then_inc(c["r_dm"].sem, 1)

            def sums(h, m):
                dve.wait_ge(c["r_d"].sem, c["r_d"].at(m + 1))
                for b in range(NS):
                    last = V.tensor_tensor_scan(t3[h][:, b], t1[h][:, b], t2[h][:, b], 0.0, ALU.mult, ALU.add)
                last.then_inc(c["r_B"].sem, 1)

            def log_state(h, m):
                dve.wait_ge(c["r_ln"].sem, c["r_ln"].at(m + 1))
                V.tensor_tensor(mid(bb[h]), mid(mx[h]), t3[h][:], ALU.add).then_inc(c["r_bb"].sem, 1)

            def peaks(h, m):
                dve.wait_ge(c["r_bb"].sem, c["r_bb"].at(m + 1))
                V.scalar_tensor_tensor(out=t4[h][:], in0=prev(bb[h]), scalar=v["w"], in1=key[h][:],
                                       op0=ALU.add, op1=ALU.max).then_inc(c["r_pm"].sem, 1)

            def peak_gap(h, m):
                dve.wait_ge(c["r_pm"].sem, c["r_pm"].at(m + 1))
                V.tensor_tensor(t1[h][:], prev(bb[h]), t4[h][:], ALU.subtract).then_inc(c["r_a1"].sem, 1)

            def numerator(h, m):
                dve.wait_ge(c["r_e"].sem, c["r_e"].at(m + 1))
                dve.wait_ge(c["r_v"].sem, c["r_v"].at(m + 1))
                V.tensor_tensor(t2[h][:], t2[h][:], val[h][:], ALU.mult).then_inc(c["r_ev"].sem, 1)

            def numerator_scan(h, m):
                dve.wait_ge(c["r_ev"].sem, c["r_ev"].at(m + 1))
                for b in range(NS):
                    last = V.tensor_tensor_scan(aa[h][:, b, 1:T1], t1[h][:, b], t2[h][:, b], 0.0, ALU.mult, ALU.add)
                last.then_inc(c["r_aa"].sem, 1)

            def diff(h, m):
                dve.wait_ge(c["r_aa"].sem, c["r_aa"].at(m + 1))
                V.tensor_tensor(t1[h][:], prev(aa[h]), val[h][:], ALU.subtract).then_inc(c["r_q"].sem, 1)

            def blend1(h, m):
                dve.wait_ge(c["r_q"].sem, c["r_q"].at(m + 1))
                dve.wait_ge(c["r_th"].sem, c["r_th"].at(m + 1))
                V.scalar_tensor_tensor(out=t1[h][:], in0=t3[h][:], scalar=1.0, in1=t1[h][:],
                                       op0=ALU.add, op1=ALU.mult).then_inc(c["r_q2"].sem, 1)

            def blend2(h, m):
                dve.wait_ge(c["r_q2"].sem, c["r_q2"].at(m + 1))
                V.scalar_tensor_tensor(out=t2[h][:], in0=t1[h][:], scalar=0.5, in1=val[h][:],
                                       op0=ALU.mult, op1=ALU.add).then_inc(c["r_y"].sem, 1)

            def receptance(h, m):
                dve.wait_ge(c["r_y"].sem, c["r_y"].at(m + 1))
                dve.wait_ge(c["r_tr"].sem, c["r_tr"].at(m + 1))
                V.scalar_tensor_tensor(out=t1[h][:], in0=rg[h][:], scalar=1.0, in1=t2[h][:],
                                       op0=ALU.add, op1=ALU.mult).then_inc(c["r_ry"].sem, 1)

            def add_x(h, m):
                dve.wait_ge(c["r_ry"].sem, c["r_ry"].at(m + 1))
                V.scalar_tensor_tensor(out=mid(x2[h]), in0=t1[h][:], scalar=0.5, in1=mid(y0[h]),
                                       op0=ALU.mult, op1=ALU.add).then_inc(c["r_x2"].sem, 1)

            def wrap_x(h, m):
                dve.wait_ge(c["r_x2"].sem, c["r_x2"].at(m + 1))
                V.tensor_copy(x2[h][:, :, 0:1], x2[h][:, :, SEQ:T1]).then_inc(c["r_x2w"].sem, 1)

            def ln2_stats(h, m):
                dve.wait_ge(c["r_t2"].sem, c["r_t2"].at(m + 1))
                for j in range(BT):
                    last = V.bn_stats(stats[h][:, j], ba[h][:, bass.ts(j, P)])
                last.then_inc(c["r_st2"].sem, 1)
                dve.wait_ge(c["r_st2"].sem, c["r_st2"].at(m + 1))
                dve.sem_inc(spare["dve"], 1)
                for j in range(BT):
                    last = V.bn_aggr(mom[h][:, j], stats[h][:, j])
                last.then_inc(c["r_mom2"].sem, 1)

            def ln2_apply(h, m):
                dve.wait_ge(c["r_rs2"].sem, c["r_rs2"].at(m + 1))
                for j in range(BT):
                    last = V.tensor_scalar(ztok[h][:, j], ba[h][:, bass.ts(j, P)], mom[h][:, j, 0:1], rs[h][:, 1, j:j + 1],
                                           ALU.subtract, ALU.mult)
                last.then_inc(c["r_tok2"].sem, 1)

            def low2(h, m):
                dve.wait_ge(c["r_zh2"].sem, c["r_zh2"].at(m + 1))
                V.tensor_tensor(blk(xt[1], m), zf[h][:], blk(xt[0], m).bitcast(F32), ALU.subtract).then_inc(c["r_zl2"].sem, 1)
                dve.wait_ge(c["r_xp2"].sem, c["r_xp2"].at(m + 1))
                V.scalar_tensor_tensor(out=xpr[h][:], in0=zf[h][:], scalar=v["cmr"], in1=xpr[h][:],
                                       op0=ALU.mult, op1=ALU.add).then_inc(c["r_rr"].sem, 1)

            def channel(i):
                for j in range(4):
                    for h in range(2):
                        dve.wait_ge(c["r_kk"].sem, c["r_kk"].at(slot(i, j, h)))
                        if j >= 1:
                            dve.wait_ge(c["r_sq"].sem, c["r_sq"].at(slot(i, j - 1, h)))
                        V.scalar_tensor_tensor(out=xpv[h][:], in0=(ba[h], bv[h])[j % 2][:], scalar=v["cmk"], in1=xpk[h][:],
                                               op0=ALU.mult, op1=ALU.add).then_inc(c["r_kx"].sem, 1)
                    for h in range(2):
                        dve.wait_ge(c["r_kx"].sem, c["r_kx"].at(slot(i, j, h)))
                        if j >= 2:
                            dve.wait_ge(c["r_sl"].sem, c["r_sl"].at(slot(i, j - 2, h)))
                        V.scalar_tensor_tensor(out=sqs[h][j % 2], in0=xpv[h][:], scalar=0.0, in1=xpv[h][:],
                                               op0=ALU.max, op1=ALU.mult).then_inc(c["r_sq"].sem, 1)
                dve.wait_ge(c["r_sl"].sem, c["r_sl"].at(slot(i, 2, 1)))
                for h in range(2):
                    dve.wait_ge(c["r_sh"].sem, c["r_sh"].at(slot(i, 3, h)))
                    V.tensor_tensor(slo[h][:, 1], sqs[h][1], shi[h][:, 1].bitcast(F32), ALU.subtract).then_inc(c["r_sl"].sem, 1)

            def gated(h, m):
                dve.wait_ge(c["r_vv"].sem, c["r_vv"].at((m - h) * 4 + (7 + h)))
                dve.wait_ge(c["r_tr2"].sem, c["r_tr2"].at(m + 1))
                V.scalar_tensor_tensor(out=t1[h][:], in0=rg[h][:], scalar=1.0, in1=seqs(bc[h]),
                                       op0=ALU.add, op1=ALU.mult).then_inc(c["r_g"].sem, 1)
                dve.wait_ge(c["r_g"].sem, c["r_g"].at(m + 1))
                V.scalar_tensor_tensor(out=t4[h][:], in0=t1[h][:], scalar=0.5, in1=mid(x2[h]),
                                       op0=ALU.mult, op1=ALU.add).then_inc(c["r_o"].sem, 1)

            def add_out(h, m):
                dve.wait_ge(c["r_ot"].sem, c["r_ot"].at(m + 1))
                xb = x[:, bass.ts(m, BT)]
                V.tensor_tensor(xb, tok((b1, b2)[h]), xb, ALU.add).then_inc(c["r_out"].sem, 1)

            for dst, src in (("omk", "tmk"), ("omv", "tmv"), ("omr", "tmr"), ("omck", "cmk"), ("omcr", "cmr")):
                V.tensor_scalar(v[dst], v[src], -1.0, 1.0, ALU.mult, ALU.add)
            V.tensor_scalar(v["nuh"], v["u"], -0.5, None, ALU.mult)
            for h in range(2):
                V.memset(mx[h][:, :, 0:1], LOW)
                V.memset(bb[h][:, :, 0:1], LOW)
                last = V.memset(aa[h][:, :, 0:1], 0.0)
            last.then_inc(c["r_pad"].sem, 1)
            dve.wait_ge(c["r_pad"].sem, c["r_pad"].at(1))
            ln_stats()
            with dve.Fori(0, NBLK // 2) as i:
                for h in range(2):
                    ln_apply(h, i * 2 + h)
                for h in range(2):
                    low(h, i * 2 + h)
                for h in range(2):
                    mix("k", h, i)
                for h in range(2):
                    running_max(h, i * 2 + h)
                for h in range(2):
                    max_step(h, i * 2 + h)
                for h in range(2):
                    mix("v", h, i)
                for h in range(2):
                    sums(h, i * 2 + h)
                for h in range(2):
                    mix("r", h, i)
                for h in range(2):
                    log_state(h, i * 2 + h)
                for h in range(2):
                    peaks(h, i * 2 + h)
                for h in range(2):
                    peak_gap(h, i * 2 + h)
                for h in range(2):
                    numerator(h, i * 2 + h)
                for h in range(2):
                    numerator_scan(h, i * 2 + h)
                for h in range(2):
                    diff(h, i * 2 + h)
                for h in range(2):
                    blend1(h, i * 2 + h)
                for h in range(2):
                    blend2(h, i * 2 + h)
                for h in range(2):
                    receptance(h, i * 2 + h)
                for h in range(2):
                    add_x(h, i * 2 + h)
                for h in range(2):
                    wrap_x(h, i * 2 + h)
                for h in range(2):
                    ln2_stats(h, i * 2 + h)
                for h in range(2):
                    ln2_apply(h, i * 2 + h)
                for h in range(2):
                    low2(h, i * 2 + h)
                channel(i)
                for h in range(2):
                    gated(h, i * 2 + h)
                for h in range(2):
                    add_out(h, i * 2 + h)

        @block.gpsimd
        def _(pool):
            G = nc.gpsimd
            half = consts["minus_half"]

            def ln_scale(n):
                some = slice(n * BT, n * BT + BT)
                r, var, half = rs1[:, :, some], mom1[:, some, 1], consts["minus_half"][:, some]
                if n == 0:
                    pool.wait_ge(c["r_mom"].sem, c["r_mom"].at(1))
                pool.sem_inc(spare["pool"], 1)
                G.tensor_scalar(r[:, 0], var, LN_EPS, None, ALU.add).then_inc(c["r_c1"].sem, 1)
                pool.wait_ge(c["r_c1"].sem, c["r_c1"].at(3 * n + 1))
                G.tensor_tensor(r[:, 1], r[:, 0], half, ALU.pow)
                G.tensor_scalar(r[:, 2], r[:, 0], LN_EPS, None, ALU.mult).then_inc(c["r_c1"].sem, 1)
                pool.wait_ge(c["r_c1"].sem, c["r_c1"].at(3 * n + 2))
                G.tensor_tensor(r[:, 3], r[:, 2], var, ALU.add).then_inc(c["r_c1"].sem, 1)
                pool.wait_ge(c["r_c1"].sem, c["r_c1"].at(3 * n + 3))
                G.tensor_tensor(r[:, 4], r[:, 3], half, ALU.pow).then_inc(c["r_rs"].sem, 1)

            def below_max(h, m):
                pool.wait_ge(c["r_M"].sem, c["r_M"].at(m + 1))
                G.tensor_tensor(t2[h][:], key[h][:], mid(mx[h]), ALU.subtract).then_inc(c["r_dk"].sem, 1)

            def below_peak(h, m):
                pool.wait_ge(c["r_pm"].sem, c["r_pm"].at(m + 1))
                G.tensor_tensor(t2[h][:], key[h][:], t4[h][:], ALU.subtract).then_inc(c["r_a2"].sem, 1)

            def bonus(h, m):
                pool.wait_ge(c["r_bb"].sem, c["r_bb"].at(m + 1))
                G.tensor_tensor(t3[h][:], prev(bb[h]), key[h][:], ALU.subtract).then_inc(c["r_du"].sem, 1)

            def ln2_scale(h, m):
                r = rs[h]
                pool.wait_ge(c["r_mom2"].sem, c["r_mom2"].at(m + 1))
                pool.sem_inc(spare["pool"], 1)
                G.tensor_scalar(r[:, 0], mom[h][:, :, 1], LN_EPS, None, ALU.add).then_inc(c["r_c2"].sem, 1)
                pool.wait_ge(c["r_c2"].sem, c["r_c2"].at(m + 1))
                G.tensor_tensor(r[:, 1], r[:, 0], half[:, 0:BT], ALU.pow).then_inc(c["r_rs2"].sem, 1)

            def square_lo(i):
                for j in range(3):
                    for h in range(2):
                        pool.wait_ge(c["r_sh"].sem, c["r_sh"].at(slot(i, j, h)))
                        G.tensor_tensor(slo[h][:, j % 2], sqs[h][j % 2], shi[h][:, j % 2].bitcast(F32),
                                        ALU.subtract).then_inc(c["r_sl"].sem, 1)

            for n in range(NBLK):
                ln_scale(n)
            with pool.Fori(0, NBLK // 2) as i:
                for h in range(2):
                    below_max(h, i * 2 + h)
                for h in range(2):
                    below_peak(h, i * 2 + h)
                for h in range(2):
                    bonus(h, i * 2 + h)
                for h in range(2):
                    ln2_scale(h, i * 2 + h)
                square_lo(i)

    per = {"r_kvr": 3, "r_kk": 4, "r_vv": 4, "r_kx": 4, "r_sq": 4, "r_sh": 4, "r_sl": 4, "r_xp": 3}
    once = {"r_pad": 1, "r_st": 1, "r_mom": 1, "r_rs": 4, "r_c1": 12}
    for name in RWKV_SEMS:
        if name in once:
            c[name].base += once[name]
        else:
            c[name].base += per.get(name, 1) * NBLK


RWKV_SEMS = ("r_st r_mom r_rs r_tok r_tt r_y0 r_zf r_zh r_zl r_xp r_kvr r_k r_v r_r r_M r_dm r_dk r_d r_B r_ln r_bb r_pm "
             "r_a1 r_a2 r_e r_ev r_aa r_du r_tr r_th r_q r_q2 r_y r_ry r_x2 r_x2w r_t2 r_st2 r_mom2 r_rs2 r_tok2 r_t3 "
             "r_zf2 r_zh2 r_zl2 r_xp2 r_rr r_tr2 r_kk r_kx r_sq r_sh r_sl r_vv r_g r_o r_ot r_out r_c1 r_c2 r_pad").split()


HEADS, STATE, HEAD_DIM = 16, 64, 8

MAMBA_SEMS = ("m_st m_mom m_c m_rs m_tok m_t m_xh m_xl m_pj m_u m_na m_ex m_ln m_dt m_dA m_dh m_dl m_zs m_sum m_ee "
              "m_bc m_bh m_rh m_rl m_D m_E m_CB m_off m_read m_sm m_xp m_xd m_Y m_yc m_sel m_yo m_yb m_yt m_yT m_yh m_yl m_ow "
              "m_out").split()


def mamba_phase(nc, counts, spare, sb, ps, x, xt, consts, w, v, keep, mb):
    c = counts
    credit = {"m_out": 1, "m_E": 2, "m_yc": 1}
    for name, k in credit.items():
        c[name].base += k
    GROUPS = HEADS // 4
    PIECES = (0, 2, 1, 3)
    USES = 3 * GROUPS
    with ExitStack() as ctx:
        def one(name, shape, dt=F32):
            return ctx.enter_context(sb(f"mb_{name}", shape, dt))

        def tiles(name, shape, dt=F32):
            return [one(f"{name}{h}", shape, dt) for h in range(2)]

        u, xraw, zs = keep["u"], keep["xraw"], keep["zs"]
        stats, mom = one("stats", [P, TILES, 6]), one("mom", [P, TILES, 2])
        rs = one("rs", [P, 2, TILES])
        na = one("na", [P, TILES, HEADS])
        dt, dA = u, na
        dAp = [one("dA" + p, [P, TILES, HEADS], F32R) for p in ("hi", "lo")]
        ee = one("ee", [P, 2, BATCH, HEADS])
        xp, xd = tiles("xp", [P, 2, HEADS, 32]), tiles("xd", [P, HEADS, 32])
        yo, ytok = one("yo", [P, P]), one("ytok", [P, 2, P])
        bc = [tiles("bc" + p, [P, 4, 4, SEQ], F32R) for p in ("hi", "lo")]
        yt = one("yt", [P, 3, P])
        yT = [one("yT" + p, [P, SEQ], F32R) for p in ("hi", "lo")]
        rh, rl = tiles("rh", [P, 4, P], F32R), tiles("rl", [P, 4, P], F32R)
        sm = [tiles(f"sm{q}", [P, 4, P]) for q in range(2)]
        off = tiles("off", [P, 4, P])
        ps_d = [ctx.enter_context(ps(f"mb_d{t}", [P, 4, P], F32)) for t in range(2)]
        ps_c = [ctx.enter_context(ps(f"mb_c{t}", [P, 4, SEQ], F32)) for t in range(2)]
        ps_yt = ctx.enter_context(ps("mb_pyt", [P, 4, P], F32))
        ps_y = ctx.enter_context(ps("mb_y", [P, 4, P], F32))
        ps_t = (ps_d[0], ps_d[1], ps_yt, ps_y)
        ps_in = [ps_c[k].rearrange("p (t f) s -> p t (f s)", t=2) for k in range(2)]
        xn = sm[0]
        ps_sum = ps_y[:, 0:2].rearrange("p t (m h) -> p t m h", h=HEADS)
        ps_turn = ps_y[:, 0:2].rearrange("p t c -> p (t c)")
        block = ctx.enter_context(nc.Block())
        ident = consts["ident"]

        def head_of(q, k):
            return 4 * q + 2 * (k % 2) + k // 2

        def by_head(t):
            return t.rearrange("p (r j d) -> p r j d", j=4, d=HEAD_DIM)

        def turned(t):
            return t.rearrange("p (j r d) -> p r j d", j=4, d=HEAD_DIM)

        def spread(t):
            return t.rearrange("p (r j) -> p r j", j=4).unsqueeze(3).broadcast_to([P, GROUPS, 4, HEAD_DIM])

        def columns(t, r):
            return t[:, 4 * r:4 * r + 4, HEAD_DIM * r:HEAD_DIM * r + HEAD_DIM]

        def use(m, q, j, more=True):
            return m * USES + (4 + (3 if more else 2) * q + j)

        def half(q, j, more=True):
            return ps_c[((3 if more else 2) * q + j) % 2]

        @block.tensor
        def _(pe):
            def piece(h, m, k, bank):
                for j in range(4):
                    last = three_pass(pe, bank[:, j], [t[:, PIECES[k], bass.ts(j, P)] for t in w["bc"]],
                                      [q[:, bass.ts(m, SEQ)] for q in xt], True, True)
                last.then_inc(c["m_bc"].sem, 1)

            def decay(h, m, q):
                for t in range(2):
                    g = m * 8 + (2 * q + t)
                    pe.wait_ge(c["m_rl"].sem, c["m_rl"].at(g + 1))
                    pe.wait_ge(c["m_rh"].sem, c["m_rh"].at(g + 1))
                    pe.wait_ge(c["m_E"].sem, c["m_E"].at(g - 1))
                    out = ps_d[t][:].rearrange("p h l -> p (h l)")
                    pe.matmul(out, consts["gt"][:], rh[t][:].rearrange("p h l -> p (h l)"), start=True, stop=False)
                    pe.matmul(out, consts["gt"][:], rl[t][:].rearrange("p h l -> p (h l)"), start=False,
                              stop=True).then_inc(c["m_D"].sem, 1)

            def products(h, m, q, t, more):
                pe.wait_ge(c["m_read"].sem, c["m_read"].at(use(m, q, t, more) - 1))
                for k in (0, 2, 1, 3):
                    hd = head_of(q, k)
                    rows = slice(STATE * (hd % 2), STATE * (hd % 2) + STATE)
                    r, j = hd // 2 // 4, hd // 2 % 4
                    B = [p[h][rows, r, j, bass.ts(t, P)] for p in bc]
                    C = [p[h][rows, 2 + r, j, t * P:SEQ] for p in bc]
                    last = three_pass(pe, half(q, t, more)[:, k, 0:SEQ - t * P], B, C, True, True)
                last.then_inc(c["m_CB"].sem, 1)

            def outputs(h, m, q):
                if q == 0:
                    pe.wait_ge(c["m_xd"].sem, c["m_xd"].at(m + 1))
                    pe.wait_ge(c["m_yc"].sem, c["m_yc"].at(m))
                pe.wait_ge(c["m_sm"].sem, c["m_sm"].at(m * 8 + (2 * q + 2)))
                pe.wait_ge(c["m_off"].sem, c["m_off"].at(m * 4 + (q + 1)))
                for part in range(3):
                    for k in range(4):
                        hd = head_of(q, k)
                        lhs = xd[h][:, hd] if part == 2 else xp[h][:, part, hd]
                        rhs = off[q % 2][:, k] if part == 2 else sm[q % 2][part][:, k]
                        rows = slice(32 * (hd % 4), 32 * (hd % 4) + 32)
                        last = pe.matmul(ps_yt[rows, part], lhs, rhs, start=q == 0 and part == 0,
                                         stop=q == GROUPS - 1 and part == 2)
                last.then_inc(c["m_Y"].sem, 1)

            def to_tokens(h, m):
                pe.wait_ge(c["m_yc"].sem, c["m_yc"].at(m + 1))
                pe.wait_ge(c["m_out"].sem, c["m_out"].at(m))
                pe.wait_ge(c["m_ee"].sem, c["m_ee"].at(1))
                for part in range(3):
                    last = pe.transpose(ps_y[:, part], yt[:, part], ident[:])
                last.then_inc(c["m_sel"].sem, 1)

            def turn_y(h, m):
                pe.wait_ge(c["m_yt"].sem, c["m_yt"].at(m + 1))
                for t in range(2):
                    last = pe.transpose(ps_y[:, t], ytok[:, t], ident[:])
                last.then_inc(c["m_yT"].sem, 1)

            def project_out(h, m):
                pe.wait_ge(c["m_yl"].sem, c["m_yl"].at(m + 1))
                for t in range(2):
                    last = three_pass(pe, ps_y[:, 2 + t], [q[:, bass.ts(t, P)] for q in yT], [q[:] for q in w["out"]],
                                      True, True)
                last.then_inc(c["m_ow"].sem, 1)

            def section(h, m, first=False, more=True):
                for q in range(GROUPS):
                    decay(h, m, q)
                    products(h, m, q, 0, more)
                    if q == 1 and not first:
                        to_tokens(1 - h, m - 1)
                    if q:
                        outputs(h, m, q - 1)
                    elif not first:
                        outputs(1 - h, m - 1, GROUPS - 1)
                    products(h, m, q, 1, more)
                    if q == 3 and not first:
                        turn_y(1 - h, m - 1)
                    if more:
                        pe.wait_ge(c["m_read"].sem, c["m_read"].at(use(m, q, 2) - 1))
                        piece(1 - h, m + 1, q, half(q, 2))
                if not first:
                    project_out(1 - h, m - 1)

            def turn(n):
                pe.wait_ge(c["m_tok"].sem, c["m_tok"].at(n + 1))
                for t in range(BT):
                    last = pe.transpose(ps_t[n][:, t], xn[n % 2][:, t], ident[:])
                last.then_inc(c["m_t"].sem, 1)

            def project(k):
                if k % 2 == 0:
                    pe.wait_ge(c["m_xl"].sem, c["m_xl"].at(k // 2 + 1))
                if k >= 2:
                    pe.wait_ge(c["m_zs"].sem, c["m_zs"].at(k - 1))
                for t in range(2):
                    last = three_pass(pe, ps_in[k % 2][:, t, 0:2 * P + HEADS], [q[:, bass.ts(2 * k + t, P)] for q in xt],
                                      [q[:] for q in w["in"]], True, True)
                last.then_inc(c["m_pj"].sem, 1)

            for name, k in credit.items():
                pe.sem_inc(c[name].sem, k)
            turn(0)
            pe.wait_ge(c["raw_lo"].sem, c["raw_lo"].at(2))
            turn(1)
            project(0)
            project(1)
            turn(2)
            project(2)
            project(3)
            turn(3)
            for k in range(4, 8):
                project(k)
            pe.wait_ge(c["raw_lo"].sem, c["raw_lo"].at(5))
            for k in range(4):
                if k < 2:
                    pe.wait_ge(c["m_zs"].sem, c["m_zs"].at(7 + k))
                else:
                    pe.wait_ge(c["m_read"].sem, c["m_read"].at(k - 1))
                piece(0, 0, k, ps_c[k % 2])
            pe.wait_ge(c["m_dl"].sem, c["m_dl"].at(1))
            for t, tri in ((0, "gt"), (1, "le")):
                for k in range(2):
                    part = dAp[k][:].rearrange("p (m t) h -> p t m h", t=2)[:, t]
                    last = pe.matmul(ps_sum[:, t], consts[tri][:], part, start=k == 0, stop=k == 1)
            last.then_inc(c["m_sum"].sem, 1)
            section(0, 0, first=True)
            with pe.Fori(0, BATCH // 2 - 1) as i:
                section(1, i * 2 + 1)
                section(0, i * 2 + 2)
            section(1, BATCH - 1, more=False)
            outputs(1, BATCH - 1, GROUPS - 1)
            to_tokens(1, BATCH - 1)
            turn_y(1, BATCH - 1)
            project_out(1, BATCH - 1)

        @block.scalar
        def _(act):
            A = nc.scalar.activation

            def take_bc(h, m, k, bank):
                act.wait_ge(c["m_bc"].sem, c["m_bc"].at(m * 4 + (k + 1)))
                nc.scalar.copy(bc[0][h][:, PIECES[k]], bank[:]).then_inc(c["m_bh"].sem, 1)

            def take_yt(h, m):
                act.wait_ge(c["m_Y"].sem, c["m_Y"].at(m * 4 + 4))
                nc.scalar.copy(yt[:], ps_yt[:, 0:3]).then_inc(c["m_yc"].sem, 1)

            def take_y(h, m):
                act.wait_ge(c["m_yT"].sem, c["m_yT"].at(m + 1))
                nc.scalar.copy(yT[0][:], ps_turn).then_inc(c["m_yh"].sem, 1)

            def section(h, m, first=False, more=True):
                for q in range(GROUPS):
                    for t in range(2):
                        g = m * 8 + (2 * q + t)
                        act.wait_ge(c["m_D"].sem, c["m_D"].at(g + 1))
                        if q >= 2 or not first:
                            act.wait_ge(c["m_Y"].sem, c["m_Y"].at(m * 4 + (q - 1)))
                        A(sm[q % 2][t][:], ps_d[t][:], ACT.Exp).then_inc(c["m_E"].sem, 1)
                        if t == 0:
                            act.wait_ge(c["m_CB"].sem, c["m_CB"].at(g + 1))
                            nc.scalar.copy(off[q % 2][:], half(q, 0, more)[:, :, P:SEQ]).then_inc(c["m_off"].sem, 1)
                    if q == 0 and not first:
                        take_yt(1 - h, m - 1)
                    if q == 3 and not first:
                        take_y(1 - h, m - 1)
                    if more:
                        take_bc(1 - h, m + 1, q, half(q, 2))

            def take_x(n):
                act.wait_ge(c["m_t"].sem, c["m_t"].at(n + 1))
                nc.scalar.copy(xt[0][:, bass.ts(n, BLK)], ps_t[n][:].rearrange("p j c -> p (j c)")).then_inc(c["m_xh"].sem, 1)

            def take_in(k):
                act.wait_ge(c["m_pj"].sem, c["m_pj"].at(k + 1))
                tiles2 = slice(2 * k, 2 * k + 2)
                nc.scalar.copy(xraw[:, tiles2], ps_in[k % 2][:, :, 0:P])
                nc.scalar.copy(u[:, tiles2], ps_in[k % 2][:, :, 2 * P:2 * P + HEADS])
                A(zs[:, tiles2], ps_in[k % 2][:, :, P:2 * P], ACT.Silu).then_inc(c["m_zs"].sem, 1)

            jobs = split_jobs([mb])
            for job in jobs:
                split_hi(nc, act, c, job)
            take_x(0)
            take_x(1)
            act.wait_ge(c["raw_lo"].sem, c["raw_lo"].at(5))
            take_in(0)
            take_in(1)
            take_x(2)
            take_in(2)
            take_in(3)
            take_x(3)
            for k in range(4, 8):
                take_in(k)
            A(v["neg_a"][:], v["a_log"][:], ACT.Exp).then_inc(c["m_ex"].sem, 1)
            take_bc(0, 0, 0, ps_c[0])
            act.wait_ge(c["m_na"].sem, c["m_na"].at(1))
            A(na[:], na[:], ACT.Exp).then_inc(c["m_ex"].sem, 1)
            take_bc(0, 0, 1, ps_c[1])
            act.wait_ge(c["m_ex"].sem, c["m_ex"].at(2))
            A(na[:], na[:], ACT.Ln, bias=1.0).then_inc(c["m_ln"].sem, 1)
            take_bc(0, 0, 2, ps_c[0])
            take_bc(0, 0, 3, ps_c[1])
            act.wait_ge(c["m_sum"].sem, c["m_sum"].at(1))
            A(ee[:], ps_sum, ACT.Exp).then_inc(c["m_ee"].sem, 1)
            section(0, 0, first=True)
            with act.Fori(0, BATCH // 2 - 1) as i:
                section(1, i * 2 + 1)
                section(0, i * 2 + 2)
            section(1, BATCH - 1, more=False)
            take_yt(1, BATCH - 1)
            take_y(1, BATCH - 1)

        @block.vector
        def _(dve):
            V = nc.vector

            def low_bc(h, m, k, bank):
                dve.wait_ge(c["m_bh"].sem, c["m_bh"].at(m * 4 + (k + 1)))
                V.tensor_tensor(bc[1][h][:, PIECES[k]], bank[:], bc[0][h][:, PIECES[k]].bitcast(F32),
                                ALU.subtract).then_inc(c["m_read"].sem, 1)

            def right(m, q, t, first=False):
                g = m * 8 + (2 * q + t)
                if not first:
                    dve.wait_ge(c["m_D"].sem, c["m_D"].at(g - 1))
                for k in range(4):
                    hd = head_of(q, k)
                    last = V.tensor_scalar(rh[t][:, k], consts["le_f"][:], dAp[0][:, m * 2 + t, hd:hd + 1].bitcast(F32),
                                           None, ALU.mult)
                last.then_inc(c["m_rh"].sem, 1)

            def decayed(m, q, t, more):
                g = m * 8 + (2 * q + t)
                dve.wait_ge(c["m_E"].sem, c["m_E"].at(g + 1))
                dve.wait_ge(c["m_CB"].sem, c["m_CB"].at(g + 1))
                if t == 0:
                    dve.wait_ge(c["m_off"].sem, c["m_off"].at(m * 4 + (q + 1)))
                V.tensor_tensor(sm[q % 2][t][:], sm[q % 2][t][:], half(q, t, more)[:, :, 0:P], ALU.mult).then_inc(c["m_read"].sem, 1)

            def gated(h, m):
                dve.wait_ge(c["m_sel"].sem, c["m_sel"].at(m + 1))
                V.tensor_tensor(by_head(yo[:]), turned(ps_y[:, 2]), spread(ee[:, 1, m]), ALU.mult).then_inc(c["m_yo"].sem, 1)
                V.tensor_tensor(by_head(ytok[:, 0]), turned(ps_y[:, 0]), by_head(zs[:, m * 2]), ALU.mult)
                dve.wait_ge(c["m_yo"].sem, c["m_yo"].at(m + 1))
                V.tensor_tensor(by_head(yo[:]), turned(ps_y[:, 1]), by_head(yo[:]), ALU.add).then_inc(c["m_yb"].sem, 1)
                dve.wait_ge(c["m_yb"].sem, c["m_yb"].at(m + 1))
                V.tensor_tensor(ytok[:, 1], yo[:], zs[:, m * 2 + 1], ALU.mult).then_inc(c["m_yt"].sem, 1)

            def low_y(h, m):
                dve.wait_ge(c["m_yh"].sem, c["m_yh"].at(m + 1))
                V.tensor_tensor(yT[1][:], ps_turn, yT[0][:].bitcast(F32), ALU.subtract).then_inc(c["m_yl"].sem, 1)

            def add_out(h, m):
                dve.wait_ge(c["m_ow"].sem, c["m_ow"].at(m + 1))
                xb = x[:, bass.ts(m, 2)]
                V.tensor_tensor(xb, ps_y[:, 2:4], xb, ALU.add).then_inc(c["m_out"].sem, 1)

            def section(h, m, first=False, more=True):
                for q in range(GROUPS):
                    for t in range(2):
                        if q + 1 < GROUPS:
                            right(m, q + 1, t)
                        elif more:
                            right(m + 1, 0, t)
                        decayed(m, q, t, more)
                    if q == 2 and not first:
                        gated(1 - h, m - 1)
                    if q == 3 and not first:
                        low_y(1 - h, m - 1)
                    if more:
                        low_bc(1 - h, m + 1, q, half(q, 2))
                if not first:
                    add_out(1 - h, m - 1)

            def norm(n):
                for j in range(n * BT, n * BT + BT):
                    last = V.bn_stats(stats[:, j], x[:, j])
                last.then_inc(c["m_st"].sem, 1)
                dve.wait_ge(c["m_st"].sem, c["m_st"].at(n + 1))
                for j in range(n * BT, n * BT + BT):
                    last = V.bn_aggr(mom[:, j], stats[:, j])
                last.then_inc(c["m_mom"].sem, 1)

            def normed(n):
                dve.wait_ge(c["m_rs"].sem, c["m_rs"].at(n + 1))
                if n >= 2:
                    dve.wait_ge(c["m_t"].sem, c["m_t"].at(n - 1))
                for j in range(BT):
                    t = n * BT + j
                    last = V.tensor_scalar(xn[n % 2][:, j], x[:, t], mom[:, t, 0:1], rs[:, 1, t:t + 1], ALU.subtract, ALU.mult)
                last.then_inc(c["m_tok"].sem, 1)

            def low_x(n):
                dve.wait_ge(c["m_xh"].sem, c["m_xh"].at(n + 1))
                V.tensor_tensor(xt[1][:, bass.ts(n, BLK)], ps_t[n][:].rearrange("p j c -> p (j c)"),
                                xt[0][:, bass.ts(n, BLK)].bitcast(F32), ALU.subtract).then_inc(c["m_xl"].sem, 1)

            jobs = split_jobs([mb])
            norm(0)
            for k in range(3):
                split_lo(nc, dve, c, jobs[k], k)
            norm(1)
            normed(0)
            split_lo(nc, dve, c, jobs[3], 3)
            normed(1)
            split_lo(nc, dve, c, jobs[4], 4)
            norm(2)
            low_x(0)
            low_x(1)
            normed(2)
            norm(3)
            low_x(2)
            normed(3)
            dve.wait_ge(c["filled"].sem, c["filled"].at(2))
            V.tensor_copy(consts["gt"][:], consts["gt_f"][:])
            V.tensor_copy(consts["le"][:], consts["le_f"][:])
            low_x(3)
            dve.wait_ge(c["m_ex"].sem, c["m_ex"].at(1))
            V.tensor_scalar(v["neg_a"][:], v["neg_a"][:], -1.0, None, ALU.mult)
            dve.wait_ge(c["m_zs"].sem, c["m_zs"].at(8))
            V.tensor_tensor(u[:], u[:], v["b_dt"][:].unsqueeze(1).broadcast_to([P, TILES, HEADS]), ALU.add).then_inc(c["m_u"].sem, 1)
            dve.wait_ge(c["m_u"].sem, c["m_u"].at(1))
            V.scalar_tensor_tensor(out=na[:], in0=u[:], scalar=-1.0, in1=u[:], op0=ALU.mult, op1=ALU.min).then_inc(c["m_na"].sem, 1)
            for k in range(2):
                low_bc(0, 0, k, ps_c[k])
            dve.wait_ge(c["m_ln"].sem, c["m_ln"].at(1))
            V.scalar_tensor_tensor(out=dt[:], in0=u[:], scalar=0.0, in1=na[:], op0=ALU.max, op1=ALU.add).then_inc(c["m_dt"].sem, 1)
            dve.wait_ge(c["m_dt"].sem, c["m_dt"].at(1))
            V.tensor_tensor(dA[:], dt[:], v["neg_a"][:].unsqueeze(1).broadcast_to([P, TILES, HEADS]), ALU.mult).then_inc(c["m_dA"].sem, 1)
            dve.wait_ge(c["m_dA"].sem, c["m_dA"].at(1))
            V.tensor_copy(dAp[0][:], dA[:]).then_inc(c["m_dh"].sem, 1)
            dve.wait_ge(c["m_dh"].sem, c["m_dh"].at(1))
            V.tensor_tensor(dAp[1][:], dA[:], dAp[0][:].bitcast(F32), ALU.subtract).then_inc(c["m_dl"].sem, 1)
            for t in range(2):
                right(0, 0, t, first=True)
                low_bc(0, 0, 2 + t, ps_c[t])
            section(0, 0, first=True)
            with dve.Fori(0, BATCH // 2 - 1) as i:
                section(1, i * 2 + 1)
                section(0, i * 2 + 2)
            section(1, BATCH - 1, more=False)
            gated(1, BATCH - 1)
            low_y(1, BATCH - 1)
            add_out(1, BATCH - 1)

        @block.gpsimd
        def _(pool):
            G = nc.gpsimd

            def inputs(h, m, used):
                if used:
                    pool.wait_ge(c["m_Y"].sem, c["m_Y"].at(m * 4 - 4))
                for t in range(2):
                    xin = xraw[:, m * 2 + t].rearrange("p (h d) -> p h d", d=HEAD_DIM)
                    for r in range(GROUPS):
                        s = slice(4 * r, 4 * r + 4)
                        last = G.tensor_tensor(columns(xp[h][:, t], r), xin[:, s],
                                               dt[:, m * 2 + t, s].unsqueeze(2).broadcast_to([P, 4, HEAD_DIM]), ALU.mult)
                last.then_inc(c["m_xp"].sem, 1)
                pool.wait_ge(c["m_xp"].sem, c["m_xp"].at(m + 1))
                for r in range(GROUPS):
                    last = G.tensor_tensor(columns(xd[h], r), columns(xp[h][:, 0], r),
                                           ee[:, 0, m, 4 * r:4 * r + 4].unsqueeze(2).broadcast_to([P, 4, HEAD_DIM]), ALU.mult)
                last.then_inc(c["m_xd"].sem, 1)

            def right(m, q, t, first=False):
                if not first:
                    pool.wait_ge(c["m_D"].sem, c["m_D"].at(m * 8 + (2 * q + t - 1)))
                part = dAp[1][:, m * 2 + t, 4 * q:4 * q + 4].bitcast(F32).rearrange("p (b a) -> p a b", a=2)
                G.tensor_tensor(rl[t][:].rearrange("p (a b) l -> p a b l", a=2),
                                consts["le_f"][:].unsqueeze(1).unsqueeze(1).broadcast_to([P, 2, 2, P]),
                                part.unsqueeze(3).broadcast_to([P, 2, 2, P]), ALU.mult).then_inc(c["m_rl"].sem, 1)

            def causal(m, q, t, more):
                pool.wait_ge(c["m_read"].sem, c["m_read"].at(use(m, q, t, more) + 1))
                pool.sem_inc(spare["pool"], 1)
                tile = sm[q % 2][t]
                G.affine_select(out=tile[:], in_=tile[:], compare_op=ALU.is_ge, fill=0.0, base=0,
                                pattern=[[0, 4], [1, P]], channel_multiplier=-1).then_inc(c["m_sm"].sem, 1)

            def section(h, m, first=False, more=True):
                for q in range(GROUPS):
                    for t in range(2):
                        if q + 1 < GROUPS:
                            right(m, q + 1, t)
                        elif more:
                            right(m + 1, 0, t)
                        causal(m, q, t, more)
                    if q == 2 and more:
                        inputs(1 - h, m + 1, not first)

            def scale(n):
                some = slice(n * BT, n * BT + BT)
                pool.wait_ge(c["m_mom"].sem, c["m_mom"].at(n + 1))
                G.tensor_scalar(rs[:, 0, some], mom[:, some, 1], LN_EPS, None, ALU.add).then_inc(c["m_c"].sem, 1)
                pool.wait_ge(c["m_c"].sem, c["m_c"].at(n + 1))
                G.tensor_tensor(rs[:, 1, some], rs[:, 0, some], consts["minus_half"][:, some], ALU.pow).then_inc(c["m_rs"].sem, 1)

            G.memset(consts["gt_f"][:], 1.0)
            G.memset(consts["le_f"][:], 1.0).then_inc(c["filled"].sem, 1)
            scale(0)
            scale(1)
            pool.wait_ge(c["filled"].sem, c["filled"].at(1))
            G.affine_select(out=consts["gt_f"][:], in_=consts["gt_f"][:], compare_op=ALU.is_gt, fill=0.0, base=0,
                            pattern=[[-1, P]], channel_multiplier=1)
            G.affine_select(out=consts["le_f"][:], in_=consts["le_f"][:], compare_op=ALU.is_ge, fill=0.0, base=0,
                            pattern=[[1, P]], channel_multiplier=-1).then_inc(c["filled"].sem, 1)
            scale(2)
            scale(3)
            for h in range(2):
                G.memset(xp[h][:], 0.0)
                last = G.memset(xd[h][:], 0.0)
            last.then_inc(c["filled"].sem, 1)
            pool.wait_ge(c["filled"].sem, c["filled"].at(3))
            pool.wait_ge(c["m_dl"].sem, c["m_dl"].at(1))
            for t in range(2):
                right(0, 0, t, first=True)
            pool.wait_ge(c["m_ee"].sem, c["m_ee"].at(1))
            inputs(0, 0, False)
            section(0, 0, first=True)
            with pool.Fori(0, BATCH // 2 - 1) as i:
                section(1, i * 2 + 1)
                section(0, i * 2 + 2)
            section(1, BATCH - 1, more=False)

    for name, k in {"m_st": 4, "m_mom": 4, "m_c": 4, "m_rs": 4, "m_tok": 4, "m_t": 4, "m_xh": 4, "m_xl": 4, "m_pj": 8, "m_zs": 8,
                    "m_u": 1, "m_na": 1, "m_ex": 2, "m_ln": 1, "m_dt": 1, "m_dA": 1, "m_dh": 1, "m_dl": 1, "m_sum": 1, "m_ee": 1,
                    "filled": 3, "raw_hi": 5, "raw_lo": 5}.items():
        c[name].base += k
    for name, k in {"m_bc": 4, "m_bh": 4, "m_rh": 8, "m_rl": 8, "m_D": 8, "m_E": 8, "m_CB": 8, "m_off": 4, "m_read": USES, "m_sm": 8,
                    "m_xp": 1, "m_xd": 1, "m_Y": 4, "m_yc": 1, "m_sel": 1, "m_yo": 1, "m_yb": 1, "m_yt": 1, "m_yT": 1,
                    "m_yh": 1, "m_yl": 1, "m_ow": 1, "m_out": 1}.items():
        c[name].base += k * BATCH


def program(nc, a, out):
    with ExitStack() as ctx:
        def sb(name, shape, dt):
            return ctx.enter_context(nc.sbuf_tensor(name, shape, dt))

        def sem(name):
            return ctx.enter_context(nc.semaphore(name))

        x = sb("x", [P, TILES, P], F32)
        xt = [sb(f"xt_{s}", [P, TOKENS], F32R) for s in ("hi", "lo")]
        consts = {
            "ident": sb("ident", [P, P], F32),
            "iota8": sb("iota8", [P, BT, EXPERTS], F32),
            "minus_half": sb("minus_half", [P, TILES], F32),
        }
        bias = sb("bias", [P, EXPERTS], F32)
        norm = {"stats": sb("norm_stats", [P, BT, 6], F32), "moments": sb("norm_moments", [P, BT, 2], F32),
                "veps": sb("norm_veps", [P, BT], F32), "rstd": sb("norm_rstd", [P, BT], F32),
                "xn": sb("norm_xn", [P, BT, P], F32)}
        names = ("a b sil p1 hhi hlo prod row0 row1 row2 row3 store stored down route xn xt xhi xlo lg lgs lgt gth gates gt gts acc_s ot out "
                 "stats moments veps rstd score gap filled io raw0 raw1 raw2 raw3 raw4 raw5 raw_hi raw_lo rw_raw w1_raw mb_raw").split()
        counts = {n: Count(sem("s_" + n)) for n in names}
        counts.update({n: Count(sem(n)) for n in RWKV_SEMS})
        counts.update({n: Count(sem(n)) for n in MAMBA_SEMS})
        spare = {n: sem("spare_" + n) for n in ("pe", "act", "dve", "pool")}
        w1 = FfnWeights(sb, "w1", 4)

        gate_dram = nc.dram_tensor("gate_rows", (NBLK * EXPERTS * BT, P), F32, kind="Internal").ap()
        x_dram = a["L0_attn_x"].rearrange("b (h p) c -> p (b h) c", p=P)
        out_dram = out.rearrange("b (h p) c -> p (b h) c", p=P)

        def ffn_jobs(w, gate, up, down, e_up, e_down, router):
            S = w.shared
            jobs = [((S, 2, P), [(lambda r: r[:, :, 0], gate), (lambda r: r[:, :, 1], up)]) + tuple(t[:, 0:S] for t in w.up),
                    ((S, P), [(lambda r: r, down)]) + tuple(t[:, 0:S] for t in w.down)]
            for h in range(2):
                s = slice(S + 4 * h, S + 4 * h + 4)
                jobs.append(((4, 2, P), [(lambda r: r.rearrange("p e a c -> p e (a c)"), e_up[:, 4 * h:4 * h + 4])])
                            + tuple(t[:, s] for t in w.up))
            jobs.append(((EXPERTS, P), [(lambda r: r, e_down)]) + tuple(t[:, S:S + EXPERTS] for t in w.down))
            jobs.append(((EXPERTS,), [(lambda r: r, router)]) + tuple(t[:] for t in w.router))
            return jobs

        def ps(name, shape, dt):
            return nc.psum_tensor(name, shape, dt)

        def scoped(name, shape, dt):
            return nc.sbuf_tensor(name, shape, dt)

        def owned(scope):
            return lambda name, shape, dt: scope.enter_context(nc.sbuf_tensor(name, shape, dt))

        def whole(r):
            return r

        w0_jobs = lambda: ffn_jobs(
            w0, a["L0_ffn_gate_w"].rearrange("d (s i) -> d s i", i=P), a["L0_ffn_up_w"].rearrange("d (s i) -> d s i", i=P),
            a["L0_ffn_down_w"].rearrange("(s i) c -> i s c", i=P), a["L0_ffn_fc1_w"].rearrange("e d r -> d e r"),
            a["L0_ffn_fc2_w"].rearrange("e i c -> i e c"), a["L0_ffn_w_router"])
        w1_jobs = ffn_jobs(
            w1, a["L1_ffn_shared_w1"].rearrange("d (s i) -> d s i", i=P), a["L1_ffn_shared_w2"].rearrange("d (s i) -> d s i", i=P),
            a["L1_ffn_shared_w3"].rearrange("(s i) c -> i s c", i=P), a["L1_ffn_w12"].rearrange("e d r -> d e r"),
            a["L1_ffn_w3"].rearrange("e r d -> r e d"), a["L1_ffn_router_w"])

        kept = {"xraw": sb("mb_xraw", [P, TILES, P], F32)}
        mb_vec = {"b_dt": sb("mb_bdt", [P, HEADS], F32), "a_log": sb("mb_alog", [P, HEADS], F32)}
        stage_a = kept["xraw"][:].rearrange("p t c -> p (t c)")
        stage_b = sb("mb_stage", [P, 3 * P + HEADS], F32)
        mb_raws = [stage_b[:, 0:2 * P], stage_b[:, 3 * P:3 * P + HEADS], stage_b[:, 2 * P:3 * P],
                   stage_a[:, 0:8 * P], stage_a[:, 8 * P:16 * P]]
        row = [P, HEADS]
        mb_sources = [a["L1_attn_W_in"], a["L1_attn_W_dt"], a["L1_attn_W_out"], a["L1_attn_W_B"], a["L1_attn_W_C"]]
        mb = RawWeights(None, counts, "mb", [(None, [(whole, source)], None, None) for source in mb_sources], [
            (mb_vec["b_dt"][:], a["L1_attn_b_dt"].rearrange("(q e) -> q e", q=1).broadcast_to(row)),
            (mb_vec["a_log"][:], a["L1_attn_A_log"].rearrange("(q e) -> q e", q=1).broadcast_to(row))], raws=mb_raws)

        layer0 = ctx.enter_context(ExitStack())
        w0 = FfnWeights(owned(layer0), "w0", 2)
        rwkv_scope = layer0.enter_context(ExitStack())
        rw = {n: [owned(rwkv_scope)(f"rw_{n}{s}", [P, k, P], F32R) for s in ("hi", "lo")]
              for n, k in (("tm", 3), ("cm", 4), ("cp", 4))}
        names = {"w": "time_decay", "u": "time_first", "g1": "g1", "b1": "b1", "g2": "g2", "b2": "b2", "tmk": "tmk",
                 "tmv": "tmv", "tmr": "tmr", "cmk": "cmk", "cmr": "cmr"}
        vec = owned(rwkv_scope)("rw_vec", [P, len(names) + 6], F32)
        v = {n: vec[:, k:k + 1] for k, n in enumerate(list(names) + ["omk", "omv", "omr", "omck", "omcr", "nuh"])}
        vectors = []
        for n, full in names.items():
            d = a["L0_attn_" + full]
            d = d.rearrange("(p q) -> p q", q=1) if len(d.shape) == 1 else d.rearrange("q r p -> p (q r)")
            vectors.append((v[n], d))
        raw_scope = rwkv_scope.enter_context(ExitStack())
        rw_set = RawWeights(owned(raw_scope), counts, "rw", [
            ((3, P), [(lambda r: r.rearrange("p q c -> p (q c)"), a["L0_attn_W_tm"])]) + tuple(t[:] for t in rw["tm"]),
            ((4, P), [(lambda r: r.rearrange("p q c -> p (q c)"), a["L0_attn_W_cm"])]) + tuple(t[:] for t in rw["cm"]),
            ((4, P), [(whole, a["L0_attn_W_cp"].rearrange("(q p) c -> p q c", p=P))]) + tuple(t[:] for t in rw["cp"]),
        ], vectors)
        w1_set = RawWeights(owned(raw_scope), counts, "w1", w1_jobs)

        def setup():
            with ExitStack() as scope:
                w0_set = RawWeights(owned(scope), counts, "w0", w0_jobs(), one_semaphore=False)
                block = scope.enter_context(nc.Block())

                @block.gpsimd
                def _(pool):
                    nc.gpsimd.memset(consts["ident"][:], 0.0).then_inc(counts["filled"].sem, 1)
                    nc.gpsimd.memset(consts["minus_half"][:], -0.5)
                    nc.gpsimd.iota(consts["iota8"][:], [[0, BT], [1, EXPERTS]], base=0, channel_multiplier=0,
                                   allow_small_or_imprecise_dtypes=True)
                    pool.wait_ge(counts["filled"].sem, counts["filled"].at(1))
                    nc.gpsimd.affine_select(out=consts["ident"][:], in_=consts["ident"][:],
                                            compare_op=ALU.not_equal, fill=1.0, base=0, pattern=[[-1, P]],
                                            channel_multiplier=1)

                @block.sync
                def _(sp):
                    sp.dma_start(x[:], x_dram).then_inc(counts["io"].sem, 16)
                    w0_set.load(sp)
                    sp.dma_start(bias[:], a["L1_ffn_expert_bias"].rearrange("(a e) -> a e", a=1).broadcast_to(
                        [P, EXPERTS])).then_inc(counts["io"].sem, 16)
                    if STAGES[0] != "ffn0":
                        for later in (rw_set, w1_set, mb):
                            later.load(sp)
                    sp.wait_ge(counts["io"].sem, counts["io"].at(32))

                @block.scalar
                def _(act):
                    for job in split_jobs([w0_set]):
                        split_hi(nc, act, counts, job)

                @block.vector
                def _(dve):
                    for k, job in enumerate(split_jobs([w0_set])):
                        split_lo(nc, dve, counts, job, k)
            for (shape, parts, hi, lo), (count, total) in zip(w0_set.jobs, w0_set.arrived):
                count.base += total
            counts["filled"].base += 1
            counts["io"].base += 32
            counts["raw_hi"].base += len(w0_set.jobs)
            counts["raw_lo"].base += len(w0_set.jobs)

        def split_first():
            with nc.Block() as block:
                @block.scalar
                def _(act):
                    for job in split_jobs([rw_set, w1_set]):
                        split_hi(nc, act, counts, job)

                @block.vector
                def _(dve):
                    for k, job in enumerate(split_jobs([rw_set, w1_set])):
                        split_lo(nc, dve, counts, job, k)
            for s in (rw_set, w1_set):
                counts["raw_hi"].base += len(s.jobs)
                counts["raw_lo"].base += len(s.jobs)

        def mamba_stage():
            with ExitStack() as scope:
                keep = owned(scope)
                kept.update(zs=keep("mb_zs", [P, TILES, P], F32),
                            u=stage_b[:, 0:TILES * HEADS].rearrange("p (t h) -> p t h", h=HEADS))
                w = {n: [keep(f"mb_w{n}{s}", shape, F32R) for s in ("hi", "lo")]
                     for n, shape in (("bc", [P, 4, 4 * P]), ("in", [P, 2 * P + HEADS]), ("out", [P, P]))}
                mv = dict(mb_vec, neg_a=keep("mb_nega", [P, HEADS], F32))
                cm = dict(consts)
                for n in ("gt_f", "le_f"):
                    cm[n] = keep("mb_" + n, [P, P], F32)
                for n in ("gt", "le"):
                    cm[n] = keep("mb_" + n, [P, P], F32R)
                places = [[t[:, 0:2 * P] for t in w["in"]], [t[:, 2 * P:2 * P + HEADS] for t in w["in"]], [t[:] for t in w["out"]]]
                places += [[t[:, 2 * k:2 * k + 2].rearrange("p r c -> p (r c)") for t in w["bc"]] for k in range(2)]
                mb.jobs = [(None, parts, *place) for (_, parts, _, _), place in zip(mb.jobs, places)]
                mamba_phase(nc, counts, spare, scoped, ps, x, xt, cm, w, mv, kept, mb)

        def begun(k):
            return 0 < k < len(STAGES) and STAGES[k - 1:k + 1] == ("ffn0", "ffn1")

        setup()
        for k, stage in enumerate(STAGES):
            if k == 0 and stage != "ffn0":
                split_first()
            if stage == "rwkv":
                raw_scope.close()
            if stage == "mamba":
                layer0.close()
                mamba_stage()
            if stage == "ffn0":
                assert k or len(rw_set.jobs) + len(w1_set.jobs) <= w0.units
                ffn_phase(nc, f"p{k}", counts, spare, scoped, ps, x, xt, consts, w0, True, None, gate_dram, norm,
                          loads=(rw_set, w1_set, mb) if k == 0 else (), splits=(rw_set, w1_set) if k == 0 else (),
                          out_dram=out_dram if k == len(STAGES) - 1 else None,
                          begun=begun(k), start_next=begun(k + 1))
            if stage == "rwkv":
                rwkv_phase(nc, counts, spare, scoped, ps, x, xt, consts, rw, v)
                rwkv_scope.close()
            if stage == "ffn1":
                ffn_phase(nc, f"p{k}", counts, spare, scoped, ps, x, xt, consts, w1, False, bias, gate_dram, norm,
                          out_dram=out_dram if k == len(STAGES) - 1 else None,
                          begun=begun(k), start_next=begun(k + 1))

        if STAGES[-1][:3] != "ffn":
            with nc.Block() as block:
                @block.sync
                def _(sp):
                    sp.dma_start(out_dram, x[:]).then_inc(counts["io"].sem, 16)
                    sp.wait_ge(counts["io"].sem, counts["io"].at(16))


_INS = ["L0_attn_x", "L0_attn_time_decay", "L0_attn_time_first", "L0_attn_W_tm", "L0_attn_g1", "L0_attn_b1",
        "L0_attn_tmk", "L0_attn_tmv", "L0_attn_tmr", "L0_attn_W_cm", "L0_attn_W_cp", "L0_attn_g2", "L0_attn_b2",
        "L0_attn_cmk", "L0_attn_cmr", "L0_ffn_w_router", "L0_ffn_fc1_w", "L0_ffn_fc2_w", "L0_ffn_gate_w",
        "L0_ffn_up_w", "L0_ffn_down_w", "L1_attn_W_in", "L1_attn_W_dt", "L1_attn_b_dt", "L1_attn_W_B",
        "L1_attn_W_C", "L1_attn_W_out", "L1_attn_A_log", "L1_ffn_w12", "L1_ffn_w3", "L1_ffn_shared_w1",
        "L1_ffn_shared_w2", "L1_ffn_shared_w3", "L1_ffn_router_w", "L1_ffn_expert_bias"]
_TURNED = {"L1_attn_W_in", "L1_attn_W_dt", "L1_attn_W_B", "L1_attn_W_C", "L1_attn_W_out", "L1_ffn_w12", "L1_ffn_w3",
           "L1_ffn_shared_w1", "L1_ffn_shared_w2", "L1_ffn_shared_w3", "L1_ffn_router_w"}


def kernel(**inputs):
    import numpy as _np
    import concourse.bacc as _bacc
    from concourse import mybir as _mybir
    from concourse.bass_utils import run_bass_kernel_spmd as _run

    nc = _bacc.Bacc("TRN2", target_bir_lowering=False, num_devices=1)
    arrays, aps = {}, {}
    for name in _INS:
        v = _np.asarray(inputs[name])
        if name in _TURNED:
            v = _np.swapaxes(v, -1, -2)
        v = _np.ascontiguousarray(v)
        arrays[f"in_{name}_dram"] = v
        aps[name] = nc.dram_tensor(f"in_{name}_dram", v.shape, _mybir.dt.from_np(v.dtype), kind="ExternalInput").ap()
    out = nc.dram_tensor("out_0_dram", (BATCH, SEQ, P), F32, kind="ExternalOutput").ap()
    program(nc, aps, out)
    r = _run(nc, [arrays], core_ids=[0])
    return r.results[0]["out_0_dram"]
```
